# Optimizing a Trainium2 kernel written in Bass

```python
import numpy as np
import jax
import jax.numpy as jnp

def _softmax(x, axis=-1):
    return jax.nn.softmax(x, axis=axis)

def _gelu(x):
    return jax.nn.gelu(x, approximate=True)

def _silu(x):
    return jax.nn.silu(x)

def _sigmoid(x):
    return jax.nn.sigmoid(x)

def _layernorm(x, axis=-1, eps=1e-05):
    m = jnp.mean(x, axis=axis, keepdims=True)
    v = jnp.var(x, axis=axis, keepdims=True)
    return (x - m) / jnp.sqrt(v + eps)

def _scatter_add(tgt, idx, src, axis=0):
    return tgt.at[idx].add(src)

def _segment_sum(src, seg, n):
    return jax.ops.segment_sum(src, seg, n)
kernel_name = 'mk_seq_preln_d2_jaxref_r8_409869'

def setup_inputs(seed: int=0):
    np.random.seed(seed)
    _w = jnp.asarray

    def _L0_attn_setup():
        import jax, jax.numpy as jnp
        import numpy as np
        H = 256
        NH = 16
        HD = H // NH
        WINDOW = 128
        EPS = 1e-06
        ROPE_THETA = 10000.0

        def _rms_norm(x, w):
            var = jnp.mean(x * x, axis=-1, keepdims=True)
            return x * jax.lax.rsqrt(var + EPS) * w

        def _rope(x, offset=0):
            S = x.shape[-2]
            pos = jnp.arange(offset, offset + S, dtype=jnp.float32)
            inv_freq = 1.0 / ROPE_THETA ** (jnp.arange(0, HD, 2, dtype=jnp.float32) / HD)
            freqs = pos[:, None] * inv_freq[None, :]
            cos = jnp.cos(freqs)[None, None]
            sin = jnp.sin(freqs)[None, None]
            x1, x2 = jnp.split(x, 2, axis=-1)
            return jnp.concatenate([x1 * cos - x2 * sin, x2 * cos + x1 * sin], axis=-1)
        key = jax.random.key(seed)
        k1, k2, k3 = jax.random.split(key, 3)
        B, S = (2, 256)
        return {'hidden_states': jax.random.normal(k1, (B, S, H), dtype=jnp.float32), 'w_qkv': jax.random.normal(k2, (3 * H, H), dtype=jnp.float32) * (1.0 / np.sqrt(H)), 'q_norm_w': jnp.ones((H,), dtype=jnp.float32), 'k_norm_w': jnp.ones((H,), dtype=jnp.float32), 'w_o': jax.random.normal(k3, (H, H), dtype=jnp.float32) * (1.0 / np.sqrt(H))}
    _L0_attn_in = _L0_attn_setup()

    def _L0_ffn_setup():
        import jax, jax.numpy as jnp
        import numpy as np
        BLOCK = 64

        def dequant4bit(q, scale):
            return (q.astype(jnp.float32) - 7.5) * jnp.repeat(scale, BLOCK, axis=1)
        key = jax.random.key(seed)
        ks = jax.random.split(key, 11)
        B, S, D, H, R = (4, 256, 256, 1024, 16)
        return {'x1': jax.random.normal(ks[0], (B, S, D), jnp.float32), 'w_up_q': jax.random.randint(ks[1], (H, D), 0, 16, dtype=jnp.int32), 'w_up_scale': jax.random.uniform(ks[2], (H, D // BLOCK), jnp.float32) * 0.02, 'b_up': jax.random.normal(ks[3], (H,), jnp.float32) * 0.01, 'w_up_lora_a': jax.random.normal(ks[4], (D, R), jnp.float32) * 0.02, 'w_up_lora_b': jax.random.normal(ks[5], (R, H), jnp.float32) * 0.02, 'w_down_q': jax.random.randint(ks[6], (D, H), 0, 16, dtype=jnp.int32), 'w_down_scale': jax.random.uniform(ks[7], (D, H // BLOCK), jnp.float32) * 0.02, 'b_down': jax.random.normal(ks[8], (D,), jnp.float32) * 0.01, 'w_down_lora_a': jax.random.normal(ks[9], (H, R), jnp.float32) * 0.02, 'w_down_lora_b': jax.random.normal(ks[10], (R, D), jnp.float32) * 0.02}
    _L0_ffn_in = _L0_ffn_setup()

    def _L1_attn_setup():
        import jax, jax.numpy as jnp
        import numpy as np
        B_SZ, L, D, DR, N = (2, 256, 256, 128, 16)
        DT_MIN, DT_MAX = (0.001, 0.1)
        key = jax.random.key(seed)
        ks = jax.random.split(key, 6)
        x = jax.random.normal(ks[0], (B_SZ, L, D), dtype=jnp.float32)
        W_xproj = jax.random.normal(ks[1], (DR + 2 * N, D), dtype=jnp.float32) / jnp.sqrt(D)
        b_xproj = jax.random.normal(ks[2], (DR + 2 * N,), dtype=jnp.float32) * 0.01
        W_dt = jax.random.uniform(ks[3], (D, DR), dtype=jnp.float32, minval=-1.0 / jnp.sqrt(DR), maxval=1.0 / jnp.sqrt(DR))
        dt = jnp.exp(jax.random.uniform(ks[4], (D,), dtype=jnp.float32) * (np.log(DT_MAX) - np.log(DT_MIN)) + np.log(DT_MIN))
        dt = jnp.clip(dt, DT_MIN, None)
        b_dt = dt + jnp.log(-jnp.expm1(-dt))
        A_log = jnp.log(jnp.broadcast_to(jnp.arange(1, N + 1, dtype=jnp.float32), (D, N)))
        return {'x': x, 'W_xproj': W_xproj, 'b_xproj': b_xproj, 'W_dt': W_dt, 'b_dt': b_dt, 'A_log': A_log}
    _L1_attn_in = _L1_attn_setup()

    def _L1_ffn_setup():
        import jax, jax.numpy as jnp
        import numpy as np
        H = 256
        NH = 32
        KVH = 4
        HD = 128
        E = 32
        TOPK = 8
        I = 128
        EPS = 1e-05
        THETA = 10000.0

        def _rmsnorm(x, w, eps=EPS):
            xf = x.astype(jnp.float32)
            var = jnp.mean(xf * xf, axis=-1, keepdims=True)
            return (w * (xf * jax.lax.rsqrt(var + eps))).astype(x.dtype)

        def _rope(x, pos):
            d = x.shape[-1]
            inv_freq = 1.0 / THETA ** (jnp.arange(0, d, 2, dtype=jnp.float32) / d)
            ang = pos.astype(jnp.float32)[:, None] * inv_freq[None, :]
            cos = jnp.cos(ang)[None, :, None, :]
            sin = jnp.sin(ang)[None, :, None, :]
            x1, x2 = jnp.split(x, 2, axis=-1)
            return jnp.concatenate([x1 * cos - x2 * sin, x1 * sin + x2 * cos], axis=-1)
        key = jax.random.key(seed)
        ks = jax.random.split(key, 16)
        s = 0.02
        n = lambda k, shape: jax.random.normal(k, shape, dtype=jnp.float32) * s
        return {'hidden_states': jax.random.normal(ks[0], (1, 64, H), dtype=jnp.float32), 'ln1_w': jnp.ones((H,), jnp.float32), 'ln2_w': jnp.ones((H,), jnp.float32), 'Wq': n(ks[1], (H, NH * HD)), 'Wk': n(ks[2], (H, KVH * HD)), 'Wv': n(ks[3], (H, KVH * HD)), 'Wo': n(ks[4], (NH * HD, H)), 'Wr': n(ks[5], (H, E)), 'expert_bias': jax.random.normal(ks[6], (E,), dtype=jnp.float32) * 0.1, 'Wg': n(ks[7], (E, H, I)), 'Wu': n(ks[8], (E, H, I)), 'Wd': n(ks[9], (E, I, H)), 'Wsg': n(ks[10], (H, I)), 'Wsu': n(ks[11], (H, I)), 'Wsd': n(ks[12], (I, H))}
    _L1_ffn_in = _L1_ffn_setup()
    _d = {'L0_attn_hidden_states': _L0_attn_in['hidden_states'], 'L0_attn_w_qkv': _L0_attn_in['w_qkv'], 'L0_attn_q_norm_w': _L0_attn_in['q_norm_w'], 'L0_attn_k_norm_w': _L0_attn_in['k_norm_w'], 'L0_attn_w_o': _L0_attn_in['w_o'], 'L0_ffn_w_up_q': _L0_ffn_in['w_up_q'], 'L0_ffn_w_up_scale': _L0_ffn_in['w_up_scale'], 'L0_ffn_b_up': _L0_ffn_in['b_up'], 'L0_ffn_w_up_lora_a': _L0_ffn_in['w_up_lora_a'], 'L0_ffn_w_up_lora_b': _L0_ffn_in['w_up_lora_b'], 'L0_ffn_w_down_q': _L0_ffn_in['w_down_q'], 'L0_ffn_w_down_scale': _L0_ffn_in['w_down_scale'], 'L0_ffn_b_down': _L0_ffn_in['b_down'], 'L0_ffn_w_down_lora_a': _L0_ffn_in['w_down_lora_a'], 'L0_ffn_w_down_lora_b': _L0_ffn_in['w_down_lora_b'], 'L1_attn_W_xproj': _L1_attn_in['W_xproj'], 'L1_attn_b_xproj': _L1_attn_in['b_xproj'], 'L1_attn_W_dt': _L1_attn_in['W_dt'], 'L1_attn_b_dt': _L1_attn_in['b_dt'], 'L1_attn_A_log': _L1_attn_in['A_log'], 'L1_ffn_ln1_w': _L1_ffn_in['ln1_w'], 'L1_ffn_ln2_w': _L1_ffn_in['ln2_w'], 'L1_ffn_Wq': _L1_ffn_in['Wq'], 'L1_ffn_Wk': _L1_ffn_in['Wk'], 'L1_ffn_Wv': _L1_ffn_in['Wv'], 'L1_ffn_Wo': _L1_ffn_in['Wo'], 'L1_ffn_Wr': _L1_ffn_in['Wr'], 'L1_ffn_expert_bias': _L1_ffn_in['expert_bias'], 'L1_ffn_Wg': _L1_ffn_in['Wg'], 'L1_ffn_Wu': _L1_ffn_in['Wu'], 'L1_ffn_Wd': _L1_ffn_in['Wd'], 'L1_ffn_Wsg': _L1_ffn_in['Wsg'], 'L1_ffn_Wsu': _L1_ffn_in['Wsu'], 'L1_ffn_Wsd': _L1_ffn_in['Wsd']}
    _x0 = _d['L0_attn_hidden_states']
    _d['L0_attn_hidden_states'] = jax.random.normal(jax.random.fold_in(jax.random.key(seed), 1), (4, 256, 256), dtype=_x0.dtype)
    del _x0
    return _d

def reference(L0_attn_hidden_states, L0_attn_w_qkv, L0_attn_q_norm_w, L0_attn_k_norm_w, L0_attn_w_o, L0_ffn_w_up_q, L0_ffn_w_up_scale, L0_ffn_b_up, L0_ffn_w_up_lora_a, L0_ffn_w_up_lora_b, L0_ffn_w_down_q, L0_ffn_w_down_scale, L0_ffn_b_down, L0_ffn_w_down_lora_a, L0_ffn_w_down_lora_b, L1_attn_W_xproj, L1_attn_b_xproj, L1_attn_W_dt, L1_attn_b_dt, L1_attn_A_log, L1_ffn_ln1_w, L1_ffn_ln2_w, L1_ffn_Wq, L1_ffn_Wk, L1_ffn_Wv, L1_ffn_Wo, L1_ffn_Wr, L1_ffn_expert_bias, L1_ffn_Wg, L1_ffn_Wu, L1_ffn_Wd, L1_ffn_Wsg, L1_ffn_Wsu, L1_ffn_Wsd):

    def _L0_attn_ref(hidden_states, w_qkv, q_norm_w, k_norm_w, w_o):
        import jax, jax.numpy as jnp
        import numpy as np
        H = 256
        NH = 16
        HD = H // NH
        WINDOW = 128
        EPS = 1e-06
        ROPE_THETA = 10000.0

        def _rms_norm(x, w):
            var = jnp.mean(x * x, axis=-1, keepdims=True)
            return x * jax.lax.rsqrt(var + EPS) * w

        def _rope(x, offset=0):
            S = x.shape[-2]
            pos = jnp.arange(offset, offset + S, dtype=jnp.float32)
            inv_freq = 1.0 / ROPE_THETA ** (jnp.arange(0, HD, 2, dtype=jnp.float32) / HD)
            freqs = pos[:, None] * inv_freq[None, :]
            cos = jnp.cos(freqs)[None, None]
            sin = jnp.sin(freqs)[None, None]
            x1, x2 = jnp.split(x, 2, axis=-1)
            return jnp.concatenate([x1 * cos - x2 * sin, x2 * cos + x1 * sin], axis=-1)
        B, S, _ = hidden_states.shape
        qkv = hidden_states @ w_qkv.T
        q, k, v = jnp.split(qkv, 3, axis=-1)
        q = _rms_norm(q, q_norm_w)
        k = _rms_norm(k, k_norm_w)
        q = q.reshape(B, S, NH, HD).transpose(0, 2, 1, 3)
        k = k.reshape(B, S, NH, HD).transpose(0, 2, 1, 3)
        v = v.reshape(B, S, NH, HD).transpose(0, 2, 1, 3)
        q = _rope(q)
        k = _rope(k)
        q_idx = jnp.arange(S)[:, None]
        k_idx = jnp.arange(S)[None, :]
        mask = (q_idx >= k_idx) & (q_idx - k_idx <= WINDOW - 1)
        scale = 1.0 / np.sqrt(HD)
        scores = jnp.einsum('bhqd,bhkd->bhqk', q, k) * scale
        scores = jnp.where(mask[None, None], scores, -jnp.inf)
        probs = jax.nn.softmax(scores, axis=-1)
        out = jnp.einsum('bhqk,bhkd->bhqd', probs, v)
        out = out.transpose(0, 2, 1, 3).reshape(B, S, H)
        return out @ w_o.T

    def _L0_ffn_ref(x1, w_up_q, w_up_scale, b_up, w_up_lora_a, w_up_lora_b, w_down_q, w_down_scale, b_down, w_down_lora_a, w_down_lora_b):
        import jax, jax.numpy as jnp
        import numpy as np
        BLOCK = 64

        def dequant4bit(q, scale):
            return (q.astype(jnp.float32) - 7.5) * jnp.repeat(scale, BLOCK, axis=1)
        w_up = dequant4bit(w_up_q, w_up_scale).T
        y1 = x1 @ w_up + b_up + x1 @ w_up_lora_a @ w_up_lora_b
        x2 = jax.nn.relu(y1)
        w_down = dequant4bit(w_down_q, w_down_scale).T
        y2 = x2 @ w_down + b_down + x2 @ w_down_lora_a @ w_down_lora_b
        return y2

    def _L1_attn_ref(x, W_xproj, b_xproj, W_dt, b_dt, A_log):
        import jax, jax.numpy as jnp
        import numpy as np
        B_SZ, L, D, DR, N = (2, 256, 256, 128, 16)
        DT_MIN, DT_MAX = (0.001, 0.1)
        dr = W_dt.shape[1]
        n = A_log.shape[1]
        proj = x @ W_xproj.T + b_xproj
        dt_r, Bm, Cm = jnp.split(proj, [dr, dr + n], axis=-1)
        dt = jax.nn.softplus(dt_r @ W_dt.T + b_dt)
        A = -jnp.exp(A_log)
        dA = jnp.exp(jnp.einsum('bld,dn->bldn', dt, A))
        dBX = jnp.einsum('bld,bln,bld->bldn', dt, Bm, x)

        def comb(e1, e2):
            a1, b1 = e1
            a2, b2 = e2
            return (a2 * a1, a2 * b1 + b2)
        _, h = jax.lax.associative_scan(comb, (dA, dBX), axis=1)
        y = jnp.einsum('bldn,bln->bld', h, Cm)
        return y

    def _L1_ffn_ref(hidden_states, ln1_w, ln2_w, Wq, Wk, Wv, Wo, Wr, expert_bias, Wg, Wu, Wd, Wsg, Wsu, Wsd):
        import jax, jax.numpy as jnp
        import numpy as np
        H = 256
        NH = 32
        KVH = 4
        HD = 128
        E = 32
        TOPK = 8
        I = 128
        EPS = 1e-05
        THETA = 10000.0

        def _rmsnorm(x, w, eps=EPS):
            xf = x.astype(jnp.float32)
            var = jnp.mean(xf * xf, axis=-1, keepdims=True)
            return (w * (xf * jax.lax.rsqrt(var + eps))).astype(x.dtype)

        def _rope(x, pos):
            d = x.shape[-1]
            inv_freq = 1.0 / THETA ** (jnp.arange(0, d, 2, dtype=jnp.float32) / d)
            ang = pos.astype(jnp.float32)[:, None] * inv_freq[None, :]
            cos = jnp.cos(ang)[None, :, None, :]
            sin = jnp.sin(ang)[None, :, None, :]
            x1, x2 = jnp.split(x, 2, axis=-1)
            return jnp.concatenate([x1 * cos - x2 * sin, x1 * sin + x2 * cos], axis=-1)
        B, S, _ = hidden_states.shape
        resid = hidden_states
        h = _rmsnorm(hidden_states, ln1_w)
        pos = jnp.arange(S)
        q = (h @ Wq).reshape(B, S, NH, HD)
        k = (h @ Wk).reshape(B, S, KVH, HD)
        v = (h @ Wv).reshape(B, S, KVH, HD)
        q = _rope(q, pos)
        k = _rope(k, pos)
        rep = NH // KVH
        k = jnp.repeat(k, rep, axis=2)
        v = jnp.repeat(v, rep, axis=2)
        scores = jnp.einsum('bqhd,bkhd->bhqk', q, k) / jnp.sqrt(jnp.float32(HD))
        causal = jnp.tril(jnp.ones((S, S), dtype=bool))
        scores = jnp.where(causal[None, None], scores, jnp.float32(-1000000000.0))
        attn = jax.nn.softmax(scores, axis=-1)
        o = jnp.einsum('bhqk,bkhd->bqhd', attn, v).reshape(B, S, NH * HD) @ Wo
        x = resid + o
        resid = x
        h = _rmsnorm(x, ln2_w)
        t = h.reshape(-1, H)
        T = t.shape[0]
        router_scores = jax.nn.sigmoid(t @ Wr)
        _, idx = jax.lax.top_k(router_scores + expert_bias[None, :], TOPK)
        w = jnp.take_along_axis(router_scores, idx, axis=1)
        w = w / jnp.sum(w, axis=-1, keepdims=True)
        wfull = jnp.zeros((T, E), jnp.float32).at[jnp.arange(T)[:, None], idx].set(w)
        g = jnp.einsum('th,ehi->tei', t, Wg)
        u = jnp.einsum('th,ehi->tei', t, Wu)
        act = jax.nn.silu(g) * u
        moe = jnp.einsum('tei,te,eih->th', act, wfull, Wd)
        shared = jax.nn.silu(t @ Wsg) * (t @ Wsu) @ Wsd
        return resid + (moe + shared).reshape(B, S, H)
    x = L0_attn_hidden_states
    x = x + _L0_attn_ref(_layernorm(x, axis=-1), L0_attn_w_qkv, L0_attn_q_norm_w, L0_attn_k_norm_w, L0_attn_w_o)
    x = x + _L0_ffn_ref(_layernorm(x, axis=-1), L0_ffn_w_up_q, L0_ffn_w_up_scale, L0_ffn_b_up, L0_ffn_w_up_lora_a, L0_ffn_w_up_lora_b, L0_ffn_w_down_q, L0_ffn_w_down_scale, L0_ffn_b_down, L0_ffn_w_down_lora_a, L0_ffn_w_down_lora_b)
    x = x + _L1_attn_ref(_layernorm(x, axis=-1), L1_attn_W_xproj, L1_attn_b_xproj, L1_attn_W_dt, L1_attn_b_dt, L1_attn_A_log)
    x = x + _L1_ffn_ref(_layernorm(x, axis=-1), L1_ffn_ln1_w, L1_ffn_ln2_w, L1_ffn_Wq, L1_ffn_Wk, L1_ffn_Wv, L1_ffn_Wo, L1_ffn_Wr, L1_ffn_expert_bias, L1_ffn_Wg, L1_ffn_Wu, L1_ffn_Wd, L1_ffn_Wsg, L1_ffn_Wsu, L1_ffn_Wsd)
    return x

_drawn_inputs = setup_inputs


def setup_inputs(seed=0):
    import zlib

    import numpy as np

    out = dict(_drawn_inputs(seed))
    spreads = {'L0_attn_q_norm_w': (1.0, 0.2),
     'L0_attn_k_norm_w': (1.0, 0.2),
     'L1_ffn_ln1_w': (1.0, 0.6),
     'L1_ffn_ln2_w': (1.0, 0.6)}
    factors = {'L0_ffn_b_up': 6.987,
     'L0_ffn_b_down': 7.677,
     'L0_ffn_w_down_lora_b': 2.752,
     'L1_attn_b_xproj': 8.0,
     'L1_ffn_Wq': 8.0,
     'L1_ffn_Wk': 8.0,
     'L1_ffn_Wr': 8.0,
     'L1_ffn_expert_bias': 8.0,
     'L1_ffn_Wg': 8.0,
     'L1_ffn_Wu': 8.0,
     'L1_ffn_Wd': 8.0,
     'L1_ffn_Wsg': 8.0,
     'L1_ffn_Wsu': 8.0,
     'L1_ffn_Wsd': 8.0}
    for name, (base, spread) in spreads.items():
        noise = np.random.default_rng([zlib.crc32(name.encode()), seed]).standard_normal(out[name].shape)
        drawn = base * np.exp(spread * noise) if base else spread * noise
        out[name] = jnp.asarray(drawn.astype(out[name].dtype))
    for name, factor in factors.items():
        out[name] = (out[name] * factor).astype(out[name].dtype)
    return out
```

```python
from contextlib import ExitStack

import numpy as np

import concourse.bass as bass
from concourse import mybir

F32 = mybir.dt.float32
F32R = mybir.dt.float32r
BF16 = mybir.dt.bfloat16
I32 = mybir.dt.int32
ALU = mybir.AluOpType
ACT = mybir.ActivationFunctionType
AX = mybir.AxisListType
ds = bass.ds

P = 128
B, S, D = 4, 256, 256
T = B * S
NT = T // P
KD = D // P
HALF = T // 2
TH = NT // 2
MASKED = -1e30

NH0, HD0 = 16, 16
FF = 1024
KF = FF // P
RANK = 16
DR, NS = 128, 16
NH1, KVH1, HD1 = 32, 4, 128
REP1 = NH1 // KVH1
NE, TOPK, FI = 32, 8, 128


class Count:

    def __init__(self, eng, sem):
        self.eng, self.sem, self.n = eng, sem, 0

    def add(self, ins):
        ins.then_inc(self.sem, 1)
        self.n += 1

    def settle(self):
        self.eng.wait_ge(self.sem, self.n)


def f(ap):
    return ap.bitcast(F32)


def product(pe, out, lhs, rhs, start=True, stop=True, shared=False):
    (lh, ll), (rh, rl) = lhs, rhs
    pe.matmul(out, ll, rh, start=start, stop=False, skip_group_check=shared)
    pe.matmul(out, lh, rl, start=False, stop=False, skip_group_check=shared)
    return pe.matmul(out, lh, rh, start=False, stop=stop, skip_group_check=shared)


class Norm:

    def __init__(self, core, tag, sb, eps, weight=None, twice=None, rms=False, plain=None, z=None):
        self.c, self.eps, self.weight, self.twice, self.rms, self.plain, self.z = core, eps, weight, twice, rms, plain, z
        sem = core.sem
        self.own = sem(f"{tag}_stats_written")
        self.var_ready = sem(f"{tag}_variance_ready")
        self.rstd_ready = sem(f"{tag}_rstd_ready")
        self.normed = sem(f"{tag}_tile_normed")
        self.turned = sem(f"{tag}_half_turned")
        self.hi_ready = sem(f"{tag}_high_ready")
        self.lo_ready = sem(f"{tag}_low_ready")
        self.st = sb(f"{tag}_stats", [P, NT, 6], F32)
        self.mv = sb(f"{tag}_mean_var", [P, NT, 2], F32)
        self.ve = sb(f"{tag}_var_eps", [P, NT], F32)
        self.rs = sb(f"{tag}_rstd", [P, NT], F32)
        self.ve2 = sb(f"{tag}_var_eps2", [P, NT], F32)
        self.rs2 = sb(f"{tag}_rstd2", [P, NT], F32)
        self.y = sb(f"{tag}_y", [P, NT, D], F32)

    def vector(self, dve, x):
        own = Count(dve, self.own)
        for t in range(NT):
            own.add(dve.bn_stats(self.st[:, t, :], x[:, t, :]))
        for t in range(NT):
            dve.wait_ge(self.own, t + 1)
            own.add(dve.bn_aggr(self.mv[:, t, :], self.st[:, t, :]))
        own.settle()
        if self.rms:
            own.add(dve.tensor_tensor(self.ve2[:], self.mv[:, :, 0], self.mv[:, :, 0], ALU.mult))
            own.settle()
            dve.scalar_tensor_tensor(self.ve[:], self.ve2[:], self.eps, self.mv[:, :, 1], ALU.add,
                                     ALU.add).then_inc(self.var_ready, 1)
        else:
            dve.tensor_scalar(self.ve[:], self.mv[:, :, 1], self.eps, None, ALU.add).then_inc(self.var_ready, 1)
        dve.wait_ge(self.rstd_ready, 1)
        scale = self.rs
        if self.twice is not None:
            own.add(dve.tensor_tensor(self.ve2[:], self.rs[:], self.rs[:], ALU.mult))
            own.settle()
            own.add(dve.tensor_tensor(self.ve2[:], self.ve2[:], self.mv[:, :, 1], ALU.mult))
            own.settle()
            dve.tensor_scalar(self.ve2[:], self.ve2[:], self.twice, None, ALU.add).then_inc(self.var_ready, 1)
            dve.wait_ge(self.rstd_ready, 2)
            own.add(dve.tensor_tensor(self.rs2[:], self.rs2[:], self.rs[:], ALU.mult))
            own.settle()
            scale = self.rs2
        for t in range(NT):
            if self.rms:
                ins = dve.tensor_scalar(self.y[:, t, :], x[:, t, :], scale[:, t:t + 1], None, ALU.mult)
            else:
                ins = dve.tensor_scalar(self.y[:, t, :], x[:, t, :], self.mv[:, t, 0:1], scale[:, t:t + 1],
                                        ALU.subtract, ALU.mult)
            ins.then_inc(self.normed, 1)
        if self.z is not None:
            for t in range(NT):
                own.add(dve.tensor_scalar(self.z[:, t, :], x[:, t, :], self.mv[:, t, 0:1], self.rs[:, t:t + 1],
                                          ALU.subtract, ALU.mult))
        self.low(dve)
        own.settle()

    def low(self, dve):
        for n, (half, k) in enumerate((h, k) for h in range(2) for k in range(KD)):
            bank = self.c.psum[:, 2 * half + k, :]
            cols = slice(half * HALF, half * HALF + HALF)
            dve.wait_ge(self.hi_ready, n + 1)
            if self.plain is not None:
                dve.tensor_copy(self.plain[:, k, cols], bank).then_inc(self.lo_ready, 1)
            elif self.weight is not None:
                dve.scalar_tensor_tensor(self.c.xt_l[:, k, cols], bank, self.weight[:, k:k + 1],
                                         f(self.c.xt_h[:, k, cols]), ALU.mult, ALU.subtract).then_inc(self.lo_ready, 1)
            else:
                dve.tensor_tensor(self.c.xt_l[:, k, cols], bank, f(self.c.xt_h[:, k, cols]),
                                  ALU.subtract).then_inc(self.lo_ready, 1)

    def gpsimd(self, pool):
        pool.wait_ge(self.var_ready, 1)
        pool.tensor_tensor(self.rs[:], self.ve[:], self.c.neg_half[:, 0:NT], ALU.pow).then_inc(self.rstd_ready, 1)
        if self.twice is not None:
            pool.wait_ge(self.var_ready, 2)
            pool.tensor_tensor(self.rs2[:], self.ve2[:], self.c.neg_half[:, 0:NT], ALU.pow).then_inc(self.rstd_ready, 1)

    def tensor(self, pe, y=None):
        for half in range(2):
            for t in range(half * TH, half * TH + TH):
                pe.wait_ge(self.normed, t + 1)
                for k in range(KD):
                    ins = pe.transpose(self.c.psum[:, 2 * half + k, (t - half * TH) * P:(t - half * TH + 1) * P],
                                       self.y[:, t, k * P:(k + 1) * P], self.c.ident[:])
            ins.then_inc(self.turned, 1)

    def scalar(self, act):
        for n, (half, k) in enumerate((h, k) for h in range(2) for k in range(KD)):
            act.wait_ge(self.turned, half + 1)
            cols = slice(half * HALF, half * HALF + HALF)
            scale = 1.0 if self.weight is None else self.weight[:, k:k + 1]
            act.activation(self.c.xt_h[:, k, cols], self.c.psum[:, 2 * half + k, :], ACT.Copy,
                           scale=scale).then_inc(self.hi_ready, 1)

    def ready(self, eng, half):
        eng.wait_ge(self.lo_ready, KD * (half + 1))


class Core:

    def __init__(self, nc, ctx):
        self.nc, self.ctx = nc, ctx
        self.sem = lambda name: ctx.enter_context(nc.semaphore(name))
        sb = lambda name, shape, dt: ctx.enter_context(nc.sbuf_tensor(name, shape, dt))
        self.psum = ctx.enter_context(nc.psum_tensor("psum", [P, 8, 512], F32))
        self.x = sb("x", [P, NT, D], F32)
        self.xt_h = sb("xt_h", [P, KD, T], F32R)
        self.xt_l = sb("xt_l", [P, KD, T], F32R)
        self.ident = sb("ident", [P, P], F32)
        self.ident_bf = sb("ident_bf", [P, P], BF16)
        self.neg_half = sb("neg_half", [P, NT * 2], F32)

    def stage(self):
        ctx = ExitStack()
        sb = lambda name, shape, dt: ctx.enter_context(self.nc.sbuf_tensor(name, shape, dt))
        return ctx, sb

    def xt(self, k, cols):
        return self.xt_h[:, k, cols], self.xt_l[:, k, cols]


def windowed_attention(core, x_in, w_qkv_t, q_norm_w, k_norm_w, w_o_t, consts):
    nc, sem, psum = core.nc, core.sem, core.psum
    QK, GROUPS, GH = 2 * D, 4, 4
    BANDS = 3 * P
    scope, sb = core.stage()
    with scope:
        norm = Norm(core, "ln0", sb, 1e-5)
        w_raw = sb("wqkv_raw", [P, KD, 3 * D], F32)
        w_h, w_l = (sb(f"wqkv_{n}", [P, KD, 3 * D], F32R) for n in "hl")
        wo_raw = sb("wo_raw", [P, KD, D], F32)
        wo_h, wo_l = (sb(f"wo_{n}", [P, KD, D], F32R) for n in "hl")
        cos_raw = sb("cos_raw", [P, 2, D], F32)
        sin_raw = sb("sin_raw", [P, 2, D], F32)
        norm_w = sb("norm_w", [P, 2, D], F32)
        cos_w = sb("cos_w", [P, 2, 2, D], F32)
        sin_w = sb("sin_w", [P, 2, 2, D], F32)
        parity = sb("parity", [P, 2], F32)
        mask = sb("mask", [P, BANDS], BF16)
        qk = sb("qk", [P, NT, QK], F32)
        scratch = sb("scratch", [P, D], F32)
        sumsq = sb("sumsq", [P, NT * 2], F32)
        msq = sb("msq", [P, NT * 2], F32)
        rqk = sb("rqk", [P, NT * 2], F32)
        part_a = sb("part_a", [P, 2, QK], F32)
        part_b = sb("part_b", [P, 2, QK], F32)
        v_h, v_l = (sb(f"v_{n}", [P, NT, D], F32R) for n in "hl")
        q_h, q_l = (sb(f"q_{n}", [P, 2, KD, T], F32R) for n in "hl")
        k_h, k_l = (sb(f"k_{n}", [P, KD, T], F32R) for n in "hl")
        qs_h, qs_l = (sb(f"qs_{n}", [P, GROUPS, S], F32R) for n in "hl")
        ks_h, ks_l = (sb(f"ks_{n}", [P, KD, S], F32R) for n in "hl")
        neg_max = sb("neg_max", [P, 2, GH], F32)
        prob = sb("prob", [P, GH, BANDS], F32)
        sums = sb("sums", [P, B, 2 * NH0], F32)
        rden = sb("rden", [P, 1, 2 * NH0], F32)
        pt_h, pt_l = (sb(f"pt_{n}", [P, GH, BANDS], F32R) for n in "hl")
        attn = norm.y

        loaded_x = sem("a_x_loaded")
        loaded_c = sem("a_constants_loaded")
        loaded_w = sem("a_weights_loaded")
        pool_own = sem("a_pool_written")
        w_ready = sem("a_weight_split")
        w_hi = sem("a_weight_high")
        tables = sem("a_tables_ready")
        qkv_done = sem("a_qkv_done")
        qk_out = sem("a_qk_copied")
        v_hi = sem("a_v_high")
        v_lo = sem("a_v_low")
        msq_ready = sem("a_meansquare_ready")
        rqk_ready = sem("a_qk_rstd_ready")
        parts = sem("a_rope_parts")
        roped = sem("a_roped")
        qk_turned = sem("a_qk_turned")
        qk_hi = sem("a_qk_high")
        qk_lo = sem("a_qk_low")
        staged = sem("a_group_staged")
        scored = sem("a_group_scored")
        max_ready = sem("a_max_ready")
        exp_done = sem("a_exp_done")
        p_turned = sem("a_probs_turned")
        p_hi = sem("a_probs_high")
        p_lo = sem("a_probs_low")
        pv_done = sem("a_pv_done")
        o_out = sem("a_attention_out")
        rden_ready = sem("a_denominators_inverted")
        x_added = sem("a_x_added")
        o_turned = sem("a_attention_turned")
        o_hi = sem("a_attention_high")
        o_lo = sem("a_attention_low")
        proj_done = sem("a_projected")
        dve_own = sem("a_vector_written")

        QKB, VB, TURNB = (4, 5), (6, 7), (0, 1, 2, 3)
        SCORE, PTURN, PV = 0, (4, 5), 6

        with nc.Block() as block:
            @block.sync
            def _(sp):
                for t in range(NT):
                    sp.dma_start(core.x[:, t, :], x_in[t * P:(t + 1) * P, :]).then_inc(loaded_x, 16)
                sp.dma_start(core.ident[:], consts["ident"]).then_inc(loaded_c, 16)
                sp.dma_start(cos_raw[:], consts["cos0"].rearrange("(t p) n -> p t n", p=P)).then_inc(loaded_c, 16)
                sp.dma_start(sin_raw[:], consts["sin0"].rearrange("(t p) n -> p t n", p=P)).then_inc(loaded_c, 16)
                for n, w in enumerate((q_norm_w, k_norm_w)):
                    sp.dma_start(norm_w[:, n, :], w.rearrange("(a n) -> a n", a=1).to_broadcast([P, D]))\
                        .then_inc(loaded_c, 16)
                sp.dma_start(parity[:], consts["parity"]).then_inc(loaded_c, 16)
                sp.dma_start(mask[:], consts["window_mask"]).then_inc(loaded_c, 16)
                sp.dma_start(core.ident_bf[:], consts["ident_bf"]).then_inc(loaded_c, 16)

            @block.scalar
            def _(act):
                act.dma_start(w_raw[:], w_qkv_t.rearrange("(k p) n -> p k n", p=P)).then_inc(loaded_w, 16)
                act.dma_start(wo_raw[:], w_o_t.rearrange("(k p) n -> p k n", p=P)).then_inc(loaded_w, 16)
                act.wait_ge(loaded_w, 32)
                act.activation(w_h[:], w_raw[:], ACT.Copy).then_inc(w_hi, 1)
                act.activation(wo_h[:], wo_raw[:], ACT.Copy).then_inc(w_hi, 1)
                norm.scalar(act)
                for t in range(NT):
                    act.wait_ge(qkv_done, t + 1)
                    if t >= 1:
                        act.wait_ge(qk_out, 3 * t)
                    for n in range(2):
                        act.activation(scratch[:], psum[:, QKB[t % 2], n * D:(n + 1) * D], ACT.Square,
                                       accum_out=sumsq[:, 2 * t + n:2 * t + n + 1]).then_inc(qk_out, 1)
                        act.wait_ge(qk_out, 3 * t + n + 1)
                    act.activation(qk[:, t, :], psum[:, QKB[t % 2], :], ACT.Copy).then_inc(qk_out, 1)
                    act.activation(v_h[:, t, :], psum[:, VB[t % 2], 0:D], ACT.Copy).then_inc(v_hi, 1)
                for t in range(NT):
                    act.wait_ge(qk_turned, t + 1)
                    cols = slice(t * P, (t + 1) * P)
                    bank = psum[:, TURNB[t % 4], :].rearrange("p (a k n) -> p a k n", a=2, k=KD)
                    for n in range(2):
                        act.activation(q_h[:, n, :, cols], bank[:, 0], ACT.Copy,
                                       scale=parity[:, n:n + 1]).then_inc(qk_hi, 1)
                    act.activation(k_h[:, :, cols], bank[:, 1], ACT.Copy).then_inc(qk_hi, 1)
                with act.Fori(0, B) as b:
                    for g in range(GROUPS):
                        head0 = (g // 2) * 8 + g % 2
                        act.wait_ge(max_ready, 4 * b + (g + 1))
                        for p in range(GH):
                            for i, cols in enumerate((slice(0, P), slice(P, BANDS))):
                                at = i * NH0 + head0 + 2 * p
                                act.activation(prob[:, p, cols], psum[:, SCORE + p, cols], ACT.Exp,
                                               bias=neg_max[:, i, p:p + 1],
                                               accum_out=sums[:, ds(b, 1), at]).then_inc(exp_done, 1)
                        for p in range(GH):
                            act.wait_ge(p_turned, 16 * b + (4 * g + p + 1))
                            act.activation(pt_h[:, p, :], psum[:, PTURN[p % 2], 0:BANDS], ACT.Copy).then_inc(p_hi, 1)
                for n in range(4):
                    half, k = n // 2, n % 2
                    act.wait_ge(o_turned, half + 1)
                    act.activation(core.xt_h[:, k, half * HALF:(half + 1) * HALF], psum[:, n, :],
                                   ACT.Copy).then_inc(o_hi, 1)

            @block.gpsimd
            def _(pool):
                pool.memset(core.neg_half[:], -0.5).then_inc(pool_own, 1)
                pool.wait_ge(w_hi, 1)
                pool.tensor_tensor(w_l[:], w_raw[:], f(w_h[:]), ALU.subtract).then_inc(w_ready, 1)
                pool.wait_ge(pool_own, 1)
                norm.gpsimd(pool)
                pool.wait_ge(w_hi, 2)
                pool.tensor_tensor(wo_l[:], wo_raw[:], f(wo_h[:]), ALU.subtract).then_inc(w_ready, 1)
                for half in range(2):
                    cols = slice(half * NT, (half + 1) * NT)
                    pool.wait_ge(msq_ready, half + 1)
                    pool.tensor_tensor(rqk[:, cols], msq[:, cols], core.neg_half[:, 0:NT], ALU.pow)\
                        .then_inc(rqk_ready, 1)
                    for t in range(half * TH, half * TH + TH):
                        pool.wait_ge(parts, t + 1)
                        pool.tensor_tensor(qk[:, t, :], part_a[:, t % 2, :], part_b[:, t % 2, :], ALU.add)\
                            .then_inc(roped, 1)
                pool.wait_ge(qk_lo, NT)
                with pool.Fori(0, B) as b:
                    for g in range(GROUPS):
                        ft, par = g // 2, g % 2
                        cols = ds(b * S, S)
                        if g % 2 == 0:
                            pool.wait_ge(scored, 4 * b + (g + 2))
                            pool.tensor_copy(ks_h[:, ft, :], f(k_h[:, ft, cols])).then_inc(staged, 1)
                            pool.tensor_copy(ks_l[:, ft, :], f(k_l[:, ft, cols])).then_inc(staged, 1)
                        else:
                            pool.wait_ge(scored, 4 * b + (g + 1))
                        pool.tensor_copy(qs_h[:, g, :], f(q_h[:, par, ft, cols])).then_inc(staged, 1)
                        pool.tensor_copy(qs_l[:, g, :], f(q_l[:, par, ft, cols])).then_inc(staged, 1)

            @block.vector
            def _(dve):
                own = Count(dve, dve_own)
                dve.wait_ge(loaded_x, 16 * NT)
                norm.vector(dve, core.x)
                dve.wait_ge(loaded_c, 16 * 8)
                for t in range(2):
                    for n in range(2):
                        scale = HD0 ** -0.5 if n == 0 else 1.0
                        own.add(dve.scalar_tensor_tensor(cos_w[:, t, n, :], cos_raw[:, t, :], scale, norm_w[:, n, :],
                                                         ALU.mult, ALU.mult))
                        sw, sr, nw = (a.rearrange("p (h c r) -> p h c r", c=2, r=HD0 // 2)
                                      for a in (sin_w[:, t, n, :], sin_raw[:, t, :], norm_w[:, n, :]))
                        for c in range(2):
                            own.add(dve.scalar_tensor_tensor(sw[:, :, c, :], sr[:, :, c, :], scale, nw[:, :, 1 - c, :],
                                                             ALU.mult, ALU.mult))
                own.settle()

                def rope(t):
                    if t % TH == 0:
                        dve.wait_ge(rqk_ready, t // TH + 1)
                    if t >= 2:
                        dve.wait_ge(roped, t - 1)
                    for n in range(2):
                        src = qk[:, t, n * D:(n + 1) * D]
                        scale = rqk[:, 2 * t + n:2 * t + n + 1]
                        dve.scalar_tensor_tensor(part_a[:, t % 2, n * D:(n + 1) * D], src, scale,
                                                 cos_w[:, t % 2, n, :], ALU.mult, ALU.mult)
                        xs, sw, out = (a.rearrange("p (h c r) -> p h c r", c=2, r=HD0 // 2)
                                       for a in (src, sin_w[:, t % 2, n, :], part_b[:, t % 2, n * D:(n + 1) * D]))
                        for c in range(2):
                            ins = dve.scalar_tensor_tensor(out[:, :, c, :], xs[:, :, 1 - c, :], scale,
                                                           sw[:, :, c, :], ALU.mult, ALU.mult)
                    ins.then_inc(parts, 1)

                for t in range(NT + TH):
                    if t < NT:
                        dve.wait_ge(v_hi, t + 1)
                        dve.tensor_tensor(v_l[:, t, :], psum[:, VB[t % 2], 0:D], f(v_h[:, t, :]),
                                          ALU.subtract).then_inc(v_lo, 1)
                        if t % TH == TH - 1:
                            half = t // TH
                            cols = slice(half * NT, (half + 1) * NT)
                            dve.wait_ge(qk_out, 3 * (half + 1) * TH)
                            dve.tensor_scalar(msq[:, cols], sumsq[:, cols], 1.0 / D, 1e-6, ALU.mult,
                                              ALU.add).then_inc(msq_ready, 1)
                    if t >= TH:
                        rope(t - TH)
                for t in range(NT):
                    dve.wait_ge(qk_hi, 3 * t + 3)
                    cols = slice(t * P, (t + 1) * P)
                    bank = psum[:, TURNB[t % 4], :].rearrange("p (a k n) -> p a k n", a=2, k=KD)
                    for n in range(2):
                        dve.scalar_tensor_tensor(q_l[:, n, :, cols], bank[:, 0], parity[:, n:n + 1],
                                                 f(q_h[:, n, :, cols]), ALU.mult, ALU.subtract)
                    dve.tensor_tensor(k_l[:, :, cols], bank[:, 1], f(k_h[:, :, cols]), ALU.subtract).then_inc(qk_lo, 1)
                with dve.Fori(0, B) as b:
                    def low(g, p):
                        dve.wait_ge(p_hi, 16 * b + (4 * g + p + 1))
                        dve.tensor_tensor(pt_l[:, p, :], psum[:, PTURN[p % 2], 0:BANDS], f(pt_h[:, p, :]),
                                          ALU.subtract).then_inc(p_lo, 1)

                    def peak(g):
                        dve.wait_ge(scored, 4 * b + (4 + g + 1))
                        for i, cols in enumerate((slice(0, P), slice(P, BANDS))):
                            ins = dve.tensor_reduce(neg_max[:, i, :], psum[:, SCORE:SCORE + GH, cols], AX.X, ALU.max,
                                                    negate=True)
                        ins.then_inc(max_ready, 1)

                    peak(0)
                    for g in range(GROUPS):
                        low(g, 0)
                        low(g, 1)
                        if g + 1 < GROUPS:
                            peak(g + 1)
                        low(g, 2)
                        low(g, 3)
                    dve.wait_ge(exp_done, 32 * b + 32)
                    dve.reciprocal(rden[:], sums[:, ds(b, 1), :]).then_inc(rden_ready, 1)
                    dve.wait_ge(rden_ready, b + 1)
                    dve.wait_ge(pv_done, b + 1)
                    out = attn[:, ds(2 * b, 2), :].rearrange("p t (h r) -> p t h r", h=NH0)
                    src = psum[:, PV, :].rearrange("p (t h r) -> p t h r", t=2, h=NH0)
                    den = rden[:].rearrange("p r (t h) -> p t h r", t=2).to_broadcast([P, 2, NH0, HD0])
                    dve.tensor_tensor(out, src, den, ALU.mult).then_inc(o_out, 1)
                for n in range(4):
                    half, k = n // 2, n % 2
                    cols = slice(half * HALF, (half + 1) * HALF)
                    dve.wait_ge(o_hi, n + 1)
                    dve.tensor_tensor(core.xt_l[:, k, cols], psum[:, n, :], f(core.xt_h[:, k, cols]),
                                      ALU.subtract).then_inc(o_lo, 1)
                for t in range(NT):
                    dve.wait_ge(proj_done, t + 1)
                    dve.tensor_tensor(core.x[:, t, :], psum[:, 4 + t % 4, 0:D], core.x[:, t, :],
                                      ALU.add).then_inc(x_added, 1)

            @block.tensor
            def _(pe):
                pe.wait_ge(loaded_c, 16 * 8)
                norm.tensor(pe)
                pe.wait_ge(w_ready, 1)
                for t in range(NT):
                    norm.ready(pe, t // TH)
                    if t >= 2:
                        pe.wait_ge(qk_out, 3 * (t - 1))
                        pe.wait_ge(v_lo, t - 1)
                    cols = slice(t * P, (t + 1) * P)
                    for k in range(KD):
                        product(pe, psum[:, QKB[t % 2], :], core.xt(k, cols), (w_h[:, k, 0:QK], w_l[:, k, 0:QK]),
                                k == 0, k == KD - 1)
                    for k in range(KD):
                        ins = product(pe, psum[:, VB[t % 2], 0:D], core.xt(k, cols), (w_h[:, k, QK:], w_l[:, k, QK:]),
                                      k == 0, k == KD - 1)
                    ins.then_inc(qkv_done, 1)
                for t in range(NT):
                    pe.wait_ge(roped, t + 1)
                    if t >= 4:
                        pe.wait_ge(qk_lo, t - 3)
                    for n in range(4):
                        ins = pe.transpose(psum[:, TURNB[t % 4], n * P:(n + 1) * P], qk[:, t, n * P:(n + 1) * P],
                                           core.ident[:])
                    ins.then_inc(qk_turned, 1)
                pe.wait_ge(qk_lo, NT)
                pe.wait_ge(v_lo, NT)
                pe.sem_inc(scored, 4)
                pe.sem_inc(p_lo, 2)
                pe.sem_inc(o_out, 1)
                with pe.Fori(0, B) as b:
                    def scores(g):
                        ft = g // 2
                        pe.wait_ge(staged, 12 * b + (4, 6, 10, 12)[g])
                        for p in range(GH):
                            rows = slice(32 * p, 32 * p + 32)
                            bank = psum[:, SCORE + p, :]
                            pe.matmul(bank[:, 0:BANDS], core.ident_bf[:], mask[:], start=True, stop=False,
                                      skip_group_check=True)
                            product(pe, bank[:, 0:P], (qs_h[rows, g, 0:P], qs_l[rows, g, 0:P]),
                                    (ks_h[rows, ft, 0:P], ks_l[rows, ft, 0:P]), False, True, True)
                            ins = product(pe, bank[:, P:BANDS], (qs_h[rows, g, P:], qs_l[rows, g, P:]),
                                          (ks_h[rows, ft, :], ks_l[rows, ft, :]), False, True, True)
                        ins.then_inc(scored, 1)

                    def turn(g, p):
                        pe.wait_ge(exp_done, 32 * b + (8 * g + 2 * p + 2))
                        pe.wait_ge(p_lo, 16 * b + (4 * g + p + 1))
                        for i in range(3):
                            ins = pe.transpose(psum[:, PTURN[p % 2], i * P:(i + 1) * P], prob[:, p, i * P:(i + 1) * P],
                                               core.ident[:])
                        ins.then_inc(p_turned, 1)

                    def values(g, p):
                        head = (g // 2) * 8 + g % 2 + 2 * p
                        cols = slice(head * HD0, (head + 1) * HD0)
                        pe.wait_ge(p_lo, 16 * b + (2 + 4 * g + p + 1))
                        out = psum[:, PV, :].rearrange("p (t n) -> p t n", t=2)
                        v0, v1 = ((v_h[:, ds(2 * b + i, 1), cols], v_l[:, ds(2 * b + i, 1), cols]) for i in range(2))
                        pt = [(pt_h[:, p, i * P:(i + 1) * P], pt_l[:, p, i * P:(i + 1) * P]) for i in range(3)]
                        product(pe, out[:, 0:1, cols], pt[0], v0)
                        product(pe, out[:, 1:2, cols], pt[1], v0, True, False)
                        return product(pe, out[:, 1:2, cols], pt[2], v1, False, True)

                    scores(0)
                    for g in range(GROUPS):
                        for p in range(GH):
                            turn(g, p)
                        if g + 1 < GROUPS:
                            scores(g + 1)
                        if g == 0:
                            pe.wait_ge(o_out, b + 1)
                        for p in range(GH):
                            ins = values(g, p)
                    ins.then_inc(pv_done, 1)
                pe.wait_ge(o_out, B + 1)
                for half in range(2):
                    for t in range(half * TH, half * TH + TH):
                        for k in range(KD):
                            ins = pe.transpose(psum[:, 2 * half + k, (t % TH) * P:(t % TH + 1) * P],
                                               attn[:, t, k * P:(k + 1) * P], core.ident[:])
                    ins.then_inc(o_turned, 1)
                pe.wait_ge(w_ready, 2)
                for t in range(NT):
                    pe.wait_ge(o_lo, KD * (t // TH + 1))
                    if t >= 4:
                        pe.wait_ge(x_added, t - 3)
                    for k in range(KD):
                        ins = product(pe, psum[:, 4 + t % 4, 0:D], core.xt(k, slice(t * P, (t + 1) * P)),
                                      (wo_h[:, k, :], wo_l[:, k, :]), k == 0, k == KD - 1)
                    ins.then_inc(proj_done, 1)


def quantized_ffn(core, up_q_t, up_scale_t, b_up, up_lora_a_t, up_lora_b, down_q_t, down_scale_t, b_down,
                  down_lora_a_t, down_lora_b):
    nc, sem, psum = core.nc, core.sem, core.psum
    BLOCK = 64
    UPC = FF // 512
    scope, sb = core.stage()
    with scope:
        norm = Norm(core, "ln1", sb, 1e-5)
        up_q = sb("up_q", [P, KD, FF], I32)
        up_s = sb("up_s", [P, KD, FF], F32)
        down_q = sb("down_q", [P, KF, D], I32)
        down_s = sb("down_s", [P, KF, D], F32)
        lora_ua = sb("lora_ua", [RANK, D], F32)
        lora_ub = sb("lora_ub", [RANK, FF], F32)
        lora_da = sb("lora_da", [RANK, FF], F32)
        lora_db = sb("lora_db", [RANK, D], F32)
        bias_up = sb("bias_up", [P, KF], F32)
        bias_down = sb("bias_down", [P, D], F32)
        up_h, up_l = (sb(f"up_{n}", [P, KD, FF], F32R) for n in "hl")
        down_h, down_l = (sb(f"down_{n}", [P, KF, D], F32R) for n in "hl")
        act_f = sb("act_f", [P, 4, HALF], F32)
        act_h, act_l = (sb(f"act_{n}", [P, KF, HALF], F32R) for n in "hl")

        loaded_up = sem("b_up_loaded")
        loaded_down = sem("b_down_loaded")
        loaded_s = sem("b_small_loaded")
        lora_done = sem("b_lora_products")
        own_dve = sem("b_vector_written")
        weights = sem("b_weight_summed")
        w_hi = sem("b_weight_high")
        w_lo = sem("b_weight_low")
        up_done = sem("b_up_projected")
        relu_done = sem("b_relu_done")
        a_hi = sem("b_activation_high")
        a_lo = sem("b_activation_low")
        down_done = sem("b_down_projected")
        x_added = sem("b_x_added")
        UPB, DOWNB = (4, 5, 6, 7), (0, 1, 2, 3)

        with nc.Block() as block:
            @block.sync
            def _(sp):
                sp.dma_start(up_q[:], up_q_t.rearrange("(k p) n -> p k n", p=P)).then_inc(loaded_up, 16)
                for k in range(KD):
                    for h in range(P // BLOCK):
                        n = k * (P // BLOCK) + h
                        sp.dma_start(up_s[h * BLOCK:(h + 1) * BLOCK, k, :],
                                     up_scale_t[n:n + 1, :].to_broadcast([BLOCK, FF])).then_inc(loaded_up, 16)
                sp.dma_start(down_q[:], down_q_t.rearrange("(k p) n -> p k n", p=P)).then_inc(loaded_down, 16)
                for k in range(KF):
                    for h in range(P // BLOCK):
                        n = k * (P // BLOCK) + h
                        sp.dma_start(down_s[h * BLOCK:(h + 1) * BLOCK, k, :],
                                     down_scale_t[n:n + 1, :].to_broadcast([BLOCK, D])).then_inc(loaded_down, 16)

            @block.scalar
            def _(act):
                for to, given in ((lora_ua, up_lora_a_t), (lora_ub, up_lora_b), (lora_da, down_lora_a_t),
                                  (lora_db, down_lora_b), (bias_up, b_up.rearrange("(k p) -> p k", p=P)),
                                  (bias_down, b_down.rearrange("(a n) -> a n", a=1).to_broadcast([P, D]))):
                    with nc.allow_non_contiguous_dma(reason="a bias of 1024 numbers"):
                        act.dma_start(to[:], given).then_inc(loaded_s, 16)
                for n in range(2):
                    act.wait_ge(weights, n + 1)
                    hi, raw = ((up_h, up_s), (down_h, down_s))[n]
                    act.activation(hi[:], raw[:], ACT.Copy).then_inc(w_hi, 1)
                norm.scalar(act)
                act.wait_ge(loaded_s, 16 * 6)
                for n in range(2 * KF):
                    m = n % KF
                    act.wait_ge(up_done, n + 1)
                    if n >= 4:
                        act.wait_ge(a_lo, n - 3)
                    act.activation(act_f[:, n % 4, :], psum[:, UPB[n % 4], :], ACT.Relu,
                                   bias=bias_up[:, m:m + 1]).then_inc(relu_done, 1)

            @block.gpsimd
            def _(pool):
                pool.wait_ge(w_hi, 1)
                pool.tensor_tensor(up_l[:], up_s[:], f(up_h[:]), ALU.subtract).then_inc(w_lo, 1)
                norm.gpsimd(pool)
                pool.wait_ge(w_hi, 2)
                pool.tensor_tensor(down_l[:], down_s[:], f(down_h[:]), ALU.subtract).then_inc(w_lo, 1)
                for n in range(2 * KF):
                    pool.wait_ge(a_hi, n + 1)
                    pool.tensor_tensor(act_l[:, n % KF, :], act_f[:, n % 4, :], f(act_h[:, n % KF, :]),
                                       ALU.subtract).then_inc(a_lo, 1)

            @block.vector
            def _(dve):
                own = Count(dve, own_dve)
                dve.wait_ge(loaded_up, 16 * (1 + D // BLOCK))
                own.add(dve.scalar_tensor_tensor(up_s[:], up_q[:], -7.5, up_s[:], ALU.add, ALU.mult))
                dve.wait_ge(loaded_down, 16 * (1 + FF // BLOCK))
                own.add(dve.scalar_tensor_tensor(down_s[:], down_q[:], -7.5, down_s[:], ALU.add, ALU.mult))
                own.settle()
                dve.wait_ge(lora_done, 1)
                dve.tensor_tensor(up_s[:].rearrange("p k (c n) -> p (k c) n", c=UPC), psum[:, 0:4, :],
                                  up_s[:].rearrange("p k (c n) -> p (k c) n", c=UPC), ALU.add).then_inc(weights, 1)
                dve.wait_ge(lora_done, 2)
                dve.tensor_tensor(down_s[:].rearrange("p (g k) n -> p g (k n)", g=4), psum[:, 4:8, :],
                                  down_s[:].rearrange("p (g k) n -> p g (k n)", g=4), ALU.add).then_inc(weights, 1)
                norm.vector(dve, core.x)
                for t in range(NT):
                    own.add(dve.tensor_tensor(core.x[:, t, :], core.x[:, t, :], bias_down[:], ALU.add))
                own.settle()

                def finish(t):
                    dve.wait_ge(down_done, t + 1)
                    dve.tensor_tensor(core.x[:, t, :], psum[:, DOWNB[t % 4], 0:D], core.x[:, t, :],
                                      ALU.add).then_inc(x_added, 1)

                for c in range(2):
                    for m in range(KF):
                        n = c * KF + m
                        dve.wait_ge(relu_done, n + 1)
                        dve.tensor_copy(act_h[:, m, :], act_f[:, n % 4, :]).then_inc(a_hi, 1)
                    for t in range(c * TH, (c + 1) * TH):
                        finish(t)

            @block.tensor
            def _(pe):
                pe.wait_ge(loaded_s, 16 * 6)
                for k in range(KD):
                    for c in range(UPC):
                        ins = pe.matmul(psum[:, k * UPC + c, :], lora_ua[:, k * P:(k + 1) * P],
                                        lora_ub[:, c * 512:(c + 1) * 512], start=True, stop=True)
                ins.then_inc(lora_done, 1)
                for k in range(KF):
                    ins = pe.matmul(psum[:, 4 + k // 2, (k % 2) * D:(k % 2 + 1) * D], lora_da[:, k * P:(k + 1) * P],
                                    lora_db[:], start=True, stop=True)
                ins.then_inc(lora_done, 1)
                pe.wait_ge(weights, 2)
                norm.tensor(pe)
                pe.wait_ge(w_lo, 1)
                for c in range(2):
                    norm.ready(pe, c)
                    for m in range(KF):
                        n = c * KF + m
                        if n >= 4:
                            pe.wait_ge(relu_done, n - 3)
                        for k in range(KD):
                            cols = slice(m * P, (m + 1) * P)
                            ins = product(pe, psum[:, UPB[n % 4], :], (up_h[:, k, cols], up_l[:, k, cols]),
                                          core.xt(k, slice(c * HALF, (c + 1) * HALF)), k == 0, k == KD - 1)
                        ins.then_inc(up_done, 1)
                    if c == 0:
                        norm.ready(pe, 1)
                        pe.wait_ge(w_lo, 2)
                    for t in range(c * TH, (c + 1) * TH):
                        if t >= 4:
                            pe.wait_ge(x_added, t - 3)
                        cols = slice((t % TH) * P, (t % TH + 1) * P)
                        for m in range(KF):
                            if t % TH == 0:
                                pe.wait_ge(a_lo, c * KF + m + 1)
                            ins = product(pe, psum[:, DOWNB[t % 4], 0:D], (act_h[:, m, cols], act_l[:, m, cols]),
                                          (down_h[:, m, :], down_l[:, m, :]), m == 0, m == KF - 1)
                        ins.then_inc(down_done, 1)


def selective_scan(core, w_xproj_t, b_xproj, w_dt_t, b_dt, a_log, consts):
    nc, sem, psum = core.nc, core.sem, core.psum
    NBC = 2 * NS
    SETS = KD * NS
    scope, sb = core.stage()
    with scope:
        norm_f = sb("xn_f", [P, KD, T], F32)
        norm = Norm(core, "ln2", sb, 1e-5, plain=norm_f)
        wx_raw = sb("wx_raw", [P, KD, DR + NBC], F32)
        wx3 = sb("wx3", [P, KD, 3 * NBC], F32)
        wx_h, wx_l = (sb(f"wx_{n}", [P, KD, DR], F32R) for n in "hl")
        wdt_raw = sb("wdt_raw", [P, D], F32)
        wdt_h, wdt_l = (sb(f"wdt_{n}", [P, D], F32R) for n in "hl")
        bias_r = sb("bias_r", [P, 1], F32)
        bias_bc = sb("bias_bc", [3 * NBC, 1], F32)
        bias_dt = sb("bias_dt", [P, KD], F32)
        a_raw = sb("a_raw", [P, KD, NS], F32)
        a_neg = sb("a_neg", [P, KD, NS], F32)
        one_hot = sb("one_hot", [3 * NBC, NBC, P], BF16)
        dtr_f = sb("dtr_f", [P, T], F32)
        dtr_h, dtr_l = (sb(f"dtr_{n}", [P, T], F32R) for n in "hl")
        bc_f = sb("bc_f", [3 * NBC, T], F32)
        bc_2 = sb("bc_2", [3 * NBC, T], BF16)
        bc_parts = sb("bc_parts", [3 * NBC, T], BF16)
        dt = sb("dt", [P, KD, T], F32)
        t1 = sb("t1", [P, KD, T], F32)
        t2 = sb("t2", [P, KD, T], F32)
        u = sb("u", [P, KD, T], F32)
        decay = sb("decay", [P, 2, B, S], F32)
        b_all = sb("b_all", [P, 2, T], F32)
        drive = sb("drive", [P, 2, T], F32)
        h = sb("h", [P, 2, T], F32)
        prod = sb("prod", [P, 2, T], F32)
        y = norm_f
        zero_bf = sb("zero_bf", [P, 512], BF16)

        loaded = sem("c_loaded")
        pool_own = sem("c_pool_written")
        w_ready = sem("c_weights_ready")
        r_done = sem("c_dt_rank_projected")
        bc_done = sem("c_bc_projected")
        r_out = sem("c_dt_rank_out")
        r_hi = sem("c_dt_rank_high")
        r_lo = sem("c_dt_rank_low")
        bc_out = sem("c_bc_out")
        split = sem("c_bc_split")
        dt_done = sem("c_dt_projected")
        soft = sem("c_softplus_steps")
        own_dve = sem("c_vector_written")
        bc_ready = sem("c_bc_ready")
        dt_ready = sem("c_dt_ready")
        a_ready = sem("c_a_ready")
        b_spread = sem("c_b_spread")
        c_spread = sem("c_c_spread")
        b_copied = sem("c_b_copied")
        decay_ready = sem("c_decay_ready")
        driven = sem("c_drive_ready")
        scanned = sem("c_scanned")
        weighed = sem("c_weighed")
        summed = sem("c_summed")
        y_out = sem("c_y_out")
        y_turned = sem("c_y_turned")
        RB, BCB, DTB = (4, 5), (6, 7), (0, 1, 2, 3)
        BB, CB, YB = 0, (2, 4), 6

        with nc.Block() as block:
            @block.sync
            def _(sp):
                with nc.allow_non_contiguous_dma(reason="biases"):
                    for to, given in (
                            (wx_raw[:], w_xproj_t.rearrange("(k p) n -> p k n", p=P)),
                            (wdt_raw[:], w_dt_t),
                            (bias_r[:], b_xproj[0:DR].rearrange("(p a) -> p a", a=1)),
                            *((bias_bc[i * NBC:(i + 1) * NBC, :], b_xproj[DR:DR + NBC].rearrange("(p a) -> p a", a=1))
                              for i in range(3)),
                            (bias_dt[:], b_dt.rearrange("(k p) -> p k", p=P)),
                            (a_raw[:], a_log.rearrange("(k p) n -> p k n", p=P)),
                            (one_hot[:], consts["one_hot"])):
                        sp.dma_start(to, given).then_inc(loaded, 16)

            @block.gpsimd
            def _(pool):
                own = Count(pool, pool_own)
                own.add(pool.memset(decay[:], 0.0))
                own.add(pool.memset(zero_bf[:], 0.0))
                pool.wait_ge(loaded, 16 * 9)
                own.add(pool.tensor_copy(wx_h[:], wx_raw[:, :, 0:DR]))
                own.add(pool.tensor_copy(wdt_h[:], wdt_raw[:]))
                for i in range(3):
                    own.add(pool.tensor_copy(wx3[:, :, i * NBC:(i + 1) * NBC], wx_raw[:, :, DR:]))
                own.settle()
                own.add(pool.tensor_tensor(wx_l[:], wx_raw[:, :, 0:DR], f(wx_h[:]), ALU.subtract))
                pool.tensor_tensor(wdt_l[:], wdt_raw[:], f(wdt_h[:]), ALU.subtract).then_inc(w_ready, 1)
                norm.gpsimd(pool)
                for half in range(2):
                    for k in range(KD):
                        cols = slice(half * HALF, (half + 1) * HALF)
                        pool.wait_ge(norm.lo_ready, 2 * half + k + 1)
                        pool.tensor_tensor(core.xt_l[:, k, cols], norm_f[:, k, cols], f(core.xt_h[:, k, cols]),
                                           ALU.subtract).then_inc(split, 1)
                for c in range(2):
                    pool.wait_ge(r_hi, c + 1)
                    cols = slice(c * HALF, (c + 1) * HALF)
                    pool.tensor_tensor(dtr_l[:, cols], dtr_f[:, cols], f(dtr_h[:, cols]), ALU.subtract).then_inc(r_lo, 1)
                pool.wait_ge(dt_ready, 1)
                for k in range(KD):
                    with pool.Fori(0, NS // 2) as i:
                        for j in range(2):
                            at = 2 * i + (k * NS + j)
                            pool.wait_ge(b_copied, at + 2)
                            pool.wait_ge(scanned, at + 1)
                            pool.tensor_tensor(drive[:, j, :], u[:, k, :], b_all[:, j, :], ALU.mult)\
                                .then_inc(driven, 1)

            @block.scalar
            def _(act):
                norm.scalar(act)
                act.wait_ge(loaded, 16 * 9)
                for c in range(2):
                    act.wait_ge(r_done, c + 1)
                    act.activation(dtr_f[:, c * HALF:(c + 1) * HALF], psum[:, RB[c], :], ACT.Identity,
                                   bias=bias_r[:]).then_inc(r_out, 1)
                for c in range(2):
                    act.wait_ge(bc_done, c + 1)
                    act.activation(bc_f[:, c * HALF:(c + 1) * HALF], psum[0:3 * NBC, BCB[c], :], ACT.Identity,
                                   bias=bias_bc[:]).then_inc(bc_out, 1)
                for k in range(KD):
                    act.wait_ge(dt_done, k + 1)
                    z = psum[:, 2 * k:2 * k + 2, :]
                    act.activation(t1[:, k, :].rearrange("p (c n) -> p c n", c=2), z, ACT.Abs,
                                   bias=bias_dt[:, k:k + 1]).then_inc(soft, 1)
                for k in range(KD):
                    act.wait_ge(soft, k + 1)
                    act.activation(t1[:, k, :], t1[:, k, :], ACT.Exp, scale=-1.0).then_inc(soft, 1)
                act.activation(a_neg[:], a_raw[:], ACT.Exp).then_inc(a_ready, 1)
                for k in range(KD):
                    act.wait_ge(soft, KD + k + 1)
                    act.activation(t2[:, k, :], t1[:, k, :], ACT.Ln, bias=1.0).then_inc(soft, 1)
                act.wait_ge(a_ready, 2)
                act.wait_ge(dt_ready, 1)
                act.wait_ge(pool_own, 1)
                for k in range(KD):
                    with act.Fori(0, NS // 2) as i:
                        for j in range(2):
                            at = 2 * i + (k * NS + j)
                            act.wait_ge(b_spread, at + 1)
                            act.wait_ge(driven, at + 1)
                            act.activation(b_all[:, j, :].rearrange("p (c n) -> p c n", c=2), psum[:, BB:BB + 2, :],
                                           ACT.Copy).then_inc(b_copied, 1)
                            act.wait_ge(scanned, at + 1)
                            src = dt[:, k, :].rearrange("p (b s) -> p b s", b=B)
                            act.activation(decay[:, j, :, 1:S], src[:, :, 1:S], ACT.Exp,
                                           scale=a_neg[:, k, ds(2 * i + j, 1)]).then_inc(decay_ready, 1)
                    act.wait_ge(summed, (k + 1) * NS + 2)
                    act.activation(y[:, k, :].rearrange("p (c n) -> p c n", c=2), psum[:, YB:YB + 2, :],
                                   ACT.Copy).then_inc(y_out, 1)

            @block.vector
            def _(dve):
                norm.vector(dve, core.x)
                own = Count(dve, own_dve)
                for c in range(2):
                    cols = slice(c * HALF, (c + 1) * HALF)
                    dve.wait_ge(r_out, c + 1)
                    dve.tensor_copy(dtr_h[:, cols], dtr_f[:, cols]).then_inc(r_hi, 1)
                dve.wait_ge(bc_out, 2)
                own.add(dve.tensor_copy(bc_parts[:], bc_f[:]))
                own.settle()
                own.add(dve.tensor_tensor(bc_f[:], bc_f[:], bc_parts[:], ALU.subtract))
                own.settle()
                own.add(dve.tensor_copy(bc_2[:], bc_f[:]))
                own.settle()
                own.add(dve.tensor_copy(bc_parts[NBC:2 * NBC, :], bc_2[NBC:2 * NBC, :]))
                dve.tensor_tensor(bc_parts[2 * NBC:3 * NBC, :], bc_f[2 * NBC:3 * NBC, :], bc_2[2 * NBC:3 * NBC, :],
                                  ALU.subtract).then_inc(bc_ready, 1)
                dve.wait_ge(a_ready, 1)
                dve.tensor_scalar(a_neg[:], a_neg[:], -1.0, None, ALU.mult).then_inc(a_ready, 1)
                dve.wait_ge(soft, 3 * KD)
                own.add(dve.tensor_scalar(dt[:], t1[:], 1.0, 1.0, ALU.add, ALU.subtract))
                own.settle()
                own.add(dve.tensor_tensor(t1[:], t1[:], dt[:], ALU.subtract))
                own.settle()
                own.add(dve.tensor_tensor(t2[:], t2[:], t1[:], ALU.add))
                for k in range(KD):
                    own.add(dve.tensor_scalar(dt[:, k, :].rearrange("p (c n) -> p c n", c=2), psum[:, 2 * k:2 * k + 2, :],
                                              bias_dt[:, k:k + 1], 0.0, ALU.add, ALU.max))
                own.settle()
                own.add(dve.tensor_tensor(dt[:], dt[:], t2[:], ALU.add))
                own.settle()
                dve.tensor_tensor(u[:], dt[:], norm_f[:], ALU.mult).then_inc(dt_ready, 1)

                def weigh(k, i, j):
                    at = 2 * i + (k * NS + j)
                    dve.wait_ge(scanned, at + 3)
                    dve.wait_ge(c_spread, at + 1)
                    dve.wait_ge(summed, at + 1)
                    dve.tensor_tensor(prod[:, j, :].rearrange("p (c n) -> p c n", c=2), psum[:, CB[j]:CB[j] + 2, :],
                                      h[:, j, :].rearrange("p (c n) -> p c n", c=2), ALU.mult).then_inc(weighed, 1)

                def scan(k, i, j):
                    at = 2 * i + (k * NS + j)
                    dve.wait_ge(decay_ready, at + 1)
                    dve.wait_ge(driven, at + 3)
                    dve.wait_ge(weighed, at + 1)
                    dve.tensor_tensor_scan(h[:, j, :], decay[:, j, :, :].rearrange("p b s -> p (b s)"), drive[:, j, :],
                                           0.0, ALU.mult, ALU.add).then_inc(scanned, 1)

                for k in range(KD):
                    scan(k, 0, 0)
                    with dve.Fori(0, NS // 2 - 1) as i:
                        scan(k, i, 1)
                        weigh(k, i, 0)
                        scan(k, i + 1, 0)
                        weigh(k, i, 1)
                    scan(k, NS // 2 - 1, 1)
                    weigh(k, NS // 2 - 1, 0)
                    weigh(k, NS // 2 - 1, 1)
                for t in range(NT):
                    dve.wait_ge(y_turned, t // 2 + 1)
                    src = psum[:, t // 2, (t % 2) * D:(t % 2 + 1) * D]
                    own.add(dve.tensor_tensor(core.x[:, t, :], src, core.x[:, t, :], ALU.add))
                own.settle()

            @block.tensor
            def _(pe):
                norm.tensor(pe)
                pe.wait_ge(w_ready, 1)
                for c in range(2):
                    pe.wait_ge(split, KD * (c + 1))
                    cols = slice(c * HALF, (c + 1) * HALF)
                    for k in range(KD):
                        ins = product(pe, psum[:, RB[c], :], (wx_h[:, k, :], wx_l[:, k, :]), core.xt(k, cols),
                                      k == 0, k == KD - 1)
                    ins.then_inc(r_done, 1)
                for c in range(2):
                    for k in range(KD):
                        ins = pe.matmul(psum[0:3 * NBC, BCB[c], :], wx3[:, k, :], norm_f[:, k, c * HALF:(c + 1) * HALF],
                                        start=k == 0, stop=k == KD - 1)
                    ins.then_inc(bc_done, 1)
                pe.wait_ge(r_lo, 2)
                for k in range(KD):
                    for c in range(2):
                        cols = slice(c * HALF, (c + 1) * HALF)
                        ins = product(pe, psum[:, DTB[2 * k + c], :], (wdt_h[:, k * P:(k + 1) * P], wdt_l[:, k * P:(k + 1) * P]),
                                      (dtr_h[:, cols], dtr_l[:, cols]))
                    ins.then_inc(dt_done, 1)
                pe.sem_inc(scanned, 2)
                pe.sem_inc(driven, 2)
                pe.sem_inc(summed, 2)
                pe.sem_inc(weighed, 2)
                pe.sem_inc(b_copied, 1)
                pe.wait_ge(bc_ready, 1)
                pe.wait_ge(dt_ready, 1)
                pe.wait_ge(pool_own, 2)

                def spread(row, bank):
                    for c in range(2):
                        ins = pe.matmul(psum[:, bank + c, :], one_hot[:, row, :], bc_parts[:, c * HALF:(c + 1) * HALF],
                                        start=True, stop=True)
                    return ins

                def spread_b(k, n):
                    pe.wait_ge(b_copied, n + (k * NS + 1))
                    spread(n, BB).then_inc(b_spread, 1)

                def spread_c(k, n, j):
                    pe.wait_ge(weighed, n + (k * NS + 1))
                    spread(n + NS, CB[j]).then_inc(c_spread, 1)

                def add(k, n, j):
                    pe.wait_ge(weighed, n + (k * NS + 3))
                    for c in range(2):
                        ins = pe.matmul(psum[:, YB + c, :], core.ident[:], prod[:, j, c * HALF:(c + 1) * HALF],
                                        start=False, stop=False, skip_group_check=True)
                    ins.then_inc(summed, 1)

                LEAD_B, LEAD_C = 4, 2
                for k in range(KD):
                    if k >= 1:
                        pe.wait_ge(y_out, k)
                    for c in range(2):
                        pe.matmul(psum[:, YB + c, :], core.ident_bf[:], zero_bf[:], start=True, stop=False,
                                  skip_group_check=True)
                    for n in range(LEAD_C):
                        spread_b(k, n)
                        spread_c(k, n, n)
                    for n in range(LEAD_C, LEAD_B):
                        spread_b(k, n)
                    with pe.Fori(0, (NS - LEAD_B) // 2) as i:
                        for j in range(2):
                            spread_b(k, 2 * i + (j + LEAD_B))
                            spread_c(k, 2 * i + (j + LEAD_C), j)
                            add(k, 2 * i + j, j)
                    for n in range(NS - LEAD_B, NS):
                        if n + LEAD_C < NS:
                            spread_c(k, n + LEAD_C, n % 2)
                        add(k, n, n % 2)
                pe.wait_ge(y_out, KD)
                for t in range(NT):
                    for k in range(KD):
                        ins = pe.transpose(psum[:, t // 2, (t % 2) * D + k * P:(t % 2) * D + (k + 1) * P],
                                           y[:, k, t * P:(t + 1) * P], core.ident[:])
                    if t % 2 == 1:
                        ins.then_inc(y_turned, 1)


def causal_attention(core, z, ln1_w, wq, wk, wv, wo, consts):
    nc, sem, psum = core.nc, core.sem, core.psum
    STEPS, BANDS, QB = B * REP1, 3 * P, 4
    QC = QB * HD1
    scope, sb = core.stage()
    with scope:
        ln_w = sb("ln1_w", [P, KD], F32)
        norm = Norm(core, "ln3", sb, 1e-5, weight=ln_w, twice=1e-5, z=z)
        wq_raw = sb("wq_raw", [P, KD, REP1 * HD1], F32)
        wkv_raw = sb("wkv_raw", [P, KD, 2 * HD1], F32)
        wo_raw = sb("wo1_raw", [P, REP1, D], F32)
        wq_h, wq_l = (sb(f"wq_{n}", [P, 2 * KD, REP1 * HD1], F32R) for n in "hl")
        wkv_h, wkv_l = (sb(f"wkv_{n}", [P, 2 * KD, 2 * HD1], F32R) for n in "hl")
        wo_h, wo_l = (sb(f"wo1_{n}", [P, 2 * REP1, D], F32R) for n in "hl")
        tables = sb("rope1", [P, 2, 2, 2, HD1], F32)
        mask = sb("causal", [P, P], BF16)
        part_a = sb("r_part_a", [P, 2, QC], F32)
        part_b = sb("r_part_b", [P, 2, QC], F32)
        qr = sb("qr", [P, 2, QC], F32)
        kr = sb("kr", [P, 2, HD1], F32)
        q_h, q_l = (sb(f"q1_{n}", [P, 2, QB, S], F32R) for n in "hl")
        k_h, k_l = (sb(f"k1_{n}", [P, 2, S], F32R) for n in "hl")
        v_h, v_l = (sb(f"v1_{n}", [P, 2, 2, HD1], F32R) for n in "hl")
        neg_max = sb("neg_max1", [P, 2, 2], F32)
        sums = sb("sums1", [P, 2, 2], F32)
        rden = sb("rden1", [P, 2, 2], F32)
        prob = sb("prob1", [P, 2, BANDS], F32)
        pt_h, pt_l = (sb(f"pt1_{n}", [P, 2, BANDS], F32R) for n in "hl")
        ot_h, ot_l = (sb(f"ot1_{n}", [P, 2, S], F32R) for n in "hl")

        loaded_c = sem("d_constants_loaded")
        loaded_w = sem("d_weights_loaded")
        tables_own = sem("d_tables_written")
        w_hi = sem("d_weights_high")
        w_ready = sem("d_weights_split")
        projected = sem("d_projected")
        parts = sem("d_rope_parts")
        roped = sem("d_roped")
        v_hi = sem("d_v_high")
        qk_turned = sem("d_qk_turned")
        qk_hi = sem("d_qk_high")
        qk_lo = sem("d_qk_low")
        scored = sem("d_scored")
        max_ready = sem("d_max_ready")
        exp_done = sem("d_exp_done")
        rden_ready = sem("d_denominator_inverted")
        p_normed = sem("d_probs_normed")
        p_turned = sem("d_probs_turned")
        p_hi = sem("d_probs_high")
        p_lo = sem("d_probs_low")
        pv_done = sem("d_pv_done")
        o_hi = sem("d_output_high")
        o_lo = sem("d_output_low")
        wo_done = sem("d_projected_out")
        z_added = sem("d_z_added")
        PROJB, TURNB, SCOREB, PTURNB, PVB, WOB = (0, 1), 2, (3, 4), 5, 6, 7

        def q_index(g, m, i):
            return 20 * g + (5 * (m // 2) + 1 + i if m % 2 == 0 else 5 * (m // 2) + 3 + i)

        def kv_index(g, b):
            return 20 * g + 5 * b

        def turn_index(g, m, c):
            return 20 * g + 5 * (m // 2) + ((1, 2), (3, 4))[m % 2][c]

        def k_turn_index(g, b):
            return 20 * g + 5 * b

        def known(value, limit):
            return isinstance(value, int) and value < limit

        def ahead(g, m):
            return (g, m) if m < 2 * B else (g + 1, m - 2 * B)

        def ahead_b(g, b):
            return (g, b) if b < B else (g + 1, b - B)

        PIECE = 512
        PIECES = KD * 2 + 1 + REP1 // 2

        def weight_piece(n):
            if n < 2 * KD:
                return wq_h, wq_l, wq_raw, n // 2, 1, slice(n % 2 * PIECE, (n % 2 + 1) * PIECE)
            if n == 2 * KD:
                return wkv_h, wkv_l, wkv_raw, 0, KD, slice(0, 2 * HD1)
            return wo_h, wo_l, wo_raw, 2 * (n - 2 * KD - 1), 2, slice(0, D)

        def schedule(g, last):
            for s in range(STEPS + 3):
                b, r = s // REP1, s % REP1
                own = s < STEPS
                if own:
                    yield "scores", s
                if 1 <= s < STEPS + 1:
                    yield "turn_probs", s - 1
                if own and r == 0:
                    yield "turn_q", (g, 2 * b, 1)
                if own and r in (3, 4):
                    yield "turn_q", (g, 2 * b + 1, r - 3)
                if own and r == 5 and (b + 1 < B or not last):
                    yield "turn_k", ahead_b(g, b + 1)
                if own and r == 7 and (b + 1 < B or not last):
                    yield "turn_q", (*ahead(g, 2 * b + 2), 0)
                if own:
                    yield "softmax", s
                if 2 <= s < STEPS + 2:
                    yield "values", s - 2
                if 3 <= s:
                    yield "project_out", s - 3
                if own and r in (0, 1):
                    yield "q", (g, 2 * b + 1, r)
                if own and r == 2 and (b + 1 < B or not last):
                    yield "kv", ahead_b(g, b + 1)
                if own and r in (4, 5) and (b + 1 < B or not last):
                    yield "q", (*ahead(g, 2 * b + 2), r - 4)
                if not last and 6 <= s < 6 + 2 * PIECES and s % 2 == 0:
                    yield "weights", (g + 1, (s - 6) // 2)

        FIRST = [("kv", (0, 0)), ("q", (0, 0, 0)), ("q", (0, 0, 1)), ("turn_k", (0, 0)), ("turn_q", (0, 0, 0))]

        def run(eng, does):
            def all_of(work, g):
                for kind, what in work:
                    if kind in does:
                        does[kind](g, *(what if isinstance(what, tuple) else (what,)))

            all_of(FIRST, 0)
            with eng.Fori(0, KVH1 - 1) as g:
                all_of(schedule(g, False), g)
            all_of(schedule(KVH1 - 1, True), KVH1 - 1)

        with nc.Block() as block:
            @block.sync
            def _(sp):
                with nc.allow_non_contiguous_dma(reason="a norm's weights"):
                    sp.dma_start(ln_w[:], ln1_w.rearrange("(k p) -> p k", p=P)).then_inc(loaded_c, 16)
                for n, name in enumerate(("cos1", "sin1")):
                    sp.dma_start(tables[:, 1, n, :, :], consts[name].rearrange("(t p) n -> p t n", p=P))\
                        .then_inc(loaded_c, 16)
                sp.dma_start(mask[:], consts["causal_mask"]).then_inc(loaded_c, 16)

                def load(g):
                    sp.dma_start(wkv_raw[:, :, 0:HD1], wk.rearrange("(k p) n -> p k n", p=P)[:, :, ds(g * HD1, HD1)])\
                        .then_inc(loaded_w, 16)
                    sp.dma_start(wkv_raw[:, :, HD1:], wv.rearrange("(k p) n -> p k n", p=P)[:, :, ds(g * HD1, HD1)])\
                        .then_inc(loaded_w, 16)
                    sp.dma_start(wq_raw[:], wq.rearrange("(k p) n -> p k n", p=P)[:, :, ds(g * REP1 * HD1, REP1 * HD1)])\
                        .then_inc(loaded_w, 16)
                    sp.dma_start(wo_raw[:], wo.rearrange("(h p) n -> p h n", p=P)[:, ds(g * REP1, REP1), :])\
                        .then_inc(loaded_w, 16)

                load(0)
                with sp.Fori(1, KVH1) as g:
                    sp.wait_ge(w_ready, g)
                    load(g)

            @block.scalar
            def _(act):
                def weights(_, g, piece):
                    hi, _, raw, row, rows, cols = weight_piece(piece)
                    if piece == 0:
                        act.wait_ge(loaded_w, 64 * g + 64)
                    act.activation(hi[:, ds((g & 1) * raw.shape[1] + row, rows), cols], raw[:, row:row + rows, cols],
                                   ACT.Copy).then_inc(w_hi, 1)

                for piece in range(PIECES):
                    weights(0, 0, piece)
                act.wait_ge(loaded_c, 16 * 4)
                norm.scalar(act)

                def turn_q(_, g, m, c):
                    act.wait_ge(qk_turned, turn_index(g, m, c) + 1)
                    act.activation(q_h[:, m % 2, 2 * c:2 * c + 2, :], psum[:, TURNB, :].rearrange("p (h n) -> p h n", h=2),
                                   ACT.Copy).then_inc(qk_hi, 1)

                def turn_k(_, g, b):
                    act.wait_ge(qk_turned, k_turn_index(g, b) + 1)
                    act.activation(k_h[:, b % 2, :], psum[:, TURNB, 0:S], ACT.Copy).then_inc(qk_hi, 1)

                def kv(_, g, b):
                    act.wait_ge(projected, kv_index(g, b) + 1)
                    bank = psum[:, PROJB[0], :].rearrange("p (t n) -> p t n", t=2)
                    act.activation(v_h[:, b % 2, :, :], bank[:, :, HD1:], ACT.Copy).then_inc(v_hi, 1)

                def softmax(g, s):
                    act.wait_ge(max_ready, STEPS * g + (s + 1))
                    for i, cols in enumerate((slice(0, P), slice(P, BANDS))):
                        act.activation(prob[:, s % 2, cols], psum[:, SCOREB[s % 2], cols], ACT.Exp,
                                       bias=neg_max[:, s % 2, i:i + 1],
                                       accum_out=sums[:, s % 2, i:i + 1]).then_inc(exp_done, 1)

                def turn_probs(g, s):
                    act.wait_ge(p_turned, STEPS * g + (s + 1))
                    act.activation(pt_h[:, s % 2, :], psum[:, PTURNB, 0:BANDS], ACT.Copy).then_inc(p_hi, 1)

                def values(g, s):
                    act.wait_ge(pv_done, STEPS * g + (s + 1))
                    act.activation(ot_h[:, s % 2, :], psum[:, PVB, 0:S], ACT.Copy).then_inc(o_hi, 1)

                run(act, dict(turn_q=turn_q, turn_k=turn_k, kv=kv, softmax=softmax, turn_probs=turn_probs, values=values,
                              weights=weights))

            @block.gpsimd
            def _(pool):
                def weights(_, g, piece):
                    hi, lo, raw, row, rows, cols = weight_piece(piece)
                    where = ds((g & 1) * raw.shape[1] + row, rows)
                    src = raw[:, row:row + rows, cols]
                    pool.wait_ge(w_hi, PIECES * g + (piece + 1))
                    ins = pool.tensor_tensor(lo[:, where, cols], src, f(hi[:, where, cols]), ALU.subtract)
                    if piece == PIECES - 1:
                        ins.then_inc(w_ready, 1)

                for piece in range(PIECES):
                    weights(0, 0, piece)
                norm.gpsimd(pool)

                def q(_, g, m, i):
                    pool.wait_ge(parts, q_index(g, m, i) + 1)
                    before = turn_index(g, m - 1, 1) if m else k_turn_index(g, 0) - 1
                    if not known(before, 0):
                        pool.wait_ge(qk_turned, before + 1)
                    slot = q_index(0, m, i) % 2
                    pool.tensor_tensor(qr[:, i, :], part_a[:, slot, :], part_b[:, slot, :], ALU.add).then_inc(roped, 1)

                def kv(_, g, b):
                    index = kv_index(g, b)
                    pool.wait_ge(parts, index + 1)
                    slot = kv_index(0, b) % 2
                    cols = slice(0, 2 * HD1)
                    pool.tensor_tensor(kr[:].rearrange("p t n -> p (t n)"), part_a[:, slot, cols], part_b[:, slot, cols],
                                       ALU.add).then_inc(roped, 1)

                def softmax(g, s):
                    pool.wait_ge(rden_ready, STEPS * g + (s + 1))
                    for i, cols in enumerate((slice(0, P), slice(P, BANDS))):
                        at = prob[:, s % 2, cols]
                        ins = pool.tensor_tensor(at, at, rden[:, s % 2, i:i + 1].to_broadcast([P, (i + 1) * P]), ALU.mult)
                    ins.then_inc(p_normed, 1)

                run(pool, dict(q=q, kv=kv, softmax=softmax, weights=weights))

            @block.vector
            def _(dve):
                norm.vector(dve, core.x)
                dve.wait_ge(loaded_c, 16 * 4)
                dve.tensor_scalar(tables[:, 0], tables[:, 1], HD1 ** -0.5, None, ALU.mult).then_inc(tables_own, 1)
                dve.wait_ge(tables_own, 1)

                def rope(slot, src, kind, t, heads):
                    cos, sin = ((tables[:, kind, n, t:t + 1, :] if t is not None else tables[:, kind, n, :, :])
                                .to_broadcast([P, heads, HD1]) for n in range(2))
                    a, b = (x[:, slot, 0:heads * HD1].rearrange("p (h n) -> p h n", h=heads) for x in (part_a, part_b))
                    dve.tensor_tensor(a, src, cos, ALU.mult)
                    for c in range(2):
                        lo, hi = slice(c * HD1 // 2, (c + 1) * HD1 // 2), slice((1 - c) * HD1 // 2, (2 - c) * HD1 // 2)
                        ins = dve.tensor_tensor(b[:, :, lo], src[:, :, hi], sin[:, :, lo], ALU.mult)
                    return ins

                def q(_, g, m, i):
                    index = q_index(g, m, i)
                    dve.wait_ge(projected, index + 1)
                    if not known(index, 2):
                        dve.wait_ge(roped, index - 1)
                    rope(q_index(0, m, i) % 2, psum[:, PROJB[i], :].rearrange("p (h n) -> p h n", h=QB), 0, i, QB)\
                        .then_inc(parts, 1)

                def kv(_, g, b):
                    index = kv_index(g, b)
                    dve.wait_ge(v_hi, B * g + (b + 1))
                    if not known(index, 2):
                        dve.wait_ge(roped, index - 1)
                    bank = psum[:, PROJB[0], :].rearrange("p (t n) -> p t n", t=2)
                    dve.tensor_tensor(v_l[:, b % 2, :, :], bank[:, :, HD1:], f(v_h[:, b % 2, :, :]), ALU.subtract)
                    rope(kv_index(0, b) % 2, bank[:, :, 0:HD1], 1, None, 2).then_inc(parts, 1)

                def turn_q(_, g, m, c):
                    dve.wait_ge(qk_hi, turn_index(g, m, c) + 1)
                    at = q_h[:, m % 2, 2 * c:2 * c + 2, :]
                    dve.tensor_tensor(q_l[:, m % 2, 2 * c:2 * c + 2, :], psum[:, TURNB, :].rearrange("p (h n) -> p h n", h=2),
                                      f(at), ALU.subtract).then_inc(qk_lo, 1)

                def turn_k(_, g, b):
                    dve.wait_ge(qk_hi, k_turn_index(g, b) + 1)
                    dve.tensor_tensor(k_l[:, b % 2, :], psum[:, TURNB, 0:S], f(k_h[:, b % 2, :]),
                                      ALU.subtract).then_inc(qk_lo, 1)

                def scores(g, s):
                    dve.wait_ge(scored, STEPS * g + (s + 1))
                    for i, cols in enumerate((slice(0, P), slice(P, BANDS))):
                        ins = dve.tensor_reduce(neg_max[:, s % 2, i:i + 1], psum[:, SCOREB[s % 2], cols], AX.X, ALU.max,
                                                negate=True)
                    ins.then_inc(max_ready, 1)

                def turn_probs(g, s):
                    dve.wait_ge(p_hi, STEPS * g + (s + 1))
                    dve.tensor_tensor(pt_l[:, s % 2, :], psum[:, PTURNB, 0:BANDS], f(pt_h[:, s % 2, :]),
                                      ALU.subtract).then_inc(p_lo, 1)

                def softmax(g, s):
                    dve.wait_ge(exp_done, 2 * STEPS * g + (2 * s + 2 + 4))
                    dve.reciprocal(rden[:, s % 2, :], sums[:, s % 2, :]).then_inc(rden_ready, 1)

                def values(g, s):
                    dve.wait_ge(o_hi, STEPS * g + (s + 1))
                    dve.tensor_tensor(ot_l[:, s % 2, :], psum[:, PVB, 0:S], f(ot_h[:, s % 2, :]),
                                      ALU.subtract).then_inc(o_lo, 1)

                def project_out(g, s):
                    if s % REP1 != REP1 - 1:
                        return
                    b = s // REP1
                    dve.wait_ge(wo_done, B * g + (b + 1))
                    dve.wait_ge(z_added, B * g + (b + 1))
                    at = z[:, 2 * b:2 * b + 2, :]
                    dve.tensor_tensor(at, psum[:, WOB, :].rearrange("p (t n) -> p t n", t=2), at, ALU.add)\
                        .then_inc(z_added, 1)

                run(dve, dict(q=q, kv=kv, turn_q=turn_q, turn_k=turn_k, scores=scores, turn_probs=turn_probs,
                              softmax=softmax, values=values, project_out=project_out))

            @block.tensor
            def _(pe):
                norm.tensor(pe)
                for half in range(2):
                    norm.ready(pe, half)
                pe.sem_inc(exp_done, 4)
                pe.sem_inc(z_added, B)
                pe.sem_inc(p_lo, 1)
                pe.sem_inc(o_lo, 1)

                def q(_, g, m, i):
                    before = bank_user_before(q_index(g, m, i), m, i)
                    bank = psum[:, PROJB[i], :]
                    if not known(before, 0):
                        pe.wait_ge(parts, before + 1)
                    if m == 0 and i == 0:
                        pe.wait_ge(w_ready, g + 1)
                    b = m // 2
                    for k in range(KD):
                        where = ds((g & 1) * KD + k, 1)
                        cols = slice((m % 2) * QC, (m % 2 + 1) * QC)
                        ins = product(pe, bank, core.xt(k, slice(b * S + i * P, b * S + (i + 1) * P)),
                                      (wq_h[:, where, cols], wq_l[:, where, cols]), k == 0, k == KD - 1)
                    ins.then_inc(projected, 1)

                def bank_user_before(index, m, i):
                    if i == 1:
                        return index - (2 if m % 2 == 1 else 3)
                    return index - (2 if m % 2 == 1 else 1)

                def kv(_, g, b):
                    index = kv_index(g, b)
                    if not known(index, 1):
                        pe.wait_ge(parts, index - 2 + 1)
                    pe.wait_ge(w_ready, g + 1)
                    for i in range(2):
                        for k in range(KD):
                            where = ds((g & 1) * KD + k, 1)
                            ins = product(pe, psum[:, PROJB[0], i * 2 * HD1:(i + 1) * 2 * HD1],
                                          core.xt(k, slice(b * S + i * P, b * S + (i + 1) * P)),
                                          (wkv_h[:, where, :], wkv_l[:, where, :]), k == 0, k == KD - 1)
                    ins.then_inc(projected, 1)

                def turn_q(_, g, m, c):
                    index = turn_index(g, m, c)
                    pe.wait_ge(roped, q_index(g, m, 1) + 1)
                    pe.wait_ge(qk_lo, index)
                    for hh in range(2):
                        for i in range(2):
                            head = 2 * c + hh
                            ins = pe.transpose(psum[:, TURNB, hh * S + i * P:hh * S + (i + 1) * P],
                                               qr[:, i, head * HD1:(head + 1) * HD1], core.ident[:])
                    ins.then_inc(qk_turned, 1)

                def turn_k(_, g, b):
                    index = k_turn_index(g, b)
                    pe.wait_ge(roped, kv_index(g, b) + 1)
                    if not known(index, 1):
                        pe.wait_ge(qk_lo, index)
                    for i in range(2):
                        ins = pe.transpose(psum[:, TURNB, i * P:(i + 1) * P], kr[:, i, :], core.ident[:])
                    ins.then_inc(qk_turned, 1)

                def scores(g, s):
                    b, h = s // REP1, s % REP1
                    m, c = 2 * b + h // QB, (h % QB) // 2
                    pe.wait_ge(qk_lo, turn_index(g, m, c) + 1)
                    pe.wait_ge(exp_done, 2 * STEPS * g + (2 * s + 2))
                    bank = psum[:, SCOREB[s % 2], :]
                    qt = (q_h[:, m % 2, h % QB, :], q_l[:, m % 2, h % QB, :])
                    kt = (k_h[:, b % 2, :], k_l[:, b % 2, :])
                    for i, cols, keys in ((0, slice(0, P), slice(0, P)), (1, slice(P, BANDS), slice(0, S))):
                        product(pe, bank[:, cols], tuple(a[:, i * P:(i + 1) * P] for a in qt),
                                tuple(a[:, keys] for a in kt), True, False, True)
                        ins = pe.matmul(bank[:, cols.stop - P:cols.stop], core.ident_bf[:], mask[:], start=False, stop=True,
                                        skip_group_check=True)
                    ins.then_inc(scored, 1)

                def turn_probs(g, s):
                    pe.wait_ge(p_normed, STEPS * g + (s + 1))
                    pe.wait_ge(p_lo, STEPS * g + (s + 1))
                    for i in range(3):
                        ins = pe.transpose(psum[:, PTURNB, i * P:(i + 1) * P], prob[:, s % 2, i * P:(i + 1) * P],
                                           core.ident[:])
                    ins.then_inc(p_turned, 1)

                def values(g, s):
                    b = s // REP1
                    pe.wait_ge(p_lo, STEPS * g + (s + 2))
                    pe.wait_ge(o_lo, STEPS * g + (s + 1))
                    v = [(v_h[:, b % 2, i, :], v_l[:, b % 2, i, :]) for i in range(2)]
                    pt = (pt_h[:, s % 2, :], pt_l[:, s % 2, :])
                    product(pe, psum[:, PVB, 0:S], v[0], tuple(a[:, 0:S] for a in pt), True, False, True)
                    product(pe, psum[:, PVB, P:S], v[1], tuple(a[:, S:] for a in pt), False, True, True)\
                        .then_inc(pv_done, 1)

                def project_out(g, s):
                    b, h = s // REP1, s % REP1
                    pe.wait_ge(o_lo, STEPS * g + (s + 2))
                    if h == 0:
                        pe.wait_ge(z_added, B * g + (b + B))
                    where = ds((g & 1) * REP1 + h, 1)
                    for i in range(2):
                        ins = product(pe, psum[:, WOB, i * D:(i + 1) * D],
                                      (ot_h[:, s % 2, i * P:(i + 1) * P], ot_l[:, s % 2, i * P:(i + 1) * P]),
                                      (wo_h[:, where, :], wo_l[:, where, :]), h == 0 and i == 0, h == REP1 - 1, True)
                    if h == REP1 - 1:
                        ins.then_inc(wo_done, 1)

                run(pe, dict(q=q, kv=kv, turn_q=turn_q, turn_k=turn_k, scores=scores, turn_probs=turn_probs,
                             values=values, project_out=project_out))


def experts(core, z, ln2_w, w_router, bias, w_gate, w_up, w_down, shared_gate, shared_up, shared_down, out):
    nc, sem, psum = core.nc, core.sem, core.psum
    scope, sb = core.stage()
    SHARED = NE
    with scope:
        ln_w = sb("ln2_w", [P, KD], F32)
        norm = Norm(core, "ln4", sb, 1e-5, weight=ln_w, rms=True)
        wr_raw = sb("wr_raw", [P, KD, NE], F32)
        wr_h, wr_l = (sb(f"wr_{n}", [P, KD, NE], F32R) for n in "hl")
        bias_sb = sb("bias_sb", [P, NE], F32)
        score = sb("score", [P, NT, NE], F32)
        biased = sb("biased", [P, NT, NE], F32)
        top = sb("top", [P, NT, TOPK], F32)
        rest = sb("rest", [P, NT, NE], F32)
        total = sb("total", [P, NT], F32)
        weight = sb("weight", [P, NE + 1, NT], F32)
        raw = sb("raw", [P, 2, 3, KD * FI], F32)
        gu_h, gu_l = (sb(f"gu_{n}", [P, 2, 2, KD, FI], F32R) for n in "hl")
        wd_h, wd_l = (sb(f"wd_{n}", [P, 2, D], F32R) for n in "hl")
        silu = sb("silu", [P, 2, HALF], F32)
        hid = sb("hid", [P, 2, HALF], F32)
        hid_h, hid_l = (sb(f"hid_{n}", [P, 2, T], F32R) for n in "hl")

        loaded_c = sem("e_constants_loaded")
        loaded = [sem(f"e_expert_loaded_{j}") for j in range(2)]
        wr_own = sem("e_router_high")
        wr_ready = sem("e_router_split")
        logits = sem("e_logits")
        sig = sem("e_scores")
        own_dve = sem("e_vector_written")
        gu_hi = sem("e_gate_up_high")
        gu_ready = sem("e_gate_up_split")
        wd_hi = sem("e_down_high")
        wd_ready = sem("e_down_split")
        gu_done = sem("e_gate_up_done")
        silu_done = sem("e_silu_done")
        hid_ready = sem("e_hidden_ready")
        hid_hi = sem("e_hidden_high")
        hid_lo = sem("e_hidden_low")
        down_done = sem("e_down_done")
        added = sem("e_added")
        stored = sem("e_stored")
        GATEB, UPB, DOWNB = 0, 2, 4

        def run(eng, step):
            step(0, 0)
            step(1, 1)
            with eng.Fori(1, NE // 2) as i:
                for j in range(2):
                    step(2 * i + j, j)
            step(SHARED, 0)

        with nc.Block() as block:
            @block.sync
            def _(sp):
                with nc.allow_non_contiguous_dma(reason="a norm's weights"):
                    sp.dma_start(ln_w[:], ln2_w.rearrange("(k p) -> p k", p=P)).then_inc(loaded_c, 16)
                sp.dma_start(wr_raw[:], w_router.rearrange("(k p) n -> p k n", p=P)).then_inc(loaded_c, 16)
                sp.dma_start(bias_sb[:], bias.rearrange("(a n) -> a n", a=1).to_broadcast([P, NE])).then_inc(loaded_c, 16)

                def load(e, j):
                    for n, w in enumerate((w_gate, w_up)):
                        src = shared_gate if n == 0 else shared_up
                        if not isinstance(e, int) or e < NE:
                            src = w.rearrange("e (k p) n -> p e k n", p=P)[:, ds(e, 1)]
                            sp.dma_start(raw[:, j, n:n + 1, :].rearrange("p a (k n) -> p a k n", k=KD), src)\
                                .then_inc(loaded[j], 16)
                        else:
                            sp.dma_start(raw[:, j, n, :].rearrange("p (k n) -> p k n", k=KD),
                                         src.rearrange("(k p) n -> p k n", p=P)).then_inc(loaded[j], 16)
                    src = w_down.rearrange("e p n -> p e n")[:, ds(e, 1)] if not isinstance(e, int) or e < NE else \
                        shared_down.rearrange("p (a n) -> p a n", a=1)
                    sp.dma_start(raw[:, j, 2:3, :], src).then_inc(loaded[j], 16)

                load(0, 0)
                load(1, 1)
                with sp.Fori(1, NE // 2) as i:
                    for j in range(2):
                        sp.wait_ge(wd_ready, 2 * i + (j - 1))
                        load(2 * i + j, j)
                sp.wait_ge(wd_ready, SHARED - 1)
                load(SHARED, 0)
                for t in range(NT):
                    sp.wait_ge(added, NT * (NE + 1) + t + 1)
                    sp.dma_start(out[t * P:(t + 1) * P, :], core.x[:, t, :]).then_inc(stored, 16)
                sp.wait_ge(stored, 16 * NT)

            @block.scalar
            def _(act):
                act.wait_ge(loaded_c, 16 * 3)
                norm.scalar(act)
                act.wait_ge(logits, 1)
                act.activation(score[:], psum[:, 4, 0:NT * NE].rearrange("p (t e) -> p t e", t=NT),
                               ACT.Sigmoid).then_inc(sig, 1)

                def split_gu(e, j):
                    act.wait_ge(loaded[j], 24 * e + (48 - 24 * j))
                    if not isinstance(e, int) or e >= 2:
                        act.wait_ge(gu_done, 2 * e - 2)
                    act.activation(gu_h[:, j], raw[:, j, 0:2, :].rearrange("p a (k n) -> p a k n", k=KD),
                                   ACT.Copy).then_inc(gu_hi, 1)

                def split_down(e, j):
                    if not isinstance(e, int) or e >= 2:
                        act.wait_ge(down_done, NT * e - NT)
                    act.activation(wd_h[:, j], raw[:, j, 2, :], ACT.Copy).then_inc(wd_hi, 1)

                split_gu(0, 0)

                def step(e, j):
                    split_down(e, j)
                    if not isinstance(e, int) or e < SHARED:
                        split_gu(e + 1, 1 - j)
                    for c in range(2):
                        cols = slice(c * HALF, (c + 1) * HALF)
                        act.wait_ge(gu_done, 2 * e + (c + 1))
                        if not isinstance(e, int) or e > 0:
                            act.wait_ge(hid_ready, 2 * e + (c - 1))
                        act.activation(silu[:, c, :], psum[:, GATEB + c, :], ACT.Silu).then_inc(silu_done, 1)
                        act.wait_ge(hid_ready, 2 * e + (c + 1))
                        act.activation(hid_h[:, j, cols], hid[:, c, :], ACT.Copy).then_inc(hid_hi, 1)

                run(act, step)

            @block.gpsimd
            def _(pool):
                pool.wait_ge(loaded_c, 16 * 3)
                pool.tensor_copy(wr_h[:], wr_raw[:]).then_inc(wr_own, 1)
                pool.wait_ge(wr_own, 1)
                pool.tensor_tensor(wr_l[:], wr_raw[:], f(wr_h[:]), ALU.subtract).then_inc(wr_ready, 1)
                norm.gpsimd(pool)

                def split_gu(e, j):
                    src = raw[:, j, 0:2, :].rearrange("p a (k n) -> p a k n", k=KD)
                    pool.wait_ge(gu_hi, e + 1)
                    pool.tensor_tensor(gu_l[:, j], src, f(gu_h[:, j]), ALU.subtract).then_inc(gu_ready, 1)

                def split_down(e, j):
                    pool.wait_ge(wd_hi, e + 1)
                    pool.tensor_tensor(wd_l[:, j], raw[:, j, 2, :], f(wd_h[:, j]), ALU.subtract).then_inc(wd_ready, 1)

                split_gu(0, 0)

                def step(e, j):
                    split_down(e, j)
                    if not isinstance(e, int) or e < SHARED:
                        split_gu(e + 1, 1 - j)
                    for c in range(2):
                        cols = slice(c * HALF, (c + 1) * HALF)
                        pool.wait_ge(hid_hi, 2 * e + (c + 1))
                        pool.tensor_tensor(hid_l[:, j, cols], hid[:, c, :], f(hid_h[:, j, cols]), ALU.subtract)\
                            .then_inc(hid_lo, 1)

                run(pool, step)

            @block.vector
            def _(dve):
                norm.vector(dve, z)
                own = Count(dve, own_dve)
                for t in range(NT):
                    dve.tensor_tensor(core.x[:, t, :], core.x[:, t, :], z[:, t, :], ALU.add).then_inc(added, 1)
                own.add(dve.memset(weight[:, NE, :], 1.0))
                dve.wait_ge(loaded_c, 16 * 3)
                dve.wait_ge(sig, 1)
                own.add(dve.tensor_tensor(biased[:], score[:],
                                          bias_sb[:].rearrange("p (t e) -> p t e", t=1).to_broadcast([P, NT, NE]), ALU.add))
                own.settle()
                for t in range(NT):
                    own.add(dve.max(top[:, t, :], biased[:, t, :]))
                own.settle()
                for t in range(NT):
                    own.add(dve.match_replace(rest[:, t, :], top[:, t, :], biased[:, t, :], MASKED))
                own.settle()
                own.add(dve.tensor_tensor(biased[:], biased[:], rest[:], ALU.not_equal))
                own.settle()
                own.add(dve.tensor_tensor(score[:], score[:], biased[:], ALU.mult))
                own.settle()
                own.add(dve.tensor_reduce(total[:], score[:], AX.X, ALU.add))
                own.settle()
                own.add(dve.reciprocal(total[:], total[:]))
                own.settle()
                own.add(dve.tensor_tensor(weight[:, 0:NE, :], score[:].rearrange("p t e -> p e t"),
                                          total[:].rearrange("p (e t) -> p e t", e=1).to_broadcast([P, NE, NT]), ALU.mult))
                own.settle()

                def add(e, t):
                    dve.wait_ge(down_done, NT * e + ((t | 1) + 1))
                    dve.wait_ge(added, NT * e + (t + 1))
                    src = psum[:, DOWNB + t // 2, (t % 2) * D:(t % 2 + 1) * D]
                    scale = weight[:, ds(e, 1), t] if not isinstance(e, int) else weight[:, e, t:t + 1]
                    dve.scalar_tensor_tensor(core.x[:, t, :], src, scale, core.x[:, t, :], ALU.mult, ALU.add)\
                        .then_inc(added, 1)

                def step(e, j):
                    for c in range(2):
                        dve.wait_ge(silu_done, 2 * e + (c + 1))
                        if not isinstance(e, int) or e > 0:
                            dve.wait_ge(hid_lo, 2 * e + (c - 1))
                        dve.tensor_tensor(hid[:, c, :], psum[:, UPB + c, :], silu[:, c, :], ALU.mult)\
                            .then_inc(hid_ready, 1)
                        if not isinstance(e, int) or e > 0:
                            for t in range(c * TH, (c + 1) * TH):
                                add(e - 1, t)

                run(dve, step)
                for t in range(NT):
                    add(SHARED, t)

            @block.tensor
            def _(pe):
                norm.tensor(pe)
                pe.wait_ge(wr_ready, 1)
                for t in range(NT):
                    norm.ready(pe, t // TH)
                    for k in range(KD):
                        ins = product(pe, psum[:, 4, t * NE:(t + 1) * NE], core.xt(k, slice(t * P, (t + 1) * P)),
                                      (wr_h[:, k, :], wr_l[:, k, :]), k == 0, k == KD - 1)
                ins.then_inc(logits, 1)
                pe.wait_ge(sig, 1)

                def down(e, t, j):
                    if t % 2 == 0:
                        pe.wait_ge(added, NT * e + (t + 2))
                    cols = slice(t * P, (t + 1) * P)
                    product(pe, psum[:, DOWNB + t // 2, (t % 2) * D:(t % 2 + 1) * D],
                            (hid_h[:, j, cols], hid_l[:, j, cols]), (wd_h[:, j, :], wd_l[:, j, :])).then_inc(down_done, 1)

                def down_half(e, c, j):
                    if c == 0:
                        pe.wait_ge(wd_ready, e + 1)
                    pe.wait_ge(hid_lo, 2 * e + (c + 1))
                    for t in range(c * TH, (c + 1) * TH):
                        down(e, t, j)

                def step(e, j):
                    pe.wait_ge(gu_ready, e + 1)
                    for c in range(2):
                        if not isinstance(e, int) or e > 0:
                            pe.wait_ge(hid_ready, 2 * e + (c - 1))
                        for n, bank in enumerate((GATEB + c, UPB + c)):
                            for k in range(KD):
                                ins = product(pe, psum[:, bank, :], (gu_h[:, j, n, k, :], gu_l[:, j, n, k, :]),
                                              core.xt(k, slice(c * HALF, (c + 1) * HALF)), k == 0, k == KD - 1)
                        ins.then_inc(gu_done, 1)
                        if not isinstance(e, int) or e > 0:
                            down_half(e - 1, c, 1 - j)

                run(pe, step)
                for c in range(2):
                    down_half(SHARED, c, 0)

_INS = ['L0_attn_hidden_states', 'L0_attn_w_qkv', 'L0_attn_q_norm_w', 'L0_attn_k_norm_w', 'L0_attn_w_o',
        'L0_ffn_w_up_q', 'L0_ffn_w_up_scale', 'L0_ffn_b_up', 'L0_ffn_w_up_lora_a', 'L0_ffn_w_up_lora_b',
        'L0_ffn_w_down_q', 'L0_ffn_w_down_scale', 'L0_ffn_b_down', 'L0_ffn_w_down_lora_a', 'L0_ffn_w_down_lora_b',
        'L1_attn_W_xproj', 'L1_attn_b_xproj', 'L1_attn_W_dt', 'L1_attn_b_dt', 'L1_attn_A_log',
        'L1_ffn_ln1_w', 'L1_ffn_ln2_w', 'L1_ffn_Wq', 'L1_ffn_Wk', 'L1_ffn_Wv', 'L1_ffn_Wo', 'L1_ffn_Wr',
        'L1_ffn_expert_bias', 'L1_ffn_Wg', 'L1_ffn_Wu', 'L1_ffn_Wd', 'L1_ffn_Wsg', 'L1_ffn_Wsu', 'L1_ffn_Wsd']
_TURNED = ['L0_attn_w_qkv', 'L0_attn_w_o', 'L0_ffn_w_up_q', 'L0_ffn_w_up_scale', 'L0_ffn_w_up_lora_a',
           'L0_ffn_w_down_q', 'L0_ffn_w_down_scale', 'L0_ffn_w_down_lora_a', 'L1_attn_W_xproj', 'L1_attn_W_dt']


def program(nc, a, consts, out):
    with ExitStack() as ctx:
        core = Core(nc, ctx)
        windowed_attention(core, a["L0_attn_hidden_states"], a["L0_attn_w_qkv"], a["L0_attn_q_norm_w"],
                           a["L0_attn_k_norm_w"], a["L0_attn_w_o"], consts)
        quantized_ffn(core, *(a["L0_ffn_" + n] for n in (
            "w_up_q", "w_up_scale", "b_up", "w_up_lora_a", "w_up_lora_b",
            "w_down_q", "w_down_scale", "b_down", "w_down_lora_a", "w_down_lora_b")))
        selective_scan(core, *(a["L1_attn_" + n] for n in ("W_xproj", "b_xproj", "W_dt", "b_dt", "A_log")), consts)
        z = ctx.enter_context(nc.sbuf_tensor("z", [P, NT, D], F32))
        causal_attention(core, z, *(a["L1_ffn_" + n] for n in ("ln1_w", "Wq", "Wk", "Wv", "Wo")), consts)
        experts(core, z, *(a["L1_ffn_" + n] for n in (
            "ln2_w", "Wr", "expert_bias", "Wg", "Wu", "Wd", "Wsg", "Wsu", "Wsd")), out)




_OUTS = [((B, S, D), "float32")]


def _constants():
    def rope(positions, width, heads):
        inv = (np.float32(1.0) / np.float32(10000.0) ** (np.arange(0, width, 2, dtype=np.float32) / np.float32(width)))
        ang = np.arange(positions, dtype=np.float32)[:, None] * inv.astype(np.float32)[None, :]
        cos, sin = np.cos(ang).astype(np.float32), np.sin(ang).astype(np.float32)
        return (np.tile(np.concatenate([cos, cos], 1), (1, heads)), np.tile(np.concatenate([-sin, sin], 1), (1, heads)))

    bf16 = mybir.dt.np(BF16)
    i = np.arange(P)
    causal = np.where(i[None, :] <= i[:, None], 0.0, MASKED)
    beyond = np.where(i[None, :] > i[:, None], 0.0, MASKED)
    cos0, sin0 = rope(S, HD0, NH0)
    cos1, sin1 = rope(S, HD1, 1)
    one_hot = np.zeros((3 * 2 * NS, 2 * NS, P), np.float32)
    for part in range(3):
        for n in range(2 * NS):
            one_hot[part * 2 * NS + n, n, :] = 1.0
    even = ((i // HD0) % 2 == 0).astype(np.float32)
    return {
        "ident": np.eye(P, dtype=np.float32), "ident_bf": np.eye(P, dtype=bf16),
        "cos0": cos0, "sin0": sin0, "cos1": cos1, "sin1": sin1,
        "parity": np.stack([even, 1 - even], 1),
        "window_mask": np.concatenate([causal, beyond, causal], 1).astype(bf16),
        "causal_mask": causal.astype(bf16),
        "one_hot": one_hot.astype(bf16),
    }


def kernel(**inputs):
    import concourse.bacc as _bacc
    from concourse.bass_utils import run_bass_kernel_spmd as _run

    def laid_out(name):
        a = np.asarray(inputs[name])
        if name in _TURNED:
            a = a.T
        if name == "L0_attn_hidden_states":
            a = a.reshape(T, D)
        return np.ascontiguousarray(a)

    nc = _bacc.Bacc("TRN2", target_bir_lowering=False, num_devices=1)
    arrays, args, consts = {}, {}, {}
    for into, given in ((args, {n: laid_out(n) for n in _INS}), (consts, _constants())):
        for name, a in given.items():
            arrays[f"in_{name}_dram"] = a
            into[name] = nc.dram_tensor(f"in_{name}_dram", a.shape, mybir.dt.from_np(a.dtype), kind="ExternalInput").ap()
    out = nc.dram_tensor("out_0_dram", _OUTS[0][0], F32, kind="ExternalOutput").ap()
    program(nc, args, consts, out.rearrange("b s d -> (b s) d"))
    r = _run(nc, [arrays], core_ids=[0])
    return r.results[0]["out_0_dram"]
```

```python
from contextlib import ExitStack

import numpy as np

import concourse.bass as bass
from concourse import mybir

F32 = mybir.dt.float32
F32R = mybir.dt.float32r
BF16 = mybir.dt.bfloat16
I32 = mybir.dt.int32
ALU = mybir.AluOpType
ACT = mybir.ActivationFunctionType
AX = mybir.AxisListType
ds = bass.ds

P = 128
B, S, D = 4, 256, 256
T = B * S
NT = T // P
KD = D // P
HALF = T // 2
TH = NT // 2
MASKED = -1e30

NH0, HD0 = 16, 16
FF = 1024
KF = FF // P
RANK = 16
DR, NS = 128, 16
NH1, KVH1, HD1 = 32, 4, 128
REP1 = NH1 // KVH1
NE, TOPK, FI = 32, 8, 128


class Count:

    def __init__(self, eng, sem):
        self.eng, self.sem, self.n = eng, sem, 0

    def add(self, ins):
        ins.then_inc(self.sem, 1)
        self.n += 1

    def settle(self):
        self.eng.wait_ge(self.sem, self.n)


def f(ap):
    return ap.bitcast(F32)


def product(pe, out, lhs, rhs, start=True, stop=True, shared=False):
    (lh, ll), (rh, rl) = lhs, rhs
    pe.matmul(out, ll, rh, start=start, stop=False, skip_group_check=shared)
    pe.matmul(out, lh, rl, start=False, stop=False, skip_group_check=shared)
    return pe.matmul(out, lh, rh, start=False, stop=stop, skip_group_check=shared)


class Norm:

    def __init__(self, core, tag, sb, eps, weight=None, twice=None, rms=False, plain=None, z=None):
        self.c, self.eps, self.weight, self.twice, self.rms, self.plain, self.z = core, eps, weight, twice, rms, plain, z
        sem = core.sem
        self.own = sem(f"{tag}_stats_written")
        self.var_ready = sem(f"{tag}_variance_ready")
        self.rstd_ready = sem(f"{tag}_rstd_ready")
        self.normed = sem(f"{tag}_tile_normed")
        self.turned = sem(f"{tag}_half_turned")
        self.hi_ready = sem(f"{tag}_high_ready")
        self.lo_ready = sem(f"{tag}_low_ready")
        self.st = sb(f"{tag}_stats", [P, NT, 6], F32)
        self.mv = sb(f"{tag}_mean_var", [P, NT, 2], F32)
        self.ve = sb(f"{tag}_var_eps", [P, NT], F32)
        self.rs = sb(f"{tag}_rstd", [P, NT], F32)
        self.ve2 = sb(f"{tag}_var_eps2", [P, NT], F32)
        self.rs2 = sb(f"{tag}_rstd2", [P, NT], F32)
        self.y = sb(f"{tag}_y", [P, NT, D], F32)

    def vector(self, dve, x, arrived=None, meanwhile=None):
        own = Count(dve, self.own)
        halves = [slice(h * TH, (h + 1) * TH) for h in range(2)]
        for h, ts in enumerate(halves):
            if arrived is not None:
                dve.wait_ge(*arrived[h])
            for t in range(h * TH, (h + 1) * TH):
                own.add(dve.bn_stats(self.st[:, t, :], x[:, t, :]))
            for t in range(h * TH, (h + 1) * TH):
                dve.wait_ge(self.own, own.n - TH + 1)
                own.add(dve.bn_aggr(self.mv[:, t, :], self.st[:, t, :]))
            own.settle()
            if self.rms:
                own.add(dve.tensor_tensor(self.ve2[:, ts], self.mv[:, ts, 0], self.mv[:, ts, 0], ALU.mult))
                own.settle()
                dve.scalar_tensor_tensor(self.ve[:, ts], self.ve2[:, ts], self.eps, self.mv[:, ts, 1], ALU.add,
                                         ALU.add).then_inc(self.var_ready, 1)
            else:
                dve.tensor_scalar(self.ve[:, ts], self.mv[:, ts, 1], self.eps, None, ALU.add).then_inc(self.var_ready, 1)
        if meanwhile is not None:
            meanwhile()
        scale = self.rs
        if self.twice is not None:
            for h, ts in enumerate(halves):
                dve.wait_ge(self.rstd_ready, h + 1)
                own.add(dve.tensor_tensor(self.ve2[:, ts], self.rs[:, ts], self.rs[:, ts], ALU.mult))
                own.settle()
                own.add(dve.tensor_tensor(self.ve2[:, ts], self.ve2[:, ts], self.mv[:, ts, 1], ALU.mult))
                own.settle()
                dve.tensor_scalar(self.ve2[:, ts], self.ve2[:, ts], self.twice, None, ALU.add).then_inc(self.var_ready, 1)
            scale = self.rs2
        for h, ts in enumerate(halves):
            if self.twice is not None:
                dve.wait_ge(self.rstd_ready, 2 + h + 1)
                own.add(dve.tensor_tensor(self.rs2[:, ts], self.rs2[:, ts], self.rs[:, ts], ALU.mult))
                own.settle()
            else:
                dve.wait_ge(self.rstd_ready, h + 1)
            for t in range(h * TH, (h + 1) * TH):
                if self.rms:
                    ins = dve.tensor_scalar(self.y[:, t, :], x[:, t, :], scale[:, t:t + 1], None, ALU.mult)
                else:
                    ins = dve.tensor_scalar(self.y[:, t, :], x[:, t, :], self.mv[:, t, 0:1], scale[:, t:t + 1],
                                            ALU.subtract, ALU.mult)
                ins.then_inc(self.normed, 1)
        self.low(dve)
        if self.z is not None:
            for t in range(NT):
                own.add(dve.tensor_scalar(self.z[:, t, :], x[:, t, :], self.mv[:, t, 0:1], self.rs[:, t:t + 1],
                                          ALU.subtract, ALU.mult))
        own.settle()

    def low(self, dve):
        for n, (half, k) in enumerate((h, k) for h in range(2) for k in range(KD)):
            bank = self.c.psum[:, 2 * half + k, :]
            cols = slice(half * HALF, half * HALF + HALF)
            dve.wait_ge(self.hi_ready, n + 1)
            if self.plain is not None:
                dve.tensor_copy(self.plain[:, k, cols], bank).then_inc(self.lo_ready, 1)
            elif self.weight is not None:
                dve.scalar_tensor_tensor(self.c.xt_l[:, k, cols], bank, self.weight[:, k:k + 1],
                                         f(self.c.xt_h[:, k, cols]), ALU.mult, ALU.subtract).then_inc(self.lo_ready, 1)
            else:
                dve.tensor_tensor(self.c.xt_l[:, k, cols], bank, f(self.c.xt_h[:, k, cols]),
                                  ALU.subtract).then_inc(self.lo_ready, 1)

    def gpsimd(self, pool):
        for n in range(2 if self.twice is None else 4):
            ts = slice(n % 2 * TH, (n % 2 + 1) * TH)
            to, src = ((self.rs, self.ve), (self.rs2, self.ve2))[n // 2]
            pool.wait_ge(self.var_ready, n + 1)
            pool.tensor_tensor(to[:, ts], src[:, ts], self.c.neg_half[:, 0:TH], ALU.pow).then_inc(self.rstd_ready, 1)

    def tensor(self, pe, y=None):
        for half in range(2):
            for t in range(half * TH, half * TH + TH):
                pe.wait_ge(self.normed, t + 1)
                for k in range(KD):
                    ins = pe.transpose(self.c.psum[:, 2 * half + k, (t - half * TH) * P:(t - half * TH + 1) * P],
                                       self.y[:, t, k * P:(k + 1) * P], self.c.ident[:])
            ins.then_inc(self.turned, 1)

    def scalar(self, act):
        for n, (half, k) in enumerate((h, k) for h in range(2) for k in range(KD)):
            act.wait_ge(self.turned, half + 1)
            cols = slice(half * HALF, half * HALF + HALF)
            scale = 1.0 if self.weight is None else self.weight[:, k:k + 1]
            act.activation(self.c.xt_h[:, k, cols], self.c.psum[:, 2 * half + k, :], ACT.Copy,
                           scale=scale).then_inc(self.hi_ready, 1)

    def ready(self, eng, half):
        eng.wait_ge(self.lo_ready, KD * (half + 1))


class Core:

    def __init__(self, nc, ctx):
        self.nc, self.ctx = nc, ctx
        self.sem = lambda name: ctx.enter_context(nc.semaphore(name))
        sb = lambda name, shape, dt: ctx.enter_context(nc.sbuf_tensor(name, shape, dt))
        self.psum = ctx.enter_context(nc.psum_tensor("psum", [P, 8, 512], F32))
        self.x = sb("x", [P, NT, D], F32)
        self.xt_h = sb("xt_h", [P, KD, T], F32R)
        self.xt_l = sb("xt_l", [P, KD, T], F32R)
        self.ident = sb("ident", [P, P], F32)
        self.ident_bf = sb("ident_bf", [P, P], BF16)
        self.neg_half = sb("neg_half", [P, NT * 2], F32)
        self.early = sb("early", [P, 4, KD * FF], F32)

    def stage(self):
        ctx = ExitStack()
        sb = lambda name, shape, dt: ctx.enter_context(self.nc.sbuf_tensor(name, shape, dt))
        return ctx, sb

    def xt(self, k, cols):
        return self.xt_h[:, k, cols], self.xt_l[:, k, cols]


def windowed_attention(core, x_in, w_qkv_t, q_norm_w, k_norm_w, w_o_t, consts, ffn):
    nc, sem, psum = core.nc, core.sem, core.psum
    QK = 2 * D
    BANDS = 3 * P
    FH = P // HD0
    scope, sb = core.stage()
    with scope:
        norm = Norm(core, "ln0", sb, 1e-5)
        w_raw = sb("wqkv_raw", [P, KD, 3 * D], F32)
        w_h, w_l = (sb(f"wqkv_{n}", [P, KD, 3 * D], F32R) for n in "hl")
        wo_raw = sb("wo_raw", [P, KD, D], F32)
        wo_h, wo_l = (sb(f"wo_{n}", [P, KD, D], F32R) for n in "hl")
        cos_raw = sb("cos_raw", [P, 2, D], F32)
        sin_raw = sb("sin_raw", [P, 2, D], F32)
        norm_w = sb("norm_w", [P, 2, D], F32)
        cos_w = sb("cos_w", [P, 2, 2, D], F32)
        sin_w = sb("sin_w", [P, 2, 2, D], F32)
        head_rows = sb("head_rows", [P, FH], F32)
        mask = sb("mask", [P, BANDS], BF16)
        qk = sb("qk", [P, NT, QK], F32)
        scratch = sb("scratch", [P, D], F32)
        sumsq = sb("sumsq", [P, NT * 2], F32)
        msq = sb("msq", [P, NT * 2], F32)
        rqk = sb("rqk", [P, NT * 2], F32)
        part_a = sb("part_a", [P, 2, QK], F32)
        part_b = sb("part_b", [P, 2, QK], F32)
        v = sb("v", [P, 2, NT, D], F32)
        qk_t = sb("qk_t", [P, 2, KD, T], F32)
        qs = sb("qs", [P, NH0, S], F32)
        ks = sb("ks", [P, KD, S], F32)
        vs = sb("vs", [P, 2, 2, D], F32)
        neg_max = sb("neg_max", [P, 2, 2, 2], F32)
        sums = sb("sums", [P, 4, 2], F32)
        rden = sb("rden", [P, 4, 2], F32)
        prob = norm.y[:].rearrange("p t n -> p (t n)")[:, 0:4 * BANDS].rearrange("p (j n) -> p j n", j=4)
        pt = sb("pt", [P, 2, BANDS], F32)

        loaded_x = [sem(f"a_x_loaded_{h}") for h in range(2)]
        loaded_c = sem("a_constants_loaded")
        loaded_w = sem("a_weights_loaded")
        pool_own = sem("a_pool_written")
        w_ready = sem("a_weight_split")
        w_hi = sem("a_weight_high")
        qkv_done = sem("a_qkv_done")
        qk_out = sem("a_qk_copied")
        v_out = sem("a_v_copied")
        zeroed = sem("a_v_zeroed")
        msq_ready = sem("a_meansquare_ready")
        rqk_ready = sem("a_qk_rstd_ready")
        parts = sem("a_rope_parts")
        roped = sem("a_roped")
        qk_turned = sem("a_qk_turned")
        qkt_out = sem("a_qk_turned_copied")
        qk_staged = sem("a_qk_staged")
        v_staged = sem("a_v_staged")
        scored = sem("a_group_scored")
        max_ready = sem("a_max_ready")
        exp_done = sem("a_exp_done")
        p_turned = sem("a_probs_turned")
        p_out = sem("a_probs_copied")
        p_normed = sem("a_probs_normed")
        rden_ready = sem("a_denominators_inverted")
        pv_done = sem("a_pv_done")
        x_added = sem("a_x_added")
        o_hi = sem("a_attention_high")
        o_lo = sem("a_attention_low")
        proj_done = sem("a_projected")
        dve_own = sem("a_vector_written")

        QKB, VB, TURNB = (4, 5), (6, 7), (0, 1, 2, 3)
        SCORE, PTURN, PV = 0, (4, 5), (6, 7)

        def head_of(j):
            return j // FH * FH + (j % FH) // 4 + 2 * (j % 4)

        def items(b, first, last, more):
            for s in range(first, last):
                if s % 2 == 0 and (more or s + 2 < last):
                    yield "scores", b + (s + 2) // NH0, (s + 2) % NH0 // 2
                if more or s < FH:
                    at = b + (s + FH) // NH0, (s + FH) % NH0 // FH * 4
                    if 1 <= s % FH <= 4:
                        yield "stage_qk", at[0], at[1] + s % FH - 1
                    if s % FH == 4:
                        yield "stage_v", at[0], at[1] // 4
                if s % 2 == 0:
                    yield "softmax", b + s // NH0, s % NH0
                    yield "softmax", b + s // NH0, s % NH0 + 1
                    yield "divide", b + s // NH0, s % NH0
                    if more or s + 2 < last:
                        yield "peak", b + (s + 2) // NH0, (s + 2) % NH0 // 2
                    yield "divide", b + s // NH0, s % NH0 + 1
                if s >= 1:
                    yield "turn", b + (s - 1) // NH0, (s - 1) % NH0
                if s >= 2:
                    yield "values", b + (s - 2) // NH0, (s - 2) % NH0
                if s >= 2 and (s - 2) % FH == FH - 1:
                    yield "finish", b + (s - 2) // NH0, (s - 2) % NH0 // FH

        def run(eng, does):
            def all_of(work):
                for kind, b, n in work:
                    if kind in does:
                        does[kind](b, n)

            all_of([("scores", 0, 0), ("peak", 0, 0), *items(0, 0, 2, True)])
            with eng.Fori(0, B - 1) as b:
                all_of(items(b, 2, NH0 + 2, True))
            all_of(items(B - 1, 2, NH0, False))
            j = NH0 - 1
            all_of([("turn", B - 1, j), ("values", B - 1, j - 1), ("values", B - 1, j), ("finish", B - 1, 1)])

        with nc.Block() as block:
            @block.sync
            def _(sp):
                for t in range(NT):
                    sp.dma_start(core.x[:, t, :], x_in[t * P:(t + 1) * P, :]).then_inc(loaded_x[t // TH], 16)
                sp.dma_start(core.ident[:], consts["ident"]).then_inc(loaded_c, 16)
                sp.dma_start(cos_raw[:], consts["cos0"].rearrange("(t p) n -> p t n", p=P)).then_inc(loaded_c, 16)
                sp.dma_start(sin_raw[:], consts["sin0"].rearrange("(t p) n -> p t n", p=P)).then_inc(loaded_c, 16)
                for n, w in enumerate((q_norm_w, k_norm_w)):
                    sp.dma_start(norm_w[:, n, :], w.rearrange("(a n) -> a n", a=1).to_broadcast([P, D]))\
                        .then_inc(loaded_c, 16)
                sp.dma_start(head_rows[:], consts["head_rows"]).then_inc(loaded_c, 16)
                sp.dma_start(mask[:], consts["window_mask"]).then_inc(loaded_c, 16)
                sp.dma_start(core.ident_bf[:], consts["ident_bf"]).then_inc(loaded_c, 16)
                sp.wait_ge(loaded_w, 32)
                ffn.load(sp)

            @block.scalar
            def _(act):
                act.dma_start(w_raw[:], w_qkv_t.rearrange("(k p) n -> p k n", p=P)).then_inc(loaded_w, 16)
                act.dma_start(wo_raw[:], w_o_t.rearrange("(k p) n -> p k n", p=P)).then_inc(loaded_w, 16)
                act.wait_ge(loaded_w, 32)
                act.activation(w_h[:], w_raw[:], ACT.Copy).then_inc(w_hi, 1)
                act.activation(wo_h[:], wo_raw[:], ACT.Copy).then_inc(w_hi, 1)
                act.wait_ge(zeroed, 1)
                norm.scalar(act)
                for t in range(NT):
                    act.wait_ge(qkv_done, t + 1)
                    if t >= 1:
                        act.wait_ge(qk_out, 3 * t)
                    for n in range(2):
                        act.activation(scratch[:], psum[:, QKB[t % 2], n * D:(n + 1) * D], ACT.Square,
                                       accum_out=sumsq[:, 2 * t + n:2 * t + n + 1]).then_inc(qk_out, 1)
                        act.wait_ge(qk_out, 3 * t + n + 1)
                    act.activation(qk[:, t, :], psum[:, QKB[t % 2], :], ACT.Copy).then_inc(qk_out, 1)
                    for par in range(2):
                        to, src = (a.rearrange("p (h c r) -> p h c r", c=2, r=HD0)[:, :, par, :]
                                   for a in (v[:, par, t, :], psum[:, VB[t % 2], 0:D]))
                        act.activation(to, src, ACT.Copy).then_inc(v_out, 1)
                for t in range(NT):
                    act.wait_ge(qk_turned, t + 1)
                    act.activation(qk_t[:, :, :, t * P:(t + 1) * P],
                                   psum[:, TURNB[t % 4], :].rearrange("p (a k n) -> p a k n", a=2, k=KD),
                                   ACT.Copy).then_inc(qkt_out, 1)

                def softmax(b, j):
                    n, p = j // 2, j % 2
                    act.wait_ge(max_ready, NH0 // 2 * b + (n + 1))
                    for i, cols in enumerate((slice(0, P), slice(P, BANDS))):
                        bank = psum[:, SCORE + j % 4, i * S:i * S + (i + 1) * P]
                        act.activation(prob[:, j % 4, cols], bank, ACT.Exp, bias=neg_max[:, n % 2, i, p:p + 1],
                                       accum_out=sums[:, j % 4, i:i + 1]).then_inc(exp_done, 1)

                def turn(b, j):
                    act.wait_ge(p_turned, NH0 * b + (j + 1))
                    act.activation(pt[:, j % 2, :], psum[:, PTURN[j % 2], 0:BANDS], ACT.Copy).then_inc(p_out, 1)

                def finish(b, ft):
                    act.wait_ge(pv_done, 2 * b + (ft + 3))
                    act.activation(core.xt_h[:, ft, ds(b * S, S)], psum[:, PV[ft], 0:S], ACT.Copy).then_inc(o_hi, 1)

                run(act, dict(softmax=softmax, turn=turn, finish=finish))

            @block.gpsimd
            def _(pool):
                pool.memset(core.neg_half[:], -0.5).then_inc(pool_own, 1)
                pool.memset(v[:], 0.0).then_inc(zeroed, 1)
                pool.wait_ge(w_hi, 1)
                pool.tensor_tensor(w_l[:], w_raw[:], f(w_h[:]), ALU.subtract).then_inc(w_ready, 1)
                pool.wait_ge(pool_own, 1)
                norm.gpsimd(pool)
                pool.wait_ge(w_hi, 2)
                pool.tensor_tensor(wo_l[:], wo_raw[:], f(wo_h[:]), ALU.subtract).then_inc(w_ready, 1)

                def stage_qk(b, n):
                    ft, n = n // 4, n % 4
                    at = ft * FH + n * 2
                    if n == 0:
                        pool.wait_ge(scored, 8 * b + (4 * ft + 4))
                        pool.tensor_copy(ks[:, ft, :], qk_t[:, 1, ft, ds(b * S, S)]).then_inc(qk_staged, 1)
                    rows = head_rows[:, n * 2:n * 2 + 2].rearrange("p (h n) -> p h n", n=1)
                    pool.tensor_tensor(qs[:, at:at + 2, :], qk_t[:, 0, ft:ft + 1, ds(b * S, S)].to_broadcast([P, 2, S]),
                                       rows.to_broadcast([P, 2, S]), ALU.mult).then_inc(qk_staged, 1)

                def stage_v(b, ft):
                    cols = slice(ft * P, (ft + 1) * P)
                    pool.wait_ge(pv_done, 2 * b + (ft + 1))
                    pool.tensor_copy(vs[:, :, :, cols], v[:, :, ds(2 * b, 2), cols]).then_inc(v_staged, 1)

                pool.wait_ge(loaded_c, 16 * 8)
                for half in range(2):
                    cols = slice(half * NT, (half + 1) * NT)
                    pool.wait_ge(msq_ready, half + 1)
                    pool.tensor_tensor(rqk[:, cols], msq[:, cols], core.neg_half[:, 0:NT], ALU.pow)\
                        .then_inc(rqk_ready, 1)
                    for t in range(half * TH, half * TH + TH):
                        pool.wait_ge(parts, t + 1)
                        pool.tensor_tensor(qk[:, t, :], part_a[:, t % 2, :], part_b[:, t % 2, :], ALU.add)\
                            .then_inc(roped, 1)
                        if half == 1:
                            pool.wait_ge(qkt_out, 2)
                            stage_qk(0, t - TH)
                stage_v(0, 0)
                pool.wait_ge(qkt_out, NT)
                run(pool, dict(stage_qk=stage_qk, stage_v=stage_v))
                ffn.dequantize(pool)

            @block.vector
            def _(dve):
                own = Count(dve, dve_own)
                norm.vector(dve, core.x, [(loaded_x[h], 16 * TH) for h in range(2)])
                dve.wait_ge(loaded_c, 16 * 8)
                for t in range(2):
                    for n in range(2):
                        scale = HD0 ** -0.5 if n == 0 else 1.0
                        own.add(dve.scalar_tensor_tensor(cos_w[:, t, n, :], cos_raw[:, t, :], scale, norm_w[:, n, :],
                                                         ALU.mult, ALU.mult))
                        sw, sr, nw = (a.rearrange("p (h c r) -> p h c r", c=2, r=HD0 // 2)
                                      for a in (sin_w[:, t, n, :], sin_raw[:, t, :], norm_w[:, n, :]))
                        for c in range(2):
                            own.add(dve.scalar_tensor_tensor(sw[:, :, c, :], sr[:, :, c, :], scale, nw[:, :, 1 - c, :],
                                                             ALU.mult, ALU.mult))
                own.settle()

                def rope(t):
                    if t % TH == 0:
                        dve.wait_ge(rqk_ready, t // TH + 1)
                    if t >= 2:
                        dve.wait_ge(roped, t - 1)
                    for n in range(2):
                        src = qk[:, t, n * D:(n + 1) * D]
                        scale = rqk[:, 2 * t + n:2 * t + n + 1]
                        dve.scalar_tensor_tensor(part_a[:, t % 2, n * D:(n + 1) * D], src, scale,
                                                 cos_w[:, t % 2, n, :], ALU.mult, ALU.mult)
                        xs, sw, out = (a.rearrange("p (h c r) -> p h c r", c=2, r=HD0 // 2)
                                       for a in (src, sin_w[:, t % 2, n, :], part_b[:, t % 2, n * D:(n + 1) * D]))
                        for c in range(2):
                            ins = dve.scalar_tensor_tensor(out[:, :, c, :], xs[:, :, 1 - c, :], scale,
                                                           sw[:, :, c, :], ALU.mult, ALU.mult)
                    ins.then_inc(parts, 1)

                for t in range(NT + TH):
                    if t < NT:
                        if t % TH == TH - 1:
                            half = t // TH
                            cols = slice(half * NT, (half + 1) * NT)
                            dve.wait_ge(qk_out, 3 * (half + 1) * TH)
                            dve.tensor_scalar(msq[:, cols], sumsq[:, cols], 1.0 / D, 1e-6, ALU.mult,
                                              ALU.add).then_inc(msq_ready, 1)
                    if t >= TH:
                        rope(t - TH)
                def peak(b, n):
                    dve.wait_ge(scored, 8 * b + (8 + n + 1))
                    bank = SCORE + 2 * (n % 2)
                    for i in range(2):
                        ins = dve.tensor_reduce(neg_max[:, n % 2, i, :], psum[:, bank:bank + 2, i * S:i * S + (i + 1) * P],
                                                AX.X, ALU.max, negate=True)
                    ins.then_inc(max_ready, 1)

                def divide(b, j):
                    dve.wait_ge(exp_done, 2 * NH0 * b + (2 * j + 2))
                    dve.reciprocal(rden[:, j % 4, :], sums[:, j % 4, :]).then_inc(rden_ready, 1)
                    dve.wait_ge(rden_ready, NH0 * b + (j + 1))
                    for i, cols in enumerate((slice(0, P), slice(P, BANDS))):
                        at = prob[:, j % 4, cols]
                        ins = dve.tensor_scalar(at, at, rden[:, j % 4, i:i + 1], None, ALU.mult)
                    ins.then_inc(p_normed, 1)

                def finish(b, ft):
                    dve.wait_ge(o_hi, 2 * b + (ft + 1))
                    at = (slice(None), ft, ds(b * S, S))
                    dve.tensor_tensor(core.xt_l[at], psum[:, PV[ft], 0:S], f(core.xt_h[at]), ALU.subtract).then_inc(o_lo, 1)

                run(dve, dict(peak=peak, divide=divide, finish=finish))
                for t in range(NT):
                    dve.wait_ge(proj_done, t + 1)
                    dve.tensor_tensor(core.x[:, t, :], psum[:, t % 4, 0:D], core.x[:, t, :],
                                      ALU.add).then_inc(x_added, 1)

            @block.tensor
            def _(pe):
                pe.sem_inc(scored, 8)
                pe.sem_inc(pv_done, 2)
                pe.sem_inc(o_lo, 2)
                pe.wait_ge(loaded_c, 16 * 8)
                norm.tensor(pe)
                pe.wait_ge(w_ready, 1)
                for t in range(NT):
                    norm.ready(pe, t // TH)
                    if t >= 2:
                        pe.wait_ge(qk_out, 3 * (t - 1))
                        pe.wait_ge(v_out, 2 * t - 2)
                    cols = slice(t * P, (t + 1) * P)
                    for k in range(KD):
                        product(pe, psum[:, QKB[t % 2], :], core.xt(k, cols), (w_h[:, k, 0:QK], w_l[:, k, 0:QK]),
                                k == 0, k == KD - 1)
                    for k in range(KD):
                        ins = product(pe, psum[:, VB[t % 2], 0:D], core.xt(k, cols), (w_h[:, k, QK:], w_l[:, k, QK:]),
                                      k == 0, k == KD - 1)
                    ins.then_inc(qkv_done, 1)
                for t in range(NT):
                    pe.wait_ge(roped, t + 1)
                    if t >= 4:
                        pe.wait_ge(qkt_out, t - 3)
                    for n in range(4):
                        ins = pe.transpose(psum[:, TURNB[t % 4], n * P:(n + 1) * P], qk[:, t, n * P:(n + 1) * P],
                                           core.ident[:])
                    ins.then_inc(qk_turned, 1)
                pe.wait_ge(qkt_out, NT)
                pe.wait_ge(v_out, 2 * NT)

                def scores(b, n):
                    ft = n // 4
                    if n % 4 == 0:
                        pe.wait_ge(qk_staged, 10 * b + (5 * ft + 5))
                    if n >= 2 or not isinstance(b, int):
                        pe.wait_ge(exp_done, 2 * NH0 * b + (4 * n - 4))
                    for j in (2 * n, 2 * n + 1):
                        head = head_of(j)
                        for i in range(2):
                            bank = psum[:, SCORE + j % 4, i * S:i * S + (i + 1) * P]
                            pe.matmul(bank, qs[:, head, i * P:(i + 1) * P], ks[:, ft, 0:(i + 1) * P], start=True,
                                      stop=False, skip_group_check=True)
                            ins = pe.matmul(bank, core.ident_bf[:], mask[:, i * P:(2 * i + 1) * P], start=False,
                                            stop=True, skip_group_check=True)
                    ins.then_inc(scored, 1)

                def turn(b, j):
                    pe.wait_ge(p_normed, NH0 * b + (j + 1))
                    for i in range(3):
                        ins = pe.transpose(psum[:, PTURN[j % 2], i * P:(i + 1) * P], prob[:, j % 4, i * P:(i + 1) * P],
                                           core.ident[:])
                    ins.then_inc(p_turned, 1)

                def values(b, j):
                    head, ft, par, p = head_of(j), j // FH, j % FH // 4, j % 4
                    if j % FH == 0:
                        pe.wait_ge(v_staged, 2 * b + (ft + 1))
                        pe.wait_ge(o_lo, 2 * b + (ft + 1))
                    pe.wait_ge(p_out, NH0 * b + (j + 1))
                    rows = slice(32 * p, 32 * p + 32)
                    cols = slice(ft * P + 32 * p, ft * P + 32 * p + 32)
                    bank = psum[rows, PV[ft], :]
                    pe.matmul(bank[:, 0:S], vs[:, par, 0, cols], pt[:, j % 2, 0:S], start=par == 0, stop=False,
                              skip_group_check=True)
                    ins = pe.matmul(bank[:, P:S], vs[:, par, 1, cols], pt[:, j % 2, S:], start=False, stop=par == 1,
                                    skip_group_check=True)
                    if j % FH == FH - 1:
                        ins.then_inc(pv_done, 1)

                run(pe, dict(scores=scores, turn=turn, values=values))
                pe.wait_ge(w_ready, 2)
                for t in range(NT):
                    pe.wait_ge(o_lo, 2 * (t // 2) + 4)
                    if t >= 4:
                        pe.wait_ge(x_added, t - 3)
                    for k in range(KD):
                        ins = product(pe, psum[:, t % 4, 0:D], core.xt(k, slice(t * P, (t + 1) * P)),
                                      (wo_h[:, k, :], wo_l[:, k, :]), k == 0, k == KD - 1)
                    ins.then_inc(proj_done, 1)


class FfnWeights:
    BLOCK = 64

    def __init__(self, core, up_q_t, up_scale_t, down_q_t, down_scale_t):
        self.given = ((up_q_t, up_scale_t), (down_q_t, down_scale_t))
        self.up_q, self.up_s = (core.early[:, n, :].rearrange("p (k n) -> p k n", k=KD) for n in (0, 1))
        self.down_q, self.down_s = (core.early[:, n, :].rearrange("p (k n) -> p k n", k=KF) for n in (2, 3))
        self.loaded = core.sem("ffn_weights_loaded")
        self.less = core.sem("ffn_weights_centred")
        self.scaled = core.sem("ffn_weights_scaled")

    def load(self, sp):
        for (q_t, scale_t), q, s in zip(self.given, (self.up_q, self.down_q), (self.up_s, self.down_s)):
            sp.dma_start(q.bitcast(I32), q_t.rearrange("(k p) n -> p k n", p=P)).then_inc(self.loaded, 16)
            blocks = P // self.BLOCK
            for n in range(scale_t.shape[0]):
                k, h = n // blocks, n % blocks
                sp.dma_start(s[h * self.BLOCK:(h + 1) * self.BLOCK, k, :],
                             scale_t[n:n + 1, :].to_broadcast([self.BLOCK, s.shape[2]])).then_inc(self.loaded, 16)

    def dequantize(self, pool):
        pool.wait_ge(self.loaded, 16 * sum(1 + scale_t.shape[0] for _, scale_t in self.given))
        for n, (q, s) in enumerate(((self.up_q, self.up_s), (self.down_q, self.down_s))):
            pool.tensor_scalar(q, q.bitcast(I32), -7.5, None, ALU.add).then_inc(self.less, 1)
            pool.wait_ge(self.less, n + 1)
            pool.tensor_tensor(s, q, s, ALU.mult).then_inc(self.scaled, 1)


def quantized_ffn(core, ffn, b_up, up_lora_a_t, up_lora_b, b_down, down_lora_a_t, down_lora_b):
    nc, sem, psum = core.nc, core.sem, core.psum
    UPC = FF // 512
    scope, sb = core.stage()
    with scope:
        norm = Norm(core, "ln1", sb, 1e-5)
        up_s, down_s = ffn.up_s, ffn.down_s
        lora_ua = sb("lora_ua", [RANK, D], F32)
        lora_ub = sb("lora_ub", [RANK, FF], F32)
        lora_da = sb("lora_da", [RANK, FF], F32)
        lora_db = sb("lora_db", [RANK, D], F32)
        bias_up = sb("bias_up", [P, KF], F32)
        bias_down = sb("bias_down", [P, D], F32)
        up_h, up_l = (sb(f"up_{n}", [P, KD, FF], F32R) for n in "hl")
        down_h, down_l = (sb(f"down_{n}", [P, KF, D], F32R) for n in "hl")
        act_f = sb("act_f", [P, 4, HALF], F32)
        act_h, act_l = (sb(f"act_{n}", [P, KF, HALF], F32R) for n in "hl")

        loaded_l = sem("b_lora_loaded")
        loaded_b = sem("b_biases_loaded")
        lora_done = sem("b_lora_products")
        own_dve = sem("b_vector_written")
        weights = sem("b_weight_summed")
        w_hi = sem("b_weight_high")
        w_lo = sem("b_weight_low")
        up_done = sem("b_up_projected")
        relu_done = sem("b_relu_done")
        a_hi = sem("b_activation_high")
        a_lo = sem("b_activation_low")
        down_done = sem("b_down_projected")
        x_added = sem("b_x_added")
        UPB, DOWNB = (4, 5, 6, 7), (0, 1, 2, 3)

        with nc.Block() as block:
            @block.sync
            def _(sp):
                for to, given in ((lora_ua, up_lora_a_t), (lora_ub, up_lora_b), (lora_da, down_lora_a_t),
                                  (lora_db, down_lora_b)):
                    sp.dma_start(to[:], given).then_inc(loaded_l, 16)

            @block.scalar
            def _(act):
                for to, given in ((bias_down, b_down.rearrange("(a n) -> a n", a=1).to_broadcast([P, D])),
                                  (bias_up, b_up.rearrange("(k p) -> p k", p=P))):
                    with nc.allow_non_contiguous_dma(reason="a bias of 1024 numbers"):
                        act.dma_start(to[:], given).then_inc(loaded_b, 16)
                act.wait_ge(weights, 1)
                act.activation(up_h[:], up_s, ACT.Copy).then_inc(w_hi, 1)
                norm.scalar(act)
                act.wait_ge(weights, 2)
                act.activation(down_h[:], down_s, ACT.Copy).then_inc(w_hi, 1)
                act.wait_ge(loaded_b, 16 * 2)
                for n in range(2 * KF):
                    m = n % KF
                    act.wait_ge(up_done, n + 1)
                    if n >= 4:
                        act.wait_ge(a_lo, n - 3)
                    act.activation(act_f[:, n % 4, :], psum[:, UPB[n % 4], :], ACT.Relu,
                                   bias=bias_up[:, m:m + 1]).then_inc(relu_done, 1)

            @block.gpsimd
            def _(pool):
                norm.gpsimd(pool)
                pool.wait_ge(w_hi, 1)
                pool.tensor_tensor(up_l[:], up_s, f(up_h[:]), ALU.subtract).then_inc(w_lo, 1)
                pool.wait_ge(w_hi, 2)
                pool.tensor_tensor(down_l[:], down_s, f(down_h[:]), ALU.subtract).then_inc(w_lo, 1)
                for n in range(2 * KF):
                    pool.wait_ge(a_hi, n + 1)
                    pool.tensor_tensor(act_l[:, n % KF, :], act_f[:, n % 4, :], f(act_h[:, n % KF, :]),
                                       ALU.subtract).then_inc(a_lo, 1)

            @block.vector
            def _(dve):
                own = Count(dve, own_dve)
                def add_lora(n):
                    raw = (up_s.rearrange("p k (c n) -> p (k c) n", c=UPC), down_s.rearrange("p (g k) n -> p g (k n)", g=4))[n]
                    dve.wait_ge(ffn.scaled, n + 1)
                    dve.wait_ge(lora_done, n + 1)
                    dve.tensor_tensor(raw, psum[:, 4 * n:4 * n + 4, :], raw, ALU.add).then_inc(weights, 1)

                norm.vector(dve, core.x, meanwhile=lambda: add_lora(0))
                add_lora(1)
                dve.wait_ge(loaded_b, 16 * 2)
                for t in range(NT):
                    own.add(dve.tensor_tensor(core.x[:, t, :], core.x[:, t, :], bias_down[:], ALU.add))
                own.settle()

                def finish(t):
                    dve.wait_ge(down_done, t + 1)
                    dve.tensor_tensor(core.x[:, t, :], psum[:, DOWNB[t % 4], 0:D], core.x[:, t, :],
                                      ALU.add).then_inc(x_added, 1)

                for c in range(2):
                    for m in range(KF):
                        n = c * KF + m
                        dve.wait_ge(relu_done, n + 1)
                        dve.tensor_copy(act_h[:, m, :], act_f[:, n % 4, :]).then_inc(a_hi, 1)
                    for t in range(c * TH, (c + 1) * TH):
                        finish(t)

            @block.tensor
            def _(pe):
                pe.wait_ge(loaded_l, 16 * 4)
                for k in range(KD):
                    for c in range(UPC):
                        ins = pe.matmul(psum[:, k * UPC + c, :], lora_ua[:, k * P:(k + 1) * P],
                                        lora_ub[:, c * 512:(c + 1) * 512], start=True, stop=True)
                ins.then_inc(lora_done, 1)
                pe.wait_ge(weights, 1)
                norm.tensor(pe)
                for k in range(KF):
                    ins = pe.matmul(psum[:, 4 + k // 2, (k % 2) * D:(k % 2 + 1) * D], lora_da[:, k * P:(k + 1) * P],
                                    lora_db[:], start=True, stop=True)
                ins.then_inc(lora_done, 1)
                pe.wait_ge(weights, 2)
                pe.wait_ge(w_lo, 1)
                for c in range(2):
                    norm.ready(pe, c)
                    for m in range(KF):
                        n = c * KF + m
                        if n >= 4:
                            pe.wait_ge(relu_done, n - 3)
                        for k in range(KD):
                            cols = slice(m * P, (m + 1) * P)
                            ins = product(pe, psum[:, UPB[n % 4], :], (up_h[:, k, cols], up_l[:, k, cols]),
                                          core.xt(k, slice(c * HALF, (c + 1) * HALF)), k == 0, k == KD - 1)
                        ins.then_inc(up_done, 1)
                    if c == 0:
                        norm.ready(pe, 1)
                        pe.wait_ge(w_lo, 2)
                    for t in range(c * TH, (c + 1) * TH):
                        if t >= 4:
                            pe.wait_ge(x_added, t - 3)
                        cols = slice((t % TH) * P, (t % TH + 1) * P)
                        for m in range(KF):
                            if t % TH == 0:
                                pe.wait_ge(a_lo, c * KF + m + 1)
                            ins = product(pe, psum[:, DOWNB[t % 4], 0:D], (act_h[:, m, cols], act_l[:, m, cols]),
                                          (down_h[:, m, :], down_l[:, m, :]), m == 0, m == KF - 1)
                        ins.then_inc(down_done, 1)


def selective_scan(core, w_xproj_t, b_xproj, w_dt_t, b_dt, a_log, consts, attention):
    nc, sem, psum = core.nc, core.sem, core.psum
    NBC = 2 * NS
    SETS = KD * NS
    scope, sb = core.stage()
    with scope:
        norm_f = sb("xn_f", [P, KD, T], F32)
        norm = Norm(core, "ln2", sb, 1e-5, plain=norm_f)
        wx_raw = sb("wx_raw", [P, KD, DR + NBC], F32)
        wx3 = sb("wx3", [P, KD, 3 * NBC], F32)
        wx_h, wx_l = (sb(f"wx_{n}", [P, KD, DR], F32R) for n in "hl")
        wdt_raw = sb("wdt_raw", [P, D], F32)
        wdt_h, wdt_l = (sb(f"wdt_{n}", [P, D], F32R) for n in "hl")
        bias_r = sb("bias_r", [P, 1], F32)
        bias_bc = sb("bias_bc", [3 * NBC, 1], F32)
        bias_dt = sb("bias_dt", [P, KD], F32)
        a_raw = sb("a_raw", [P, KD, NS], F32)
        a_neg = sb("a_neg", [P, KD, NS], F32)
        one_hot = sb("one_hot", [3 * NBC, NBC, P], BF16)
        dtr_f = sb("dtr_f", [P, T], F32)
        dtr_h, dtr_l = (sb(f"dtr_{n}", [P, T], F32R) for n in "hl")
        bc_f = sb("bc_f", [3 * NBC, T], F32)
        bc_2 = sb("bc_2", [3 * NBC, T], BF16)
        bc_parts = sb("bc_parts", [3 * NBC, T], BF16)
        dt = sb("dt", [P, KD, T], F32)
        t1 = sb("t1", [P, KD, T], F32)
        t2 = sb("t2", [P, KD, T], F32)
        u = sb("u", [P, KD, T], F32)
        decay = sb("decay", [P, 2, B, S], F32)
        b_all = sb("b_all", [P, 2, T], F32)
        drive = sb("drive", [P, 2, T], F32)
        h = sb("h", [P, 2, T], F32)
        prod = sb("prod", [P, 2, T], F32)
        y = norm_f
        zero_bf = sb("zero_bf", [P, 512], BF16)

        loaded = sem("c_loaded")
        pool_own = sem("c_pool_written")
        w_ready = sem("c_weights_ready")
        r_done = sem("c_dt_rank_projected")
        bc_done = sem("c_bc_projected")
        r_out = sem("c_dt_rank_out")
        r_hi = sem("c_dt_rank_high")
        r_lo = sem("c_dt_rank_low")
        bc_out = sem("c_bc_out")
        split = sem("c_bc_split")
        dt_done = sem("c_dt_projected")
        soft = sem("c_softplus_steps")
        own_dve = sem("c_vector_written")
        bc_ready = sem("c_bc_ready")
        dt_ready = sem("c_dt_ready")
        a_ready = sem("c_a_ready")
        b_spread = sem("c_b_spread")
        c_spread = sem("c_c_spread")
        b_copied = sem("c_b_copied")
        decay_ready = sem("c_decay_ready")
        driven = sem("c_drive_ready")
        scanned = sem("c_scanned")
        weighed = sem("c_weighed")
        summed = sem("c_summed")
        y_out = sem("c_y_out")
        y_turned = sem("c_y_turned")
        RB, BCB, DTB = (4, 5), (6, 7), (0, 1, 2, 3)
        BB, CB, YB = 0, (2, 4), 6

        with nc.Block() as block:
            @block.sync
            def _(sp):
                with nc.allow_non_contiguous_dma(reason="biases"):
                    for to, given in (
                            (wx_raw[:], w_xproj_t.rearrange("(k p) n -> p k n", p=P)),
                            (wdt_raw[:], w_dt_t),
                            (bias_r[:], b_xproj[0:DR].rearrange("(p a) -> p a", a=1)),
                            *((bias_bc[i * NBC:(i + 1) * NBC, :], b_xproj[DR:DR + NBC].rearrange("(p a) -> p a", a=1))
                              for i in range(3)),
                            (bias_dt[:], b_dt.rearrange("(k p) -> p k", p=P)),
                            (a_raw[:], a_log.rearrange("(k p) n -> p k n", p=P)),
                            (one_hot[:], consts["one_hot"])):
                        sp.dma_start(to, given).then_inc(loaded, 16)
                attention.load(sp, 0)

            @block.gpsimd
            def _(pool):
                norm.gpsimd(pool)
                own = Count(pool, pool_own)
                own.add(pool.memset(decay[:], 0.0))
                own.add(pool.memset(zero_bf[:], 0.0))
                pool.wait_ge(loaded, 16 * 9)
                own.add(pool.tensor_copy(wx_h[:], wx_raw[:, :, 0:DR]))
                own.add(pool.tensor_copy(wdt_h[:], wdt_raw[:]))
                for i in range(3):
                    own.add(pool.tensor_copy(wx3[:, :, i * NBC:(i + 1) * NBC], wx_raw[:, :, DR:]))
                own.settle()
                own.add(pool.tensor_tensor(wx_l[:], wx_raw[:, :, 0:DR], f(wx_h[:]), ALU.subtract))
                pool.tensor_tensor(wdt_l[:], wdt_raw[:], f(wdt_h[:]), ALU.subtract).then_inc(w_ready, 1)
                for half in range(2):
                    for k in range(KD):
                        cols = slice(half * HALF, (half + 1) * HALF)
                        pool.wait_ge(norm.lo_ready, 2 * half + k + 1)
                        pool.tensor_tensor(core.xt_l[:, k, cols], norm_f[:, k, cols], f(core.xt_h[:, k, cols]),
                                           ALU.subtract).then_inc(split, 1)
                for c in range(2):
                    pool.wait_ge(r_hi, c + 1)
                    cols = slice(c * HALF, (c + 1) * HALF)
                    pool.tensor_tensor(dtr_l[:, cols], dtr_f[:, cols], f(dtr_h[:, cols]), ALU.subtract).then_inc(r_lo, 1)
                for k in range(KD):
                    pool.wait_ge(dt_ready, k + 1)
                    with pool.Fori(0, NS // 2) as i:
                        for j in range(2):
                            at = 2 * i + (k * NS + j)
                            pool.wait_ge(b_copied, at + 2)
                            pool.wait_ge(scanned, at + 1)
                            pool.tensor_tensor(drive[:, j, :], u[:, k, :], b_all[:, j, :], ALU.mult)\
                                .then_inc(driven, 1)

            @block.scalar
            def _(act):
                norm.scalar(act)
                act.wait_ge(loaded, 16 * 9)
                for c in range(2):
                    act.wait_ge(r_done, c + 1)
                    act.activation(dtr_f[:, c * HALF:(c + 1) * HALF], psum[:, RB[c], :], ACT.Identity,
                                   bias=bias_r[:]).then_inc(r_out, 1)
                for c in range(2):
                    act.wait_ge(bc_done, c + 1)
                    act.activation(bc_f[:, c * HALF:(c + 1) * HALF], psum[0:3 * NBC, BCB[c], :], ACT.Identity,
                                   bias=bias_bc[:]).then_inc(bc_out, 1)
                for k in range(KD):
                    act.wait_ge(dt_done, k + 1)
                    z = psum[:, 2 * k:2 * k + 2, :]
                    act.activation(t1[:, k, :].rearrange("p (c n) -> p c n", c=2), z, ACT.Abs,
                                   bias=bias_dt[:, k:k + 1]).then_inc(soft, 1)
                for k in range(KD):
                    act.wait_ge(soft, k + 1)
                    act.activation(t1[:, k, :], t1[:, k, :], ACT.Exp, scale=-1.0).then_inc(soft, 1)
                act.activation(a_neg[:], a_raw[:], ACT.Exp).then_inc(a_ready, 1)
                for k in range(KD):
                    act.wait_ge(soft, KD + k + 1)
                    act.activation(t2[:, k, :], t1[:, k, :], ACT.Ln, bias=1.0).then_inc(soft, 1)
                act.wait_ge(a_ready, 2)
                act.wait_ge(pool_own, 1)

                def pair(k, i):
                    for j in range(2):
                        at = 2 * i + (k * NS + j)
                        act.wait_ge(b_spread, at + 1)
                        act.wait_ge(driven, at + 1)
                        act.activation(b_all[:, j, :].rearrange("p (c n) -> p c n", c=2), psum[:, BB:BB + 2, :],
                                       ACT.Copy).then_inc(b_copied, 1)
                        act.wait_ge(scanned, at + 1)
                        src = dt[:, k, :].rearrange("p (b s) -> p b s", b=B)
                        act.activation(decay[:, j, :, 1:S], src[:, :, 1:S], ACT.Exp,
                                       scale=a_neg[:, k, ds(2 * i + j, 1)]).then_inc(decay_ready, 1)

                def copy_y(k):
                    act.wait_ge(summed, (k + 1) * NS + 2)
                    act.activation(y[:, k, :].rearrange("p (c n) -> p c n", c=2), psum[:, YB:YB + 2, :],
                                   ACT.Copy).then_inc(y_out, 1)

                for k in range(KD):
                    act.wait_ge(dt_ready, k + 1)
                    pair(k, 0)
                    if k >= 1:
                        copy_y(k - 1)
                    with act.Fori(1, NS // 2) as i:
                        pair(k, i)
                copy_y(KD - 1)

            @block.vector
            def _(dve):
                norm.vector(dve, core.x)
                own = Count(dve, own_dve)
                for c in range(2):
                    cols = slice(c * HALF, (c + 1) * HALF)
                    dve.wait_ge(r_out, c + 1)
                    dve.tensor_copy(dtr_h[:, cols], dtr_f[:, cols]).then_inc(r_hi, 1)
                dve.wait_ge(bc_out, 2)
                own.add(dve.tensor_copy(bc_parts[:], bc_f[:]))
                own.settle()
                own.add(dve.tensor_tensor(bc_f[:], bc_f[:], bc_parts[:], ALU.subtract))
                own.settle()
                own.add(dve.tensor_copy(bc_2[:], bc_f[:]))
                own.settle()
                own.add(dve.tensor_copy(bc_parts[NBC:2 * NBC, :], bc_2[NBC:2 * NBC, :]))
                dve.tensor_tensor(bc_parts[2 * NBC:3 * NBC, :], bc_f[2 * NBC:3 * NBC, :], bc_2[2 * NBC:3 * NBC, :],
                                  ALU.subtract).then_inc(bc_ready, 1)
                dve.wait_ge(a_ready, 1)
                dve.tensor_scalar(a_neg[:], a_neg[:], -1.0, None, ALU.mult).then_inc(a_ready, 1)
                dve.wait_ge(soft, 2 * KD)
                for k in range(KD):
                    own.add(dve.tensor_scalar(dt[:, k, :], t1[:, k, :], 1.0, 1.0, ALU.add, ALU.subtract))
                own.settle()
                own.add(dve.tensor_tensor(u[:], t1[:], dt[:], ALU.subtract))
                own.settle()
                for k in range(KD):
                    own.add(dve.tensor_scalar(dt[:, k, :].rearrange("p (c n) -> p c n", c=2), psum[:, 2 * k:2 * k + 2, :],
                                              bias_dt[:, k:k + 1], 0.0, ALU.add, ALU.max))
                own.settle()
                own.add(dve.tensor_tensor(u[:], u[:], dt[:], ALU.add))
                own.settle()
                for k in range(KD):
                    dve.wait_ge(soft, 2 * KD + k + 1)
                    own.add(dve.tensor_tensor(dt[:, k, :], t2[:, k, :], u[:, k, :], ALU.add))
                    own.settle()
                    dve.tensor_tensor(u[:, k, :], dt[:, k, :], norm_f[:, k, :], ALU.mult).then_inc(dt_ready, 1)

                def weigh(k, i, j):
                    at = 2 * i + (k * NS + j)
                    dve.wait_ge(scanned, at + 3)
                    dve.wait_ge(c_spread, at + 1)
                    dve.wait_ge(summed, at + 1)
                    dve.tensor_tensor(prod[:, j, :].rearrange("p (c n) -> p c n", c=2), psum[:, CB[j]:CB[j] + 2, :],
                                      h[:, j, :].rearrange("p (c n) -> p c n", c=2), ALU.mult).then_inc(weighed, 1)

                def scan(k, i, j):
                    at = 2 * i + (k * NS + j)
                    dve.wait_ge(decay_ready, at + 1)
                    dve.wait_ge(driven, at + 3)
                    dve.wait_ge(weighed, at + 1)
                    dve.tensor_tensor_scan(h[:, j, :], decay[:, j, :, :].rearrange("p b s -> p (b s)"), drive[:, j, :],
                                           0.0, ALU.mult, ALU.add).then_inc(scanned, 1)

                for k in range(KD):
                    scan(k, 0, 0)
                    with dve.Fori(0, NS // 2 - 1) as i:
                        scan(k, i, 1)
                        weigh(k, i, 0)
                        scan(k, i + 1, 0)
                        weigh(k, i, 1)
                    scan(k, NS // 2 - 1, 1)
                    weigh(k, NS // 2 - 1, 0)
                    weigh(k, NS // 2 - 1, 1)
                for t in range(NT):
                    dve.wait_ge(y_turned, t // 2 + 1)
                    src = psum[:, t // 2, (t % 2) * D:(t % 2 + 1) * D]
                    own.add(dve.tensor_tensor(core.x[:, t, :], src, core.x[:, t, :], ALU.add))
                own.settle()

            @block.tensor
            def _(pe):
                norm.tensor(pe)
                pe.wait_ge(w_ready, 1)
                for c in range(2):
                    pe.wait_ge(split, KD * (c + 1))
                    cols = slice(c * HALF, (c + 1) * HALF)
                    for k in range(KD):
                        ins = product(pe, psum[:, RB[c], :], (wx_h[:, k, :], wx_l[:, k, :]), core.xt(k, cols),
                                      k == 0, k == KD - 1)
                    ins.then_inc(r_done, 1)
                for c in range(2):
                    for k in range(KD):
                        ins = pe.matmul(psum[0:3 * NBC, BCB[c], :], wx3[:, k, :], norm_f[:, k, c * HALF:(c + 1) * HALF],
                                        start=k == 0, stop=k == KD - 1)
                    ins.then_inc(bc_done, 1)
                pe.wait_ge(r_lo, 2)
                for k in range(KD):
                    for c in range(2):
                        cols = slice(c * HALF, (c + 1) * HALF)
                        ins = product(pe, psum[:, DTB[2 * k + c], :], (wdt_h[:, k * P:(k + 1) * P], wdt_l[:, k * P:(k + 1) * P]),
                                      (dtr_h[:, cols], dtr_l[:, cols]))
                    ins.then_inc(dt_done, 1)
                pe.sem_inc(scanned, 2)
                pe.sem_inc(driven, 2)
                pe.sem_inc(summed, 2)
                pe.sem_inc(weighed, 2)
                pe.sem_inc(b_copied, 1)
                pe.wait_ge(bc_ready, 1)
                pe.wait_ge(dt_ready, 1)
                pe.wait_ge(pool_own, 2)

                def spread(row, bank):
                    for c in range(2):
                        ins = pe.matmul(psum[:, bank + c, :], one_hot[:, row, :], bc_parts[:, c * HALF:(c + 1) * HALF],
                                        start=True, stop=True)
                    return ins

                def spread_b(k, n):
                    pe.wait_ge(b_copied, n + (k * NS + 1))
                    spread(n, BB).then_inc(b_spread, 1)

                def spread_c(k, n, j):
                    pe.wait_ge(weighed, n + (k * NS + 1))
                    spread(n + NS, CB[j]).then_inc(c_spread, 1)

                def add(k, n, j):
                    pe.wait_ge(weighed, n + (k * NS + 3))
                    for c in range(2):
                        ins = pe.matmul(psum[:, YB + c, :], core.ident[:], prod[:, j, c * HALF:(c + 1) * HALF],
                                        start=False, stop=False, skip_group_check=True)
                    ins.then_inc(summed, 1)

                LEAD_B, LEAD_C = 4, 2
                for n in range(LEAD_C):
                    spread_b(0, n)
                    spread_c(0, n, n)
                for n in range(LEAD_C, LEAD_B):
                    spread_b(0, n)
                for k in range(KD):
                    if k >= 1:
                        pe.wait_ge(y_out, k)
                    for c in range(2):
                        pe.matmul(psum[:, YB + c, :], core.ident_bf[:], zero_bf[:], start=True, stop=False,
                                  skip_group_check=True)
                    with pe.Fori(0, (NS - LEAD_B) // 2) as i:
                        for j in range(2):
                            spread_b(k, 2 * i + (j + LEAD_B))
                            spread_c(k, 2 * i + (j + LEAD_C), j)
                            add(k, 2 * i + j, j)
                    for n in range(NS - LEAD_B, NS):
                        later, m = divmod(n + LEAD_C, NS)
                        if k + later < KD:
                            spread_c(k + later, m, n % 2)
                        add(k, n, n % 2)
                        if k + 1 < KD:
                            spread_b(k + 1, n - (NS - LEAD_B))
                pe.wait_ge(y_out, KD)
                for t in range(NT):
                    for k in range(KD):
                        ins = pe.transpose(psum[:, t // 2, (t % 2) * D + k * P:(t % 2) * D + (k + 1) * P],
                                           y[:, k, t * P:(t + 1) * P], core.ident[:])
                    if t % 2 == 1:
                        ins.then_inc(y_turned, 1)


class AttentionWeights:

    def __init__(self, core, wq, wk, wv, wo):
        self.given = wq, wk, wv, wo
        part = lambda n, k: core.early[:, n, :].rearrange("p (k n) -> p k n", k=k)
        self.wq, self.wo, self.wkv = part(0, KD), part(1, REP1), core.early[:, 2, 0:2 * KD * HD1]\
            .rearrange("p (k n) -> p k n", k=KD)
        self.loaded = core.sem("attention_weights_loaded")

    def load(self, sp, g):
        wq, wk, wv, wo = self.given
        for to, src in ((self.wkv[:, :, 0:HD1], wk.rearrange("(k p) n -> p k n", p=P)[:, :, ds(g * HD1, HD1)]),
                        (self.wkv[:, :, HD1:], wv.rearrange("(k p) n -> p k n", p=P)[:, :, ds(g * HD1, HD1)]),
                        (self.wq, wq.rearrange("(k p) n -> p k n", p=P)[:, :, ds(g * REP1 * HD1, REP1 * HD1)]),
                        (self.wo, wo.rearrange("(h p) n -> p h n", p=P)[:, ds(g * REP1, REP1), :])):
            sp.dma_start(to, src).then_inc(self.loaded, 16)


def causal_attention(core, z, ln1_w, weights_in, consts):
    nc, sem, psum = core.nc, core.sem, core.psum
    STEPS, BANDS, QB = B * REP1, 3 * P, 4
    QC = QB * HD1
    scope, sb = core.stage()
    with scope:
        ln_w = sb("ln1_w", [P, KD], F32)
        norm = Norm(core, "ln3", sb, 1e-5, weight=ln_w, twice=1e-5, z=z)
        wq_raw, wkv_raw, wo_raw = weights_in.wq, weights_in.wkv, weights_in.wo
        wq_h, wq_l = (sb(f"wq_{n}", [P, 2 * KD, REP1 * HD1], F32R) for n in "hl")
        wkv_h, wkv_l = (sb(f"wkv_{n}", [P, 2 * KD, 2 * HD1], F32R) for n in "hl")
        wo_h, wo_l = (sb(f"wo1_{n}", [P, 2 * REP1, D], F32R) for n in "hl")
        tables = sb("rope1", [P, 2, 2, 2, HD1], F32)
        mask = sb("causal", [P, P], F32)
        part_a = sb("r_part_a", [P, 2, QC], F32)
        part_b = sb("r_part_b", [P, 2, QC], F32)
        qr = sb("qr", [P, 2, QC], F32)
        kr = sb("kr", [P, 2, HD1], F32)
        q_0 = sb("q1_0", [P, 2, QB, P], F32)
        q_h, q_l = (sb(f"q1_{n}", [P, 2, QB, P], F32R) for n in "hl")
        k_0 = sb("k1_0", [P, 2, P], F32)
        k_h, k_l = (sb(f"k1_{n}", [P, 2, S], F32R) for n in "hl")
        v_h, v_l = (sb(f"v1_{n}", [P, 2, HD1], F32R) for n in "hl")
        v_1 = sb("v1_1", [P, 2, HD1], F32)
        neg_max = sb("neg_max1", [P, 2, 2], F32)
        sums = sb("sums1", [P, 2, 2], F32)
        rden = sb("rden1", [P, 2, 2], F32)
        prob = sb("prob1", [P, 2, BANDS], F32)
        pt_h, pt_l = (sb(f"pt1_{n}", [P, 2, S], F32R) for n in "hl")
        pt_1 = sb("pt1_1", [P, 2, P], F32)
        ot_h, ot_l = (sb(f"ot1_{n}", [P, 2, S], F32R) for n in "hl")

        loaded_c = sem("d_constants_loaded")
        loaded_w = weights_in.loaded
        tables_own = sem("d_tables_written")
        w_hi = sem("d_weights_high")
        w_ready = sem("d_weights_split")
        projected = sem("d_projected")
        parts = sem("d_rope_parts")
        roped = sem("d_roped")
        v_hi = sem("d_v_high")
        qk_turned = sem("d_qk_turned")
        qk_hi = sem("d_qk_high")
        qk_lo = sem("d_qk_low")
        scored = sem("d_scored")
        masked = sem("d_masked")
        max_ready = sem("d_max_ready")
        exp_done = sem("d_exp_done")
        rden_ready = sem("d_denominator_inverted")
        p_normed = sem("d_probs_normed")
        first_out = sem("d_plain_copied")
        p_turned = sem("d_probs_turned")
        p_hi = sem("d_probs_high")
        p_lo = sem("d_probs_low")
        pv_done = sem("d_pv_done")
        o_hi = sem("d_output_high")
        o_lo = sem("d_output_low")
        wo_done = sem("d_projected_out")
        z_added = sem("d_z_added")
        PROJB, TURNB, SCOREB, PTURNB, PVB, WOB = (0, 1), 2, (3, 4), 5, 6, 7

        def q_index(g, m, i):
            return 20 * g + (5 * (m // 2) + 1 + i if m % 2 == 0 else 5 * (m // 2) + 3 + i)

        def kv_index(g, b):
            return 20 * g + 5 * b

        def turn_index(g, m, c):
            return 20 * g + 5 * (m // 2) + ((1, 2), (3, 4))[m % 2][c]

        def k_turn_index(g, b):
            return 20 * g + 5 * b

        def known(value, limit):
            return isinstance(value, int) and value < limit

        def ahead(g, m):
            return (g, m) if m < 2 * B else (g + 1, m - 2 * B)

        def ahead_b(g, b):
            return (g, b) if b < B else (g + 1, b - B)

        PIECE = 512
        PIECES = KD * 2 + 1 + REP1 // 2

        def weight_piece(n):
            if n < 2 * KD:
                return wq_h, wq_l, wq_raw, n // 2, 1, slice(n % 2 * PIECE, (n % 2 + 1) * PIECE)
            if n == 2 * KD:
                return wkv_h, wkv_l, wkv_raw, 0, KD, slice(0, 2 * HD1)
            return wo_h, wo_l, wo_raw, 2 * (n - 2 * KD - 1), 2, slice(0, D)

        def schedule(g, first, end, last):
            for n in range(first, end):
                at = lambda k: (g + (n + k) // STEPS, (n + k) % STEPS)
                own = not last or n < STEPS
                (gg, s), more = at(0), own and (not last or n // REP1 + 1 < B)
                b, r = s // REP1, s % REP1
                if own and (not last or n + 1 < STEPS):
                    yield "scores", *at(1)
                if own:
                    yield "softmax", *at(0)
                if own and (not last or n + 1 < STEPS):
                    yield "peak", *at(1)
                if n >= 1 and (not last or n < STEPS + 1):
                    yield "turn_probs", *at(-1)
                if own and r in (1, 2):
                    yield "turn_q", gg, 2 * b + 1, r - 1
                if more and r == 4:
                    yield "turn_k", *ahead_b(gg, b + 1)
                if more and r in (5, 6):
                    yield "turn_q", *ahead(gg, 2 * b + 2), r - 5
                if n >= 2 and (not last or n < STEPS + 2):
                    yield "values", *at(-2)
                if n >= 3:
                    yield "project_out", *at(-3)
                if more and r == 1:
                    yield "kv", *ahead_b(gg, b + 1)
                if more and r in (2, 3):
                    yield "q", *ahead(gg, 2 * b + 2), r - 2
                if more and r in (6, 7):
                    yield "q", *ahead(gg, 2 * b + 3), r - 6
                if not last and 6 <= s < 6 + 2 * PIECES and s % 2 == 0:
                    yield "weights", gg + 1, (s - 6) // 2

        FIRST = [("kv", 0, 0), ("q", 0, 0, 0), ("q", 0, 0, 1), ("turn_k", 0, 0), ("turn_q", 0, 0, 0),
                 ("turn_q", 0, 0, 1), ("q", 0, 1, 0), ("q", 0, 1, 1), ("scores", 0, 0), ("peak", 0, 0)]

        def run(eng, does):
            def all_of(work):
                for kind, *what in work:
                    if kind in does:
                        does[kind](*what)

            all_of([*FIRST, *schedule(0, 0, 3, False)])
            with eng.Fori(0, KVH1 - 1) as g:
                all_of(schedule(g, 3, STEPS + 3, False))
            all_of(schedule(KVH1 - 1, 3, STEPS + 3, True))

        with nc.Block() as block:
            @block.sync
            def _(sp):
                with nc.allow_non_contiguous_dma(reason="a norm's weights"):
                    sp.dma_start(ln_w[:], ln1_w.rearrange("(k p) -> p k", p=P)).then_inc(loaded_c, 16)
                for n, name in enumerate(("cos1", "sin1")):
                    sp.dma_start(tables[:, 1, n, :, :], consts[name].rearrange("(t p) n -> p t n", p=P))\
                        .then_inc(loaded_c, 16)
                sp.dma_start(mask[:], consts["causal_mask"]).then_inc(loaded_c, 16)

                with sp.Fori(1, KVH1) as g:
                    sp.wait_ge(w_ready, 2 * g)
                    weights_in.load(sp, g)

            @block.scalar
            def _(act):
                def weights(g, piece):
                    hi, _, raw, row, rows, cols = weight_piece(piece)
                    if piece == 0:
                        act.wait_ge(loaded_w, 64 * g + 64)
                    act.activation(hi[:, ds((g & 1) * raw.shape[1] + row, rows), cols], raw[:, row:row + rows, cols],
                                   ACT.Copy).then_inc(w_hi, 1)

                for piece in range(PIECES):
                    weights(0, piece)
                act.wait_ge(loaded_c, 16 * 4)
                norm.scalar(act)

                def turn_q(g, m, c):
                    act.wait_ge(qk_turned, turn_index(g, m, c) + 1)
                    bank = psum[:, TURNB, :].rearrange("p (h t n) -> p h t n", h=2, t=2)
                    act.activation(q_0[:, m % 2, 2 * c:2 * c + 2, :], bank[:, :, 0, :], ACT.Copy).then_inc(first_out, 1)
                    act.activation(q_h[:, m % 2, 2 * c:2 * c + 2, :], bank[:, :, 1, :], ACT.Copy).then_inc(qk_hi, 1)

                def turn_k(g, b):
                    act.wait_ge(qk_turned, k_turn_index(g, b) + 1)
                    act.activation(k_0[:, b % 2, :], psum[:, TURNB, 0:P], ACT.Copy).then_inc(first_out, 1)
                    act.activation(k_h[:, b % 2, :], psum[:, TURNB, 0:S], ACT.Copy).then_inc(qk_hi, 1)

                def kv(g, b):
                    act.wait_ge(projected, kv_index(g, b) + 1)
                    bank = psum[:, PROJB[0], :].rearrange("p (t n) -> p t n", t=2)
                    act.activation(v_1[:, b % 2, :], bank[:, 1, HD1:], ACT.Copy).then_inc(first_out, 1)
                    act.activation(v_h[:, b % 2, :], bank[:, 0, HD1:], ACT.Copy).then_inc(v_hi, 1)

                def softmax(g, s):
                    act.wait_ge(max_ready, STEPS * g + (s + 1))
                    for i, cols in enumerate((slice(0, P), slice(P, BANDS))):
                        act.activation(prob[:, s % 2, cols], psum[:, SCOREB[s % 2], cols], ACT.Exp,
                                       bias=neg_max[:, s % 2, i:i + 1],
                                       accum_out=sums[:, s % 2, i:i + 1]).then_inc(exp_done, 1)

                def turn_probs(g, s):
                    act.wait_ge(p_turned, STEPS * g + (s + 1))
                    act.activation(pt_1[:, s % 2, :], psum[:, PTURNB, S:BANDS], ACT.Copy).then_inc(first_out, 1)
                    act.activation(pt_h[:, s % 2, :], psum[:, PTURNB, 0:S], ACT.Copy).then_inc(p_hi, 1)

                def values(g, s):
                    act.wait_ge(pv_done, STEPS * g + (s + 1))
                    act.activation(ot_h[:, s % 2, :], psum[:, PVB, 0:S], ACT.Copy).then_inc(o_hi, 1)

                run(act, dict(turn_q=turn_q, turn_k=turn_k, kv=kv, softmax=softmax, turn_probs=turn_probs, values=values,
                              weights=weights))

            @block.gpsimd
            def _(pool):
                def weights(g, piece):
                    hi, lo, raw, row, rows, cols = weight_piece(piece)
                    where = ds((g & 1) * raw.shape[1] + row, rows)
                    src = raw[:, row:row + rows, cols]
                    pool.wait_ge(w_hi, PIECES * g + (piece + 1))
                    ins = pool.tensor_tensor(lo[:, where, cols], src, f(hi[:, where, cols]), ALU.subtract)
                    if piece in (2 * KD, PIECES - 1):
                        ins.then_inc(w_ready, 1)

                for piece in range(2):
                    weights(0, piece)
                norm.gpsimd(pool)
                for piece in range(2, PIECES):
                    weights(0, piece)

                def q(g, m, i):
                    pool.wait_ge(parts, q_index(g, m, i) + 1)
                    before = turn_index(g, m - 1, 1) if m else k_turn_index(g, 0) - 1
                    if not known(before, 0):
                        pool.wait_ge(qk_turned, before + 1)
                    slot = q_index(0, m, i) % 2
                    pool.tensor_tensor(qr[:, i, :], part_a[:, slot, :], part_b[:, slot, :], ALU.add).then_inc(roped, 1)

                def kv(g, b):
                    index = kv_index(g, b)
                    pool.wait_ge(parts, index + 1)
                    slot = kv_index(0, b) % 2
                    cols = slice(0, 2 * HD1)
                    pool.tensor_tensor(kr[:].rearrange("p t n -> p (t n)"), part_a[:, slot, cols], part_b[:, slot, cols],
                                       ALU.add).then_inc(roped, 1)

                def softmax(g, s):
                    pool.wait_ge(rden_ready, STEPS * g + (s + 1))
                    for i, cols in enumerate((slice(0, P), slice(P, BANDS))):
                        at = prob[:, s % 2, cols]
                        ins = pool.tensor_tensor(at, at, rden[:, s % 2, i:i + 1].to_broadcast([P, (i + 1) * P]), ALU.mult)
                    ins.then_inc(p_normed, 1)

                run(pool, dict(q=q, kv=kv, softmax=softmax, weights=weights))

            @block.vector
            def _(dve):
                norm.vector(dve, core.x)
                dve.wait_ge(loaded_c, 16 * 4)
                dve.tensor_scalar(tables[:, 0], tables[:, 1], HD1 ** -0.5, None, ALU.mult).then_inc(tables_own, 1)
                dve.wait_ge(tables_own, 1)

                def rope(slot, src, kind, t, heads):
                    cos, sin = ((tables[:, kind, n, t:t + 1, :] if t is not None else tables[:, kind, n, :, :])
                                .to_broadcast([P, heads, HD1]) for n in range(2))
                    a, b = (x[:, slot, 0:heads * HD1].rearrange("p (h n) -> p h n", h=heads) for x in (part_a, part_b))
                    dve.tensor_tensor(a, src, cos, ALU.mult)
                    for c in range(2):
                        lo, hi = slice(c * HD1 // 2, (c + 1) * HD1 // 2), slice((1 - c) * HD1 // 2, (2 - c) * HD1 // 2)
                        ins = dve.tensor_tensor(b[:, :, lo], src[:, :, hi], sin[:, :, lo], ALU.mult)
                    return ins

                def q(g, m, i):
                    index = q_index(g, m, i)
                    dve.wait_ge(projected, index + 1)
                    if not known(index, 2):
                        dve.wait_ge(roped, index - 1)
                    rope(q_index(0, m, i) % 2, psum[:, PROJB[i], :].rearrange("p (h n) -> p h n", h=QB), 0, i, QB)\
                        .then_inc(parts, 1)

                def kv(g, b):
                    index = kv_index(g, b)
                    dve.wait_ge(v_hi, B * g + (b + 1))
                    if not known(index, 2):
                        dve.wait_ge(roped, index - 1)
                    bank = psum[:, PROJB[0], :].rearrange("p (t n) -> p t n", t=2)
                    dve.tensor_tensor(v_l[:, b % 2, :], bank[:, 0, HD1:], f(v_h[:, b % 2, :]), ALU.subtract)
                    rope(kv_index(0, b) % 2, bank[:, :, 0:HD1], 1, None, 2).then_inc(parts, 1)

                def turn_q(g, m, c):
                    dve.wait_ge(qk_hi, turn_index(g, m, c) + 1)
                    at = q_h[:, m % 2, 2 * c:2 * c + 2, :]
                    bank = psum[:, TURNB, :].rearrange("p (h t n) -> p h t n", h=2, t=2)
                    dve.tensor_tensor(q_l[:, m % 2, 2 * c:2 * c + 2, :], bank[:, :, 1, :], f(at),
                                      ALU.subtract).then_inc(qk_lo, 1)

                def turn_k(g, b):
                    dve.wait_ge(qk_hi, k_turn_index(g, b) + 1)
                    dve.tensor_tensor(k_l[:, b % 2, :], psum[:, TURNB, 0:S], f(k_h[:, b % 2, :]),
                                      ALU.subtract).then_inc(qk_lo, 1)

                def peak(g, s):
                    dve.wait_ge(scored, STEPS * g + (s + 1))
                    at = psum[:, SCOREB[s % 2], :].rearrange("p (c n) -> p c n", c=2)[:, :, 0:P]
                    dve.tensor_tensor(at, at, mask[:].rearrange("p (c n) -> p c n", c=1).to_broadcast([P, 2, P]),
                                      ALU.add).then_inc(masked, 1)
                    dve.wait_ge(masked, STEPS * g + (s + 1))
                    for i, cols in enumerate((slice(0, P), slice(P, BANDS))):
                        ins = dve.tensor_reduce(neg_max[:, s % 2, i:i + 1], psum[:, SCOREB[s % 2], cols], AX.X, ALU.max,
                                                negate=True)
                    ins.then_inc(max_ready, 1)

                def turn_probs(g, s):
                    dve.wait_ge(p_hi, STEPS * g + (s + 1))
                    dve.tensor_tensor(pt_l[:, s % 2, :], psum[:, PTURNB, 0:S], f(pt_h[:, s % 2, :]),
                                      ALU.subtract).then_inc(p_lo, 1)

                def softmax(g, s):
                    dve.wait_ge(exp_done, 2 * STEPS * g + (2 * s + 2 + 4))
                    dve.reciprocal(rden[:, s % 2, :], sums[:, s % 2, :]).then_inc(rden_ready, 1)

                def values(g, s):
                    dve.wait_ge(o_hi, STEPS * g + (s + 1))
                    dve.tensor_tensor(ot_l[:, s % 2, :], psum[:, PVB, 0:S], f(ot_h[:, s % 2, :]),
                                      ALU.subtract).then_inc(o_lo, 1)

                def project_out(g, s):
                    if s % REP1 != REP1 - 1:
                        return
                    b = s // REP1
                    dve.wait_ge(wo_done, B * g + (b + 1))
                    dve.wait_ge(z_added, B * g + (b + 1))
                    at = z[:, 2 * b:2 * b + 2, :]
                    dve.tensor_tensor(at, psum[:, WOB, :].rearrange("p (t n) -> p t n", t=2), at, ALU.add)\
                        .then_inc(z_added, 1)

                run(dve, dict(q=q, kv=kv, turn_q=turn_q, turn_k=turn_k, peak=peak, turn_probs=turn_probs,
                              softmax=softmax, values=values, project_out=project_out))

            @block.tensor
            def _(pe):
                norm.tensor(pe)
                for half in range(2):
                    norm.ready(pe, half)
                pe.sem_inc(exp_done, 4)
                pe.sem_inc(z_added, B)
                pe.sem_inc(p_lo, 1)
                pe.sem_inc(o_lo, 1)

                def q(g, m, i):
                    before = bank_user_before(q_index(g, m, i), m, i)
                    bank = psum[:, PROJB[i], :]
                    if not known(before, 0):
                        pe.wait_ge(parts, before + 1)
                    if m == 0 and i == 0:
                        pe.wait_ge(w_ready, 2 * g + 1)
                    b = m // 2
                    for k in range(KD):
                        where = ds((g & 1) * KD + k, 1)
                        cols = slice((m % 2) * QC, (m % 2 + 1) * QC)
                        ins = product(pe, bank, core.xt(k, slice(b * S + i * P, b * S + (i + 1) * P)),
                                      (wq_h[:, where, cols], wq_l[:, where, cols]), k == 0, k == KD - 1)
                    ins.then_inc(projected, 1)

                def bank_user_before(index, m, i):
                    if i == 1:
                        return index - (2 if m % 2 == 1 else 3)
                    return index - (2 if m % 2 == 1 else 1)

                def kv(g, b):
                    index = kv_index(g, b)
                    if not known(index, 1):
                        pe.wait_ge(parts, index - 2 + 1)
                    pe.wait_ge(w_ready, 2 * g + 1)
                    for i in range(2):
                        for k in range(KD):
                            where = ds((g & 1) * KD + k, 1)
                            ins = product(pe, psum[:, PROJB[0], i * 2 * HD1:(i + 1) * 2 * HD1],
                                          core.xt(k, slice(b * S + i * P, b * S + (i + 1) * P)),
                                          (wkv_h[:, where, :], wkv_l[:, where, :]), k == 0, k == KD - 1)
                    ins.then_inc(projected, 1)

                def turn_q(g, m, c):
                    index = turn_index(g, m, c)
                    pe.wait_ge(roped, q_index(g, m, 1) + 1)
                    pe.wait_ge(qk_lo, index)
                    for hh in range(2):
                        for i in range(2):
                            head = 2 * c + hh
                            ins = pe.transpose(psum[:, TURNB, hh * S + i * P:hh * S + (i + 1) * P],
                                               qr[:, i, head * HD1:(head + 1) * HD1], core.ident[:])
                    ins.then_inc(qk_turned, 1)

                def turn_k(g, b):
                    index = k_turn_index(g, b)
                    pe.wait_ge(roped, kv_index(g, b) + 1)
                    if not known(index, 1):
                        pe.wait_ge(qk_lo, index)
                    for i in range(2):
                        ins = pe.transpose(psum[:, TURNB, i * P:(i + 1) * P], kr[:, i, :], core.ident[:])
                    ins.then_inc(qk_turned, 1)

                def scores(g, s):
                    b, h = s // REP1, s % REP1
                    m, c = 2 * b + h // QB, (h % QB) // 2
                    pe.wait_ge(qk_lo, turn_index(g, m, c) + 1)
                    pe.wait_ge(exp_done, 2 * STEPS * g + (2 * s + 2))
                    bank = psum[:, SCOREB[s % 2], :]
                    first, second = bank[:, 0:P], bank[:, P:BANDS]
                    pe.matmul(first, q_0[:, m % 2, h % QB, :], k_0[:, b % 2, :], start=True, stop=True,
                              skip_group_check=True)
                    ins = product(pe, second, (q_h[:, m % 2, h % QB, :], q_l[:, m % 2, h % QB, :]),
                                  (k_h[:, b % 2, :], k_l[:, b % 2, :]), True, True, True)
                    ins.then_inc(scored, 1)

                def turn_probs(g, s):
                    pe.wait_ge(p_normed, STEPS * g + (s + 1))
                    pe.wait_ge(p_lo, STEPS * g + (s + 1))
                    for i in range(3):
                        ins = pe.transpose(psum[:, PTURNB, i * P:(i + 1) * P], prob[:, s % 2, i * P:(i + 1) * P],
                                           core.ident[:])
                    ins.then_inc(p_turned, 1)

                def values(g, s):
                    b = s // REP1
                    pe.wait_ge(p_lo, STEPS * g + (s + 2))
                    pe.wait_ge(o_lo, STEPS * g + (s + 1))
                    product(pe, psum[:, PVB, 0:S], (v_h[:, b % 2, :], v_l[:, b % 2, :]),
                            (pt_h[:, s % 2, :], pt_l[:, s % 2, :]), True, False, True)
                    pe.matmul(psum[:, PVB, P:S], v_1[:, b % 2, :], pt_1[:, s % 2, :], start=False, stop=True,
                              skip_group_check=True).then_inc(pv_done, 1)

                def project_out(g, s):
                    b, h = s // REP1, s % REP1
                    pe.wait_ge(o_lo, STEPS * g + (s + 2))
                    if s == 0:
                        pe.wait_ge(w_ready, 2 * g + 2)
                    if h == 0:
                        pe.wait_ge(z_added, B * g + (b + B))
                    where = ds((g & 1) * REP1 + h, 1)
                    for i in range(2):
                        ins = product(pe, psum[:, WOB, i * D:(i + 1) * D],
                                      (ot_h[:, s % 2, i * P:(i + 1) * P], ot_l[:, s % 2, i * P:(i + 1) * P]),
                                      (wo_h[:, where, :], wo_l[:, where, :]), h == 0 and i == 0, h == REP1 - 1, True)
                    if h == REP1 - 1:
                        ins.then_inc(wo_done, 1)

                run(pe, dict(q=q, kv=kv, turn_q=turn_q, turn_k=turn_k, scores=scores, turn_probs=turn_probs,
                             values=values, project_out=project_out))


def experts(core, z, ln2_w, w_router, bias, w_gate, w_up, w_down, shared_gate, shared_up, shared_down, out):
    nc, sem, psum = core.nc, core.sem, core.psum
    scope, sb = core.stage()
    SHARED = NE
    with scope:
        ln_w = sb("ln2_w", [P, KD], F32)
        norm = Norm(core, "ln4", sb, 1e-5, weight=ln_w, rms=True)
        wr_raw = sb("wr_raw", [P, KD, NE], F32)
        wr_h, wr_l = (sb(f"wr_{n}", [P, KD, NE], F32R) for n in "hl")
        bias_sb = sb("bias_sb", [P, NE], F32)
        score = sb("score", [P, NT, NE], F32)
        biased = sb("biased", [P, NT, NE], F32)
        top = sb("top", [P, NT, TOPK], F32)
        rest = sb("rest", [P, NT, NE], F32)
        total = sb("total", [P, NT], F32)
        weight = sb("weight", [P, NE + 1, NT], F32)
        raw = sb("raw", [P, 2, 3, KD * FI], F32)
        gu_h, gu_l = (sb(f"gu_{n}", [P, 2, 2, KD, FI], F32R) for n in "hl")
        wd_h, wd_l = (sb(f"wd_{n}", [P, 2, D], F32R) for n in "hl")
        silu = sb("silu", [P, 2, HALF], F32)
        hid = sb("hid", [P, 2, HALF], F32)
        hid_h, hid_l = (sb(f"hid_{n}", [P, 2, T], F32R) for n in "hl")

        loaded_c = sem("e_constants_loaded")
        loaded = [sem(f"e_expert_loaded_{j}") for j in range(2)]
        wr_own = sem("e_router_high")
        wr_ready = sem("e_router_split")
        logits = sem("e_logits")
        sig = sem("e_scores")
        own_dve = sem("e_vector_written")
        gu_hi = sem("e_gate_up_high")
        gu_ready = sem("e_gate_up_split")
        wd_hi = sem("e_down_high")
        wd_ready = sem("e_down_split")
        gu_done = sem("e_gate_up_done")
        silu_done = sem("e_silu_done")
        hid_ready = sem("e_hidden_ready")
        hid_hi = sem("e_hidden_high")
        hid_lo = sem("e_hidden_low")
        down_done = sem("e_down_done")
        added = sem("e_added")
        stored = sem("e_stored")
        GATEB, UPB, DOWNB = 0, 2, 4

        def run(eng, step):
            step(0, 0)
            step(1, 1)
            with eng.Fori(1, NE // 2) as i:
                for j in range(2):
                    step(2 * i + j, j)
            step(SHARED, 0)

        with nc.Block() as block:
            @block.sync
            def _(sp):
                with nc.allow_non_contiguous_dma(reason="a norm's weights"):
                    sp.dma_start(ln_w[:], ln2_w.rearrange("(k p) -> p k", p=P)).then_inc(loaded_c, 16)
                sp.dma_start(wr_raw[:], w_router.rearrange("(k p) n -> p k n", p=P)).then_inc(loaded_c, 16)
                sp.dma_start(bias_sb[:], bias.rearrange("(a n) -> a n", a=1).to_broadcast([P, NE])).then_inc(loaded_c, 16)

                def load(e, j):
                    for n, w in enumerate((w_gate, w_up)):
                        src = shared_gate if n == 0 else shared_up
                        if not isinstance(e, int) or e < NE:
                            src = w.rearrange("e (k p) n -> p e k n", p=P)[:, ds(e, 1)]
                            sp.dma_start(raw[:, j, n:n + 1, :].rearrange("p a (k n) -> p a k n", k=KD), src)\
                                .then_inc(loaded[j], 16)
                        else:
                            sp.dma_start(raw[:, j, n, :].rearrange("p (k n) -> p k n", k=KD),
                                         src.rearrange("(k p) n -> p k n", p=P)).then_inc(loaded[j], 16)
                    src = w_down.rearrange("e p n -> p e n")[:, ds(e, 1)] if not isinstance(e, int) or e < NE else \
                        shared_down.rearrange("p (a n) -> p a n", a=1)
                    sp.dma_start(raw[:, j, 2:3, :], src).then_inc(loaded[j], 16)

                load(0, 0)
                load(1, 1)
                with sp.Fori(1, NE // 2) as i:
                    for j in range(2):
                        sp.wait_ge(wd_ready, 2 * i + (j - 1))
                        load(2 * i + j, j)
                sp.wait_ge(wd_ready, SHARED - 1)
                load(SHARED, 0)
                for t in range(NT):
                    sp.wait_ge(added, NT * (NE + 1) + t + 1)
                    sp.dma_start(out[t * P:(t + 1) * P, :], core.x[:, t, :]).then_inc(stored, 16)
                sp.wait_ge(stored, 16 * NT)

            @block.scalar
            def _(act):
                act.wait_ge(loaded_c, 16 * 3)
                norm.scalar(act)
                act.wait_ge(logits, 1)
                act.activation(score[:], psum[:, 4, 0:NT * NE].rearrange("p (t e) -> p t e", t=NT),
                               ACT.Sigmoid).then_inc(sig, 1)

                def split_gu(e, j):
                    act.wait_ge(loaded[j], 24 * e + (48 - 24 * j))
                    if not isinstance(e, int) or e >= 2:
                        act.wait_ge(gu_done, 2 * e - 2)
                    act.activation(gu_h[:, j], raw[:, j, 0:2, :].rearrange("p a (k n) -> p a k n", k=KD),
                                   ACT.Copy).then_inc(gu_hi, 1)

                def split_down(e, j):
                    if not isinstance(e, int) or e >= 2:
                        act.wait_ge(down_done, NT * e - NT)
                    act.activation(wd_h[:, j], raw[:, j, 2, :], ACT.Copy).then_inc(wd_hi, 1)

                split_gu(0, 0)

                def step(e, j):
                    split_down(e, j)
                    if not isinstance(e, int) or e < SHARED:
                        split_gu(e + 1, 1 - j)
                    for c in range(2):
                        cols = slice(c * HALF, (c + 1) * HALF)
                        act.wait_ge(gu_done, 2 * e + (c + 1))
                        if not isinstance(e, int) or e > 0:
                            act.wait_ge(hid_ready, 2 * e + (c - 1))
                        act.activation(silu[:, c, :], psum[:, GATEB + c, :], ACT.Silu).then_inc(silu_done, 1)
                        act.wait_ge(hid_ready, 2 * e + (c + 1))
                        act.activation(hid_h[:, j, cols], hid[:, c, :], ACT.Copy).then_inc(hid_hi, 1)

                run(act, step)

            @block.gpsimd
            def _(pool):
                norm.gpsimd(pool)
                pool.wait_ge(loaded_c, 16 * 3)
                pool.tensor_copy(wr_h[:], wr_raw[:]).then_inc(wr_own, 1)
                pool.wait_ge(wr_own, 1)
                pool.tensor_tensor(wr_l[:], wr_raw[:], f(wr_h[:]), ALU.subtract).then_inc(wr_ready, 1)

                def split_gu(e, j):
                    src = raw[:, j, 0:2, :].rearrange("p a (k n) -> p a k n", k=KD)
                    pool.wait_ge(gu_hi, e + 1)
                    pool.tensor_tensor(gu_l[:, j], src, f(gu_h[:, j]), ALU.subtract).then_inc(gu_ready, 1)

                def split_down(e, j):
                    pool.wait_ge(wd_hi, e + 1)
                    pool.tensor_tensor(wd_l[:, j], raw[:, j, 2, :], f(wd_h[:, j]), ALU.subtract).then_inc(wd_ready, 1)

                split_gu(0, 0)

                def step(e, j):
                    split_down(e, j)
                    if not isinstance(e, int) or e < SHARED:
                        split_gu(e + 1, 1 - j)
                    for c in range(2):
                        cols = slice(c * HALF, (c + 1) * HALF)
                        pool.wait_ge(hid_hi, 2 * e + (c + 1))
                        pool.tensor_tensor(hid_l[:, j, cols], hid[:, c, :], f(hid_h[:, j, cols]), ALU.subtract)\
                            .then_inc(hid_lo, 1)

                run(pool, step)

            @block.vector
            def _(dve):
                norm.vector(dve, z)
                own = Count(dve, own_dve)
                for t in range(NT):
                    dve.tensor_tensor(core.x[:, t, :], core.x[:, t, :], z[:, t, :], ALU.add).then_inc(added, 1)
                own.add(dve.memset(weight[:, NE, :], 1.0))
                dve.wait_ge(loaded_c, 16 * 3)
                dve.wait_ge(sig, 1)
                own.add(dve.tensor_tensor(biased[:], score[:],
                                          bias_sb[:].rearrange("p (t e) -> p t e", t=1).to_broadcast([P, NT, NE]), ALU.add))
                own.settle()
                for t in range(NT):
                    own.add(dve.max(top[:, t, :], biased[:, t, :]))
                own.settle()
                for t in range(NT):
                    own.add(dve.match_replace(rest[:, t, :], top[:, t, :], biased[:, t, :], MASKED))
                own.settle()
                own.add(dve.tensor_tensor(biased[:], biased[:], rest[:], ALU.not_equal))
                own.settle()
                own.add(dve.tensor_tensor(score[:], score[:], biased[:], ALU.mult))
                own.settle()
                own.add(dve.tensor_reduce(total[:], score[:], AX.X, ALU.add))
                own.settle()
                own.add(dve.reciprocal(total[:], total[:]))
                own.settle()
                own.add(dve.tensor_tensor(weight[:, 0:NE, :], score[:].rearrange("p t e -> p e t"),
                                          total[:].rearrange("p (e t) -> p e t", e=1).to_broadcast([P, NE, NT]), ALU.mult))
                own.settle()

                def add(e, t):
                    dve.wait_ge(down_done, NT * e + ((t | 1) + 1))
                    dve.wait_ge(added, NT * e + (t + 1))
                    src = psum[:, DOWNB + t // 2, (t % 2) * D:(t % 2 + 1) * D]
                    scale = weight[:, ds(e, 1), t] if not isinstance(e, int) else weight[:, e, t:t + 1]
                    dve.scalar_tensor_tensor(core.x[:, t, :], src, scale, core.x[:, t, :], ALU.mult, ALU.add)\
                        .then_inc(added, 1)

                def step(e, j):
                    for c in range(2):
                        dve.wait_ge(silu_done, 2 * e + (c + 1))
                        if not isinstance(e, int) or e > 0:
                            dve.wait_ge(hid_lo, 2 * e + (c - 1))
                        dve.tensor_tensor(hid[:, c, :], psum[:, UPB + c, :], silu[:, c, :], ALU.mult)\
                            .then_inc(hid_ready, 1)
                        if not isinstance(e, int) or e > 0:
                            for t in range(c * TH, (c + 1) * TH):
                                add(e - 1, t)

                run(dve, step)
                for t in range(NT):
                    add(SHARED, t)

            @block.tensor
            def _(pe):
                norm.tensor(pe)
                pe.wait_ge(wr_ready, 1)
                for t in range(NT):
                    norm.ready(pe, t // TH)
                    for k in range(KD):
                        ins = product(pe, psum[:, 4, t * NE:(t + 1) * NE], core.xt(k, slice(t * P, (t + 1) * P)),
                                      (wr_h[:, k, :], wr_l[:, k, :]), k == 0, k == KD - 1)
                ins.then_inc(logits, 1)
                pe.wait_ge(sig, 1)

                def down(e, t, j):
                    if t % 2 == 0:
                        pe.wait_ge(added, NT * e + (t + 2))
                    cols = slice(t * P, (t + 1) * P)
                    product(pe, psum[:, DOWNB + t // 2, (t % 2) * D:(t % 2 + 1) * D],
                            (hid_h[:, j, cols], hid_l[:, j, cols]), (wd_h[:, j, :], wd_l[:, j, :])).then_inc(down_done, 1)

                def down_half(e, c, j):
                    if c == 0:
                        pe.wait_ge(wd_ready, e + 1)
                    pe.wait_ge(hid_lo, 2 * e + (c + 1))
                    for t in range(c * TH, (c + 1) * TH):
                        down(e, t, j)

                def step(e, j):
                    pe.wait_ge(gu_ready, e + 1)
                    for c in range(2):
                        if not isinstance(e, int) or e > 0:
                            pe.wait_ge(hid_ready, 2 * e + (c - 1))
                        for n, bank in enumerate((GATEB + c, UPB + c)):
                            for k in range(KD):
                                ins = product(pe, psum[:, bank, :], (gu_h[:, j, n, k, :], gu_l[:, j, n, k, :]),
                                              core.xt(k, slice(c * HALF, (c + 1) * HALF)), k == 0, k == KD - 1)
                        ins.then_inc(gu_done, 1)
                        if not isinstance(e, int) or e > 0:
                            down_half(e - 1, c, 1 - j)

                run(pe, step)
                for c in range(2):
                    down_half(SHARED, c, 0)

_INS = ['L0_attn_hidden_states', 'L0_attn_w_qkv', 'L0_attn_q_norm_w', 'L0_attn_k_norm_w', 'L0_attn_w_o',
        'L0_ffn_w_up_q', 'L0_ffn_w_up_scale', 'L0_ffn_b_up', 'L0_ffn_w_up_lora_a', 'L0_ffn_w_up_lora_b',
        'L0_ffn_w_down_q', 'L0_ffn_w_down_scale', 'L0_ffn_b_down', 'L0_ffn_w_down_lora_a', 'L0_ffn_w_down_lora_b',
        'L1_attn_W_xproj', 'L1_attn_b_xproj', 'L1_attn_W_dt', 'L1_attn_b_dt', 'L1_attn_A_log',
        'L1_ffn_ln1_w', 'L1_ffn_ln2_w', 'L1_ffn_Wq', 'L1_ffn_Wk', 'L1_ffn_Wv', 'L1_ffn_Wo', 'L1_ffn_Wr',
        'L1_ffn_expert_bias', 'L1_ffn_Wg', 'L1_ffn_Wu', 'L1_ffn_Wd', 'L1_ffn_Wsg', 'L1_ffn_Wsu', 'L1_ffn_Wsd']
_TURNED = ['L0_attn_w_qkv', 'L0_attn_w_o', 'L0_ffn_w_up_q', 'L0_ffn_w_up_scale', 'L0_ffn_w_up_lora_a',
           'L0_ffn_w_down_q', 'L0_ffn_w_down_scale', 'L0_ffn_w_down_lora_a', 'L1_attn_W_xproj', 'L1_attn_W_dt']


def program(nc, a, consts, out):
    with ExitStack() as ctx:
        core = Core(nc, ctx)
        ffn = FfnWeights(core, *(a["L0_ffn_" + n] for n in ("w_up_q", "w_up_scale", "w_down_q", "w_down_scale")))
        windowed_attention(core, a["L0_attn_hidden_states"], a["L0_attn_w_qkv"], a["L0_attn_q_norm_w"],
                           a["L0_attn_k_norm_w"], a["L0_attn_w_o"], consts, ffn)
        quantized_ffn(core, ffn, *(a["L0_ffn_" + n] for n in (
            "b_up", "w_up_lora_a", "w_up_lora_b", "b_down", "w_down_lora_a", "w_down_lora_b")))
        weights = AttentionWeights(core, *(a["L1_ffn_" + n] for n in ("Wq", "Wk", "Wv", "Wo")))
        selective_scan(core, *(a["L1_attn_" + n] for n in ("W_xproj", "b_xproj", "W_dt", "b_dt", "A_log")), consts,
                       weights)
        z = ctx.enter_context(nc.sbuf_tensor("z", [P, NT, D], F32))
        causal_attention(core, z, a["L1_ffn_ln1_w"], weights, consts)
        experts(core, z, *(a["L1_ffn_" + n] for n in (
            "ln2_w", "Wr", "expert_bias", "Wg", "Wu", "Wd", "Wsg", "Wsu", "Wsd")), out)




_OUTS = [((B, S, D), "float32")]


def _constants():
    def rope(positions, width, heads):
        inv = (np.float32(1.0) / np.float32(10000.0) ** (np.arange(0, width, 2, dtype=np.float32) / np.float32(width)))
        ang = np.arange(positions, dtype=np.float32)[:, None] * inv.astype(np.float32)[None, :]
        cos, sin = np.cos(ang).astype(np.float32), np.sin(ang).astype(np.float32)
        return (np.tile(np.concatenate([cos, cos], 1), (1, heads)), np.tile(np.concatenate([-sin, sin], 1), (1, heads)))

    bf16 = mybir.dt.np(BF16)
    i = np.arange(P)
    causal = np.where(i[None, :] <= i[:, None], 0.0, MASKED)
    beyond = np.where(i[None, :] > i[:, None], 0.0, MASKED)
    cos0, sin0 = rope(S, HD0, NH0)
    cos1, sin1 = rope(S, HD1, 1)
    one_hot = np.zeros((3 * 2 * NS, 2 * NS, P), np.float32)
    for part in range(3):
        for n in range(2 * NS):
            one_hot[part * 2 * NS + n, n, :] = 1.0
    head_rows = (i[:, None] // HD0 == np.arange(P // HD0)[None, :]).astype(np.float32)
    return {
        "ident": np.eye(P, dtype=np.float32), "ident_bf": np.eye(P, dtype=bf16),
        "cos0": cos0, "sin0": sin0, "cos1": cos1, "sin1": sin1,
        "head_rows": head_rows,
        "window_mask": np.concatenate([causal, beyond, causal], 1).astype(bf16),
        "causal_mask": causal.astype(np.float32),
        "one_hot": one_hot.astype(bf16),
    }


def kernel(**inputs):
    import concourse.bacc as _bacc
    from concourse.bass_utils import run_bass_kernel_spmd as _run

    def laid_out(name):
        a = np.asarray(inputs[name])
        if name in _TURNED:
            a = a.T
        if name == "L0_attn_hidden_states":
            a = a.reshape(T, D)
        return np.ascontiguousarray(a)

    nc = _bacc.Bacc("TRN2", target_bir_lowering=False, num_devices=1)
    arrays, args, consts = {}, {}, {}
    for into, given in ((args, {n: laid_out(n) for n in _INS}), (consts, _constants())):
        for name, a in given.items():
            arrays[f"in_{name}_dram"] = a
            into[name] = nc.dram_tensor(f"in_{name}_dram", a.shape, mybir.dt.from_np(a.dtype), kind="ExternalInput").ap()
    out = nc.dram_tensor("out_0_dram", _OUTS[0][0], F32, kind="ExternalOutput").ap()
    program(nc, args, consts, out.rearrange("b s d -> (b s) d"))
    r = _run(nc, [arrays], core_ids=[0])
    return r.results[0]["out_0_dram"]
```
